# Optimizing a Trainium2 kernel written in Bass

```python
import numpy as np
import jax
import jax.numpy as jnp

def _softmax(x, axis=-1):
    return jax.nn.softmax(x, axis=axis)

def _gelu(x):
    return jax.nn.gelu(x, approximate=True)

def _silu(x):
    return jax.nn.silu(x)

def _sigmoid(x):
    return jax.nn.sigmoid(x)

def _layernorm(x, axis=-1, eps=1e-05):
    m = jnp.mean(x, axis=axis, keepdims=True)
    v = jnp.var(x, axis=axis, keepdims=True)
    return (x - m) / jnp.sqrt(v + eps)

def _scatter_add(tgt, idx, src, axis=0):
    return tgt.at[idx].add(src)

def _segment_sum(src, seg, n):
    return jax.ops.segment_sum(src, seg, n)
kernel_name = 'mk_sandwich_d1_jaxref_r8_eae685'

def setup_inputs(seed: int=0):
    np.random.seed(seed)
    _w = jnp.asarray

    def _L0_attn_setup():
        import jax, jax.numpy as jnp
        import numpy as np
        D = 128
        H = 16
        KVH = 4
        HD = D // H
        LAT = 32
        WIN = 32
        B, S = (1, 256)
        BASE_G, BASE_L = (1000000.0, 10000.0)
        EPS = 1e-06

        def rmsnorm(x, w):
            return x * jax.lax.rsqrt(jnp.mean(x * x, axis=-1, keepdims=True) + EPS) * w

        def qk_norm(x):
            return x * jax.lax.rsqrt(jnp.mean(x * x, axis=-1, keepdims=True) + EPS)

        def rope(x, base):
            s, hd = (x.shape[-2], x.shape[-1])
            inv_freq = 1.0 / base ** (jnp.arange(0, hd, 2, dtype=jnp.float32) / hd)
            freqs = jnp.arange(s, dtype=jnp.float32)[:, None] * inv_freq[None, :]
            cos, sin = (jnp.cos(freqs), jnp.sin(freqs))
            xe, xo = (x[..., ::2], x[..., 1::2])
            out = jnp.stack([xe * cos - xo * sin, xe * sin + xo * cos], axis=-1)
            return out.reshape(x.shape)

        def split_heads(x, n_heads):
            b, s, _ = x.shape
            return x.reshape(b, s, n_heads, HD).transpose(0, 2, 1, 3)

        def repeat_kv(x):
            return jnp.repeat(x, H // KVH, axis=1)

        def sdpa(q, k, v, mask):
            scores = jnp.einsum('bhqd,bhkd->bhqk', q, k) / np.sqrt(HD).astype(np.float32)
            scores = jnp.where(mask, scores, jnp.float32(-1e+30))
            probs = jax.nn.softmax(scores, axis=-1)
            return jnp.einsum('bhqk,bhkd->bhqd', probs, v)

        def merge_heads(x):
            b, h, s, hd = x.shape
            return x.transpose(0, 2, 1, 3).reshape(b, s, h * hd)

        def global_latent_attn(x, wq, w_kv_down, w_k_up, w_v_up, wo):
            q = split_heads(x @ wq, H)
            latent = x @ w_kv_down
            k = split_heads(latent @ w_k_up, KVH)
            v = split_heads(latent @ w_v_up, KVH)
            q, k = (rope(q, BASE_G), rope(k, BASE_G))
            q, k = (qk_norm(q), qk_norm(k))
            k, v = (repeat_kv(k), repeat_kv(v))
            i = jnp.arange(x.shape[1])
            causal = i[:, None] >= i[None, :]
            return merge_heads(sdpa(q, k, v, causal)) @ wo

        def local_gqa_attn(x, wq, wk, wv, wo):
            q = split_heads(x @ wq, H)
            k = split_heads(x @ wk, KVH)
            v = split_heads(x @ wv, KVH)
            q, k = (rope(q, BASE_L), rope(k, BASE_L))
            q, k = (qk_norm(q), qk_norm(k))
            k, v = (repeat_kv(k), repeat_kv(v))
            i = jnp.arange(x.shape[1])
            diff = i[:, None] - i[None, :]
            mask = (diff >= 0) & (diff < WIN)
            return merge_heads(sdpa(q, k, v, mask)) @ wo
        key = jax.random.key(seed)
        ks = jax.random.split(key, 12)
        std = 0.02
        return {'hidden': jax.random.normal(ks[0], (B, S, D), dtype=jnp.float32), 'norm1_w': jnp.ones((D,), jnp.float32), 'norm2_w': jnp.ones((D,), jnp.float32), 'g_wq': jax.random.normal(ks[1], (D, H * HD), jnp.float32) * std, 'g_kv_down': jax.random.normal(ks[2], (D, LAT), jnp.float32) * std, 'g_k_up': jax.random.normal(ks[3], (LAT, KVH * HD), jnp.float32) * std, 'g_v_up': jax.random.normal(ks[4], (LAT, KVH * HD), jnp.float32) * std, 'g_wo': jax.random.normal(ks[5], (D, D), jnp.float32) * std, 'l_wq': jax.random.normal(ks[6], (D, H * HD), jnp.float32) * std, 'l_wk': jax.random.normal(ks[7], (D, KVH * HD), jnp.float32) * std, 'l_wv': jax.random.normal(ks[8], (D, KVH * HD), jnp.float32) * std, 'l_wo': jax.random.normal(ks[9], (D, D), jnp.float32) * std}
    _L0_attn_in = _L0_attn_setup()

    def _L0_ffn_setup():
        import jax, jax.numpy as jnp
        import numpy as np
        D_MODEL = 128
        EXPERT_DIM = 256
        N_EXPERTS = 8
        LN_EPS = 1e-05

        def _bit_quant(W):
            scale = jnp.clip(jnp.mean(jnp.abs(W), axis=-1, keepdims=True), 1e-05, None)
            w_q = jnp.clip(jnp.round(W / scale), -1.0, 1.0) * scale
            return W + jax.lax.stop_gradient(w_q - W)
        key = jax.random.key(seed)
        ks = jax.random.split(key, 7)
        x = jax.random.normal(ks[0], (4, 256, D_MODEL), dtype=jnp.float32)
        shared_w1 = jax.random.normal(ks[1], (EXPERT_DIM, D_MODEL), dtype=jnp.float32) / np.sqrt(EXPERT_DIM)
        shared_w2 = jax.random.normal(ks[2], (D_MODEL, EXPERT_DIM), dtype=jnp.float32) / np.sqrt(D_MODEL)
        expert_w1 = jax.random.normal(ks[3], (N_EXPERTS, EXPERT_DIM, D_MODEL), dtype=jnp.float32) / np.sqrt(EXPERT_DIM)
        expert_w2 = jax.random.normal(ks[4], (N_EXPERTS, D_MODEL, EXPERT_DIM), dtype=jnp.float32) / np.sqrt(D_MODEL)
        router_w = 0.02 * jax.random.normal(ks[5], (N_EXPERTS, D_MODEL), dtype=jnp.float32)
        ln_gamma = jnp.ones((D_MODEL,), dtype=jnp.float32)
        ln_beta = jnp.zeros((D_MODEL,), dtype=jnp.float32)
        return {'x': x, 'shared_w1': shared_w1, 'shared_w2': shared_w2, 'expert_w1': expert_w1, 'expert_w2': expert_w2, 'router_w': router_w, 'ln_gamma': ln_gamma, 'ln_beta': ln_beta}
    _L0_ffn_in = _L0_ffn_setup()
    _d = {'L0_attn_hidden': _L0_attn_in['hidden'], 'L0_attn_norm1_w': _L0_attn_in['norm1_w'], 'L0_attn_norm2_w': _L0_attn_in['norm2_w'], 'L0_attn_g_wq': _L0_attn_in['g_wq'], 'L0_attn_g_kv_down': _L0_attn_in['g_kv_down'], 'L0_attn_g_k_up': _L0_attn_in['g_k_up'], 'L0_attn_g_v_up': _L0_attn_in['g_v_up'], 'L0_attn_g_wo': _L0_attn_in['g_wo'], 'L0_attn_l_wq': _L0_attn_in['l_wq'], 'L0_attn_l_wk': _L0_attn_in['l_wk'], 'L0_attn_l_wv': _L0_attn_in['l_wv'], 'L0_attn_l_wo': _L0_attn_in['l_wo'], 'L0_ffn_shared_w1': _L0_ffn_in['shared_w1'], 'L0_ffn_shared_w2': _L0_ffn_in['shared_w2'], 'L0_ffn_expert_w1': _L0_ffn_in['expert_w1'], 'L0_ffn_expert_w2': _L0_ffn_in['expert_w2'], 'L0_ffn_router_w': _L0_ffn_in['router_w'], 'L0_ffn_ln_gamma': _L0_ffn_in['ln_gamma'], 'L0_ffn_ln_beta': _L0_ffn_in['ln_beta']}
    _x0 = _d['L0_attn_hidden']
    _d['L0_attn_hidden'] = jax.random.normal(jax.random.fold_in(jax.random.key(seed), 1), (1, 2048, 128), dtype=_x0.dtype)
    del _x0
    return _d

def reference(L0_attn_hidden, L0_attn_norm1_w, L0_attn_norm2_w, L0_attn_g_wq, L0_attn_g_kv_down, L0_attn_g_k_up, L0_attn_g_v_up, L0_attn_g_wo, L0_attn_l_wq, L0_attn_l_wk, L0_attn_l_wv, L0_attn_l_wo, L0_ffn_shared_w1, L0_ffn_shared_w2, L0_ffn_expert_w1, L0_ffn_expert_w2, L0_ffn_router_w, L0_ffn_ln_gamma, L0_ffn_ln_beta):

    def _L0_attn_ref(hidden, norm1_w, norm2_w, g_wq, g_kv_down, g_k_up, g_v_up, g_wo, l_wq, l_wk, l_wv, l_wo):
        import jax, jax.numpy as jnp
        import numpy as np
        D = 128
        H = 16
        KVH = 4
        HD = D // H
        LAT = 32
        WIN = 32
        B, S = (1, 256)
        BASE_G, BASE_L = (1000000.0, 10000.0)
        EPS = 1e-06

        def rmsnorm(x, w):
            return x * jax.lax.rsqrt(jnp.mean(x * x, axis=-1, keepdims=True) + EPS) * w

        def qk_norm(x):
            return x * jax.lax.rsqrt(jnp.mean(x * x, axis=-1, keepdims=True) + EPS)

        def rope(x, base):
            s, hd = (x.shape[-2], x.shape[-1])
            inv_freq = 1.0 / base ** (jnp.arange(0, hd, 2, dtype=jnp.float32) / hd)
            freqs = jnp.arange(s, dtype=jnp.float32)[:, None] * inv_freq[None, :]
            cos, sin = (jnp.cos(freqs), jnp.sin(freqs))
            xe, xo = (x[..., ::2], x[..., 1::2])
            out = jnp.stack([xe * cos - xo * sin, xe * sin + xo * cos], axis=-1)
            return out.reshape(x.shape)

        def split_heads(x, n_heads):
            b, s, _ = x.shape
            return x.reshape(b, s, n_heads, HD).transpose(0, 2, 1, 3)

        def repeat_kv(x):
            return jnp.repeat(x, H // KVH, axis=1)

        def sdpa(q, k, v, mask):
            scores = jnp.einsum('bhqd,bhkd->bhqk', q, k) / np.sqrt(HD).astype(np.float32)
            scores = jnp.where(mask, scores, jnp.float32(-1e+30))
            probs = jax.nn.softmax(scores, axis=-1)
            return jnp.einsum('bhqk,bhkd->bhqd', probs, v)

        def merge_heads(x):
            b, h, s, hd = x.shape
            return x.transpose(0, 2, 1, 3).reshape(b, s, h * hd)

        def global_latent_attn(x, wq, w_kv_down, w_k_up, w_v_up, wo):
            q = split_heads(x @ wq, H)
            latent = x @ w_kv_down
            k = split_heads(latent @ w_k_up, KVH)
            v = split_heads(latent @ w_v_up, KVH)
            q, k = (rope(q, BASE_G), rope(k, BASE_G))
            q, k = (qk_norm(q), qk_norm(k))
            k, v = (repeat_kv(k), repeat_kv(v))
            i = jnp.arange(x.shape[1])
            causal = i[:, None] >= i[None, :]
            return merge_heads(sdpa(q, k, v, causal)) @ wo

        def local_gqa_attn(x, wq, wk, wv, wo):
            q = split_heads(x @ wq, H)
            k = split_heads(x @ wk, KVH)
            v = split_heads(x @ wv, KVH)
            q, k = (rope(q, BASE_L), rope(k, BASE_L))
            q, k = (qk_norm(q), qk_norm(k))
            k, v = (repeat_kv(k), repeat_kv(v))
            i = jnp.arange(x.shape[1])
            diff = i[:, None] - i[None, :]
            mask = (diff >= 0) & (diff < WIN)
            return merge_heads(sdpa(q, k, v, mask)) @ wo
        x = hidden
        x = x + global_latent_attn(rmsnorm(x, norm1_w), g_wq, g_kv_down, g_k_up, g_v_up, g_wo)
        x = x + local_gqa_attn(rmsnorm(x, norm2_w), l_wq, l_wk, l_wv, l_wo)
        return x

    def _L0_ffn_ref(x, shared_w1, shared_w2, expert_w1, expert_w2, router_w, ln_gamma, ln_beta):
        import jax, jax.numpy as jnp
        import numpy as np
        D_MODEL = 128
        EXPERT_DIM = 256
        N_EXPERTS = 8
        LN_EPS = 1e-05

        def _bit_quant(W):
            scale = jnp.clip(jnp.mean(jnp.abs(W), axis=-1, keepdims=True), 1e-05, None)
            w_q = jnp.clip(jnp.round(W / scale), -1.0, 1.0) * scale
            return W + jax.lax.stop_gradient(w_q - W)
        mu = jnp.mean(x, axis=-1, keepdims=True)
        var = jnp.mean(jnp.square(x - mu), axis=-1, keepdims=True)
        h = (x - mu) / jnp.sqrt(var + LN_EPS) * ln_gamma + ln_beta
        sw1, sw2 = (_bit_quant(shared_w1), _bit_quant(shared_w2))
        shared_out = jax.nn.silu(jnp.einsum('btd,fd->btf', h, sw1)) @ sw2.T
        probs = jax.nn.softmax(h @ router_w.T, axis=-1)
        top_prob = jnp.max(probs, axis=-1)
        top_idx = jnp.argmax(probs, axis=-1)
        ew1, ew2 = (_bit_quant(expert_w1), _bit_quant(expert_w2))
        h1 = jax.nn.silu(jnp.einsum('btd,efd->ebtf', h, ew1))
        eo = jnp.einsum('ebtf,edf->ebtd', h1, ew2)
        gate = jax.nn.one_hot(top_idx, N_EXPERTS, dtype=h.dtype) * top_prob[..., None]
        routed_out = jnp.einsum('ebtd,bte->btd', eo, gate)
        return shared_out + routed_out
    x = L0_attn_hidden
    x = x + _layernorm(_L0_attn_ref(_layernorm(x, axis=-1), L0_attn_norm1_w, L0_attn_norm2_w, L0_attn_g_wq, L0_attn_g_kv_down, L0_attn_g_k_up, L0_attn_g_v_up, L0_attn_g_wo, L0_attn_l_wq, L0_attn_l_wk, L0_attn_l_wv, L0_attn_l_wo), axis=-1)
    x = x + _layernorm(_L0_ffn_ref(_layernorm(x, axis=-1), L0_ffn_shared_w1, L0_ffn_shared_w2, L0_ffn_expert_w1, L0_ffn_expert_w2, L0_ffn_router_w, L0_ffn_ln_gamma, L0_ffn_ln_beta), axis=-1)
    return x

_drawn_inputs = setup_inputs


def setup_inputs(seed=0):
    import zlib

    import numpy as np

    out = dict(_drawn_inputs(seed))
    spreads = {'L0_attn_norm1_w': (1.0, 0.6),
     'L0_attn_norm2_w': (1.0, 0.6),
     'L0_ffn_ln_gamma': (1.0, 0.2),
     'L0_ffn_ln_beta': (0.0, 0.1)}
    factors = {'L0_attn_g_wq': 8.0,
     'L0_attn_g_kv_down': 8.0,
     'L0_attn_g_k_up': 8.0,
     'L0_attn_g_v_up': 8.0,
     'L0_attn_g_wo': 8.0,
     'L0_attn_l_wq': 8.0,
     'L0_attn_l_wk': 7.58,
     'L0_attn_l_wv': 6.926,
     'L0_attn_l_wo': 6.678}
    for name, (base, spread) in spreads.items():
        noise = np.random.default_rng([zlib.crc32(name.encode()), seed]).standard_normal(out[name].shape)
        drawn = base * np.exp(spread * noise) if base else spread * noise
        out[name] = jnp.asarray(drawn.astype(out[name].dtype))
    for name, factor in factors.items():
        out[name] = (out[name] * factor).astype(out[name].dtype)
    return out
```

```python
from contextlib import ExitStack

import numpy as np

import concourse.bass as bass
from concourse import mybir

F32 = mybir.dt.float32
BF16 = mybir.dt.bfloat16
I32 = mybir.dt.int32
ALU = mybir.AluOpType
ACT = mybir.ActivationFunctionType
AX = mybir.AxisListType

P = 128
TILES = 16
NB = TILES // 2
QB = 2 * P
H, KVH, HD = 16, 4, 8
GRP = H // KVH
WIN = 32
NE, FT = 8, 2
QKW = (H + KVH) * HD
PW = QKW + KVH * HD
TERMS = 8
EPS_LN, EPS_RMS = 1e-5, 1e-6
MAGIC = float(0x5F3759DF)
G, L = 0, 1
NMISC = 3
NP = 4
LAG = 2

SLOT_OF = [0, 2, 1, 3]


def units_of(a, b):
    if a == G:
        return [(g, kb) for g in range(KVH) for kb in range(2 * b + 2)]
    return [(g, u) for g in range(KVH) for u in range(2)]


def pieces(a, b, kb):
    if a == G:
        lo = P if kb == 2 * b + 1 else 0
        return [(kb, lo, QB - lo, lo)]
    if kb == 1:
        return [(2 * b + 1, P, P, 0)]
    return ([(2 * b - 1, 0, WIN, 0)] if b else []) + [(2 * b, 0, P + WIN, WIN)]


def front_steps(a, b):
    return [("norm", a, b), ("xT", a, b), ("proj", a, b), ("split", a, b), ("kT", a, b), ("qT", a, b, 0),
            ("qT", a, b, 1)]


def out_steps(a, b):
    return [("oT", a, b, 0), ("oT", a, b, 1), ("onT", a, b), ("wo", a, b)]


def ffn_steps(b):
    return [("fnorm", b), ("fhT", b), ("frouter", b), ("fohT", b), ("fmask", b, 0), ("fmask", b, 1),
            ("fw1s", b), ("fw1", b, 0), ("fw1", b, 1), ("fact", b), ("fw2", b, 0), ("fw2s", b, 0),
            ("fw2", b, 1), ("fw2s", b, 1)]


def local_steps(b):
    out = []
    for g in range(KVH):
        out += [("qk", L, b, g, 0), ("qk", L, b, g, 1)]
        out += [("pv", L, b, g, 0), ("pv", L, b, g, 1), ("oevac", L, b, g)]
    return out


TURNS = [[(1, k, 0) for k in range(8)], [(1, k, 0) for k in range(8, 16)],
         [(1, 16, 0), (1, 17, 0), (2, NE, 0), (2, NE, 1)],
         [(2, k, f) for k in range(4) for f in range(FT)], [(2, k, f) for k in range(4, 8) for f in range(FT)]]


def make_plan():
    plan = [("weights",)]
    plan += front_steps(G, 0)
    waiting = []
    for b in range(NB):
        first = (out_steps(G, b - 1) if b else []) + (front_steps(G, b + 1) if b + 1 < NB else [])
        if b == 0:
            waiting += [("prep",)]
            for k in range(len(TURNS)):
                waiting += [("ternary", k), ("wturn", k)]
            waiting += [("scales",)]
        units = [(G, b, g, kb) for g, kb in units_of(G, b)]
        per = min(2, -(-(len(first) + len(waiting)) // len(units)))
        for n, u in enumerate([*units, *[None] * LAG]):
            if u:
                plan.append(("qk", *u))
            if n >= LAG:
                w = units[n - LAG]
                plan.append(("pv", *w))
                if w[3] == 2 * b + 1:
                    while first and first[0][0] in ("oT", "onT", "wo"):
                        plan.append(first.pop(0))
                    plan.append(("oevac", *w[:3]))
            for _ in range(per if u else 0):
                if first and (n % 2 == 0 or not waiting or per == 1):
                    plan.append(first.pop(0))
                elif waiting:
                    plan.append(waiting.pop(0))
        plan += first
        waiting += front_steps(L, b) + local_steps(b) + out_steps(L, b) + ffn_steps(b)
    return plan + out_steps(G, NB - 1) + waiting


PLAN = make_plan()
TAKES = {"weights": 3, "wturn": 1, "scales": 2, "xT": 1, "proj": 1, "qT": 1, "kT": 1, "oT": 1, "onT": 1, "wo": 1, "fhT": 1, "frouter": 1, "fohT": 1,
         "fmask": 1, "fw1s": 2, "fw1": 1, "fw2": 2, "fw2s": 1}


def number():
    unit, pv, osum, take, masks = {}, {}, {}, {}, {}
    n = 0
    for s in PLAN:
        if s[0] == "qk":
            unit[s[1:]] = len(unit)
            if s[1] == L or s[4] >= 2 * s[2]:
                masks[s[1:]] = len(masks)
        if s[0] == "pv":
            pv[s[1:]] = len(pv)
            if s[1] == G and s[4] == 0:
                osum[s[2:4]] = len(osum)
        k = TAKES.get(s[0], 0)
        if s[0] == "pv" and s[1] == L and s[4] == 0:
            k = 1
        for j in range(k):
            take[(*s, j)] = (n % NMISC, n // NMISC)
            n += 1
    return unit, pv, osum, take, masks


UNIT, PV, OSUM, TAKE, MASK = number()
UNIT_LIST = list(UNIT)


def build(nc, x, norm1_w, norm2_w, g_wq, g_kv_down, g_k_up, g_v_up, g_wo, l_wq, l_wk, l_wv, l_wo,
          sw1, sw2, ew1, ew2, router_w, ln_gamma, ln_beta, ident_d, rope_d, band_d, rank_d, out):
    with ExitStack() as ctx:
        def sb(name, shape, dt=F32):
            return ctx.enter_context(nc.sbuf_tensor(name, shape, dt))

        def sem(name):
            return ctx.enter_context(nc.semaphore(name))

        def pair(name):
            return [sem(f"{name}_g"), sem(f"{name}_l")]

        def two(name, shape, dt=F32):
            return [sb(f"{name}_g", shape, dt), sb(f"{name}_l", shape, dt)]

        scores = [ctx.enter_context(nc.psum_tensor(f"scores{i}", [P, 1024], F32)) for i in range(2)]
        osum_g = ctx.enter_context(nc.psum_tensor("osum_g", [P, 512], F32))
        misc = [ctx.enter_context(nc.psum_tensor(f"misc{i}", [P, 512], F32)) for i in range(NMISC)]

        ident = sb("ident", [P, P])
        identb = sb("identb", [P, P], BF16)
        rope = sb("rope", [P, 2, 2, TILES, HD])
        band = sb("band", [P, P + 2 * WIN])
        rank = sb("rank", [P, NE])
        mhalf = sb("mhalf", [P, 4])
        ones = sb("ones", [P, P])
        nw = [sb("nw_g", [P, 1]), sb("nw_l", [P, 1])]
        wraw = two("wraw", [P, PW])
        wqkv = two("wqkv", [P, PW])
        wo_sb = two("wo", [P, P])
        kvd = sb("kvd", [P, 32])
        kvdT = sb("kvdT", [32, P])
        kvup = sb("kvup", [32, 64])
        gamma = sb("gamma", [P, 1])
        beta = sb("beta", [P, 1])
        rw = sb("rw", [NE, P])
        rwT = sb("rwT", [P, NE])
        early = sb("early", [P, 2 * (NE + 1) * FT * P])
        w1n = early[:, 0:(NE + 1) * FT * P].rearrange("p (k d) -> p k d", d=P)
        w2n = early[:, (NE + 1) * FT * P:].rearrange("p (k d) -> p k d", d=FT * P)
        s1c = sb("s1c", [P, NE * FT + FT])
        s2c = sb("s2c", [P, NE + 1])
        half1 = sb("half1", [P, 2, NE * FT + FT])
        half2 = sb("half2", [P, 2, NE + 1])
        early2 = sb("early2", [P, 2 * (NE + 1) * FT * P])
        NW = (NE + 1) * FT * P
        tb = early2[:].bitcast(BF16)
        t1, t1b = [tb[:, k * NW:k * NW + NW].rearrange("p (k d) -> p k d", d=P) for k in (0, 1)]
        t2, t2b = [tb[:, k * NW:k * NW + NW].rearrange("p (k d) -> p k d", d=FT * P) for k in (2, 3)]
        t1T = sb("t1T", [P, NE * FT + FT, P], BF16)
        t2T = sb("t2T", [P, FT, NE + 1, P], BF16)
        s1p = sb("s1p", [P, FT, 3, NE], BF16)
        s1q = sb("s1q", [P, FT, NE])
        s2p = sb("s2p", [P, 3, NE], BF16)
        s2q = sb("s2q", [P, NE])
        s1pT = sb("s1pT", [3 * NE, FT, P], BF16)
        s2pT = sb("s2pT", [3 * NE, P], BF16)
        s2diag = sb("s2diag", [P, P])
        s2row = sb("s2row", [P, P])

        X = sb("X", [P, TILES, P])
        Hn = sb("Hn", [P, 4, 2, P])
        X1 = sb("X1", [P, NB, 2, P])
        X2 = sb("X2", [P, 2, P])
        stats = two("stats", [P, 2, 6])
        mv = two("mv", [P, 2, 2])
        rs = two("rs", [P, 8, 2])
        xn = two("xn", [P, 2, P])
        xT = two("xT", [P, QB])
        cosp = two("cosp", [P, 2, QKW])
        sinp = two("sinp", [P, 2, QKW])
        qk = two("qk", [P, 2, QKW])
        ss = two("ss", [P, 2 * (H + KVH)])
        nv = two("nv", [P, 2 * (H + KVH)])
        ny = two("ny", [P, 2 * (H + KVH)])
        nt = two("nt", [P, 2 * (H + KVH)])
        qn = two("qn", [P, 2, QKW])
        res = two("res", [P, 2, QKW])
        part = two("part", [P, 3, 2, QKW], BF16)
        qe = two("qe", [P, 2, H, TERMS, HD], BF16)
        ke = two("ke", [P, 2, KVH, TERMS, HD], BF16)
        qT = two("qT", [P, 2, H // 2, QB], BF16)
        kept = [TILES, 4]
        kT = [sb(f"kT{a}", [P, KVH, kept[a] * P], BF16) for a in (G, L)]
        V = [sb(f"V{a}", [P, kept[a], KVH, 32]) for a in (G, L)]
        prob = sb("prob", [P, NP, 4, QB])
        oTs = two("oTs", [P, KVH, QB])
        rec = two("rec", [P, H])
        on = two("on", [P, 2, P])
        onT = two("onT", [P, QB])

        fst = sb("fst", [P, 3, 2, 6])
        fmv = sb("fmv", [P, 3, 2, 2])
        frs = sb("frs", [P, 10, 2])
        ftmp = sb("ftmp", [P, 2, P])
        xa = sb("xa", [P, 2, P])
        fh = sb("fh", [P, 2, P])
        hT = sb("hT", [P, QB])
        hres = sb("hres", [P, QB])
        hp = sb("hp", [P, 3, QB], BF16)
        lmax = sb("lmax", [P, 2])
        lsh = sb("lsh", [P, 2, NE])
        lex = sb("lex", [P, 2, NE])
        lsum = sb("lsum", [P, 2])
        tp = sb("tp", [P, 2])
        leq = sb("leq", [P, 2, NE])
        lrk = sb("lrk", [P, 2, NE])
        lbest = sb("lbest", [P, 2])
        oh = sb("oh", [P, 2, 3, NE], BF16)
        ohT = sb("ohT", [3 * NE, QB], BF16)
        hm = early[:].bitcast(BF16)[:, 0:NE * 3 * QB].rearrange("p (e a q) -> p e a q", e=NE, a=3)
        s1s = sb("s1s", [P, FT, QB])
        z, ez, zr, h1 = [early2[:, 2 * FT * QB * k:2 * FT * QB * (k + 1)].rearrange("p (f q) -> p f q", q=QB)
                         for k in range(4)]
        h1p = sb("h1p", [P, 3, 2 * FT, QB], BF16)
        sel = sb("sel", [P, NE, P])
        acc = sb("acc", [P, P])
        accs = sb("accs", [P, P])
        shd = sb("shd", [P, P])
        fo = sb("fo", [P, P])
        fl = sb("fl", [P, P])
        yout = sb("yout", [P, 2, P])

        x_in = [sem(f"x_in{b}") for b in range(NB)]
        small_in = sem("small_in")
        wa_in = sem("wa_in")
        wf_in = sem("wf_in")
        y_out = sem("y_out")
        dch = sem("dch")
        pch = sem("pch")
        ach = sem("ach")
        const_ready = sem("const_ready")
        bank_full = [sem(f"bank_full{i}") for i in range(NMISC)]
        bank_free = [sem(f"bank_free{i}") for i in range(NMISC)]
        wqkv_ready = sem("wqkv_ready")
        tern_ready = sem("tern_ready")
        scale_ready = sem("scale_ready")
        prep_read = sem("prep_read")
        mv_ready = pair("mv_ready")
        rs_ready = pair("rs_ready")
        xn_ready = pair("xn_ready")
        xT_ready = pair("xT_ready")
        v_ready = pair("v_ready")
        ss_ready = pair("ss_ready")
        ny_ready = pair("ny_ready")
        part_ready = pair("part_ready")
        term_ready = pair("term_ready")
        qT_ready = pair("qT_ready")
        kT_ready = pair("kT_ready")
        qk_done = sem("qk_done")
        exp_done = sem("exp_done")
        mask_done = sem("mask_done")
        pv_done = sem("pv_done")
        o_free = sem("o_free")
        oT_ready = pair("oT_ready")
        on_ready = pair("on_ready")
        onT_ready = pair("onT_ready")
        fmv_ready = sem("fmv_ready")
        frs_ready = sem("frs_ready")
        fh_ready = sem("fh_ready")
        hT_ready = sem("hT_ready")
        lsh_ready = sem("lsh_ready")
        lex_ready = sem("lex_ready")
        oh_ready = sem("oh_ready")
        ohT_ready = sem("ohT_ready")
        hm_ready = sem("hm_ready")
        hp_ready = sem("hp_ready")
        s1s_ready = sem("s1s_ready")
        z_ready = sem("z_ready")
        ez_ready = sem("ez_ready")
        den_ready = sem("den_ready")
        h1p_ready = sem("h1p_ready")
        y_ready = sem("y_ready")

        def bank(step, j=0):
            return misc[TAKE[(*step, j)][0]]

        def take(pe, step, j=0):
            i, n = TAKE[(*step, j)]
            if n:
                pe.wait_ge(bank_free[i], n)

        def full(step, j=0):
            return bank_full[TAKE[(*step, j)][0]]

        def free(step, j=0):
            return bank_free[TAKE[(*step, j)][0]]

        def wait_full(eng, step, j=0):
            i, n = TAKE[(*step, j)]
            eng.wait_ge(bank_full[i], n + 1)

        x_v = x.rearrange("a (t p) d -> p (a t) d", p=P)
        out_v = out.rearrange("a (t p) d -> p (a t) d", p=P)
        col = lambda w: w.rearrange("(p a) -> p a", a=1)

        block = ctx.enter_context(nc.Block())

        @block.sync
        def _(sp):
            sp.dma_start(X[:, 0:2, :], x_v[:, 0:2, :]).then_inc(x_in[0], 16)
            sp.dma_start(ident[:], ident_d).then_inc(small_in, 16)
            sp.dma_start(rope[:], rope_d).then_inc(small_in, 16)
            sp.dma_start(wraw[G][:, 0:P], g_wq).then_inc(wa_in, 16)
            sp.dma_start(kvd[:], g_kv_down).then_inc(wa_in, 16)
            sp.dma_start(kvup[:, 0:32], g_k_up).then_inc(wa_in, 16)
            sp.dma_start(kvup[:, 32:64], g_v_up).then_inc(wa_in, 16)
            sp.dma_start(nw[G][:], col(norm1_w)).then_inc(wa_in, 16)
            sp.dma_start(rw[:], router_w).then_inc(wa_in, 16)
            for b in range(1, NB):
                sp.dma_start(X[:, 2 * b:2 * b + 2, :], x_v[:, 2 * b:2 * b + 2, :]).then_inc(x_in[b], 16)
            for b in range(NB):
                for i in range(2):
                    sp.wait_ge(y_ready, 2 * b + i + 1)
                    sp.dma_start(out_v[:, 2 * b + i, :], yout[:, i, :]).then_inc(y_out, 16)
            sp.wait_ge(y_out, 16 * TILES)

        @block.gpsimd
        def _(pool):
            chain = [0]

            def link(ins):
                chain[0] += 1
                ins.then_inc(pch, 1)
                pool.wait_ge(pch, chain[0])

            def weights():
                pool.memset(mhalf[:], -0.5).then_inc(const_ready, 1)
                pool.memset(ones[:], 1.0).then_inc(const_ready, 1)
                pool.memset(V[G][:], 1.0).then_inc(const_ready, 1)
                pool.memset(V[L][:], 1.0).then_inc(const_ready, 1)
                pool.wait_ge(const_ready, 4)
                pool.dma_start(wraw[L][:, 0:P], l_wq).then_inc(wf_in, 16)
                pool.dma_start(wraw[L][:, P:QKW], l_wk).then_inc(wf_in, 16)
                pool.dma_start(wraw[L][:, QKW:PW], l_wv).then_inc(wf_in, 16)
                pool.dma_start(nw[L][:], col(norm2_w)).then_inc(wf_in, 16)
                pool.dma_start(wo_sb[G][:], g_wo).then_inc(wf_in, 16)
                pool.dma_start(wo_sb[L][:], l_wo).then_inc(wf_in, 16)
                pool.dma_start(band[:], band_d).then_inc(wf_in, 16)
                pool.dma_start(rank[:], rank_d).then_inc(wf_in, 16)
                pool.dma_start(gamma[:], col(ln_gamma)).then_inc(wf_in, 16)
                pool.dma_start(beta[:], col(ln_beta)).then_inc(wf_in, 16)
                pool.dma_start(w1n[:, 0:NE * FT, :], ew1.rearrange("e (t p) d -> p (e t) d", p=P)).then_inc(wf_in, 16)
                pool.dma_start(w1n[:, NE * FT:, :], sw1.rearrange("(t p) d -> p t d", p=P)).then_inc(wf_in, 16)
                pool.dma_start(w2n[:, 0:NE, :], ew2.rearrange("e p f -> p e f")).then_inc(wf_in, 16)
                pool.dma_start(w2n[:, NE, :], sw2).then_inc(wf_in, 16)

            def rsqrt(out, value, eps):
                link(pool.tensor_scalar(out, value, 1.0, eps, ALU.mult, ALU.add))
                link(pool.tensor_tensor(out, out, mhalf[:, 0:2], ALU.pow))

            def norm(a, b):
                r, m, v = rs[a], mv[a][:, :, 0], mv[a][:, :, 1]
                pool.wait_ge(mv_ready[a], b + 1)
                if a == G:
                    if b:
                        pool.wait_ge(xn_ready[a], b)
                    rsqrt(r[:, 0, :], v, EPS_LN)
                    link(pool.tensor_tensor(r[:, 1, :], r[:, 0, :], r[:, 0, :], ALU.mult))
                    link(pool.tensor_tensor(r[:, 1, :], r[:, 1, :], v, ALU.mult))
                    rsqrt(r[:, 2, :], r[:, 1, :], EPS_RMS)
                    pool.tensor_tensor(r[:, 3, :], r[:, 0, :], r[:, 2, :], ALU.mult).then_inc(rs_ready[a], 1)
                else:
                    if b:
                        pool.wait_ge(xn_ready[a], b)
                    link(pool.tensor_tensor(r[:, 1, :], m, m, ALU.mult))
                    link(pool.tensor_tensor(r[:, 1, :], r[:, 1, :], v, ALU.add))
                    link(pool.tensor_scalar(r[:, 1, :], r[:, 1, :], 1.0, EPS_RMS, ALU.mult, ALU.add))
                    pool.tensor_tensor(r[:, 3, :], r[:, 1, :], mhalf[:, 0:2], ALU.pow).then_inc(rs_ready[a], 1)

            def proj(a, b):
                v, y, t = nv[a][:], ny[a][:], nt[a][:]
                pool.wait_ge(ss_ready[a], b + 1)
                if b:
                    pool.wait_ge(part_ready[a], b)
                link(pool.tensor_scalar(v, ss[a][:], 1.0 / HD, EPS_RMS, ALU.mult, ALU.add))
                link(pool.tensor_scalar(y.bitcast(I32), v.bitcast(I32), -0.5, MAGIC, ALU.mult, ALU.add))
                for k in range(3):
                    link(pool.tensor_tensor(t, y, y, ALU.mult))
                    link(pool.tensor_tensor(t, t, v, ALU.mult))
                    link(pool.tensor_scalar(t, t, -0.5, 1.5, ALU.mult, ALU.add))
                    ins = pool.tensor_tensor(y, y, t, ALU.mult)
                    if k < 2:
                        link(ins)
                ins.then_inc(ny_ready[a], 1)

            def split(a, b):
                pool.wait_ge(part_ready[a], b + 1)
                if b:
                    pool.wait_ge(kT_ready[a], b)
                    pool.wait_ge(qT_ready[a], 2 * b)
                for i in range(2):
                    for p, (lo, n) in enumerate([(0, 3), (3, 3), (6, 2)]):
                        src = part[a][:, p, i, 0:P].rearrange("p (h d) -> p h d", d=HD)
                        pool.tensor_scalar(qe[a][:, i, :, lo:lo + n, :], src.unsqueeze(2).broadcast_to([P, H, n, HD]),
                                           1.0, 0.0, ALU.mult, ALU.add)
                    for p in range(3):
                        src = part[a][:, p, i, P:QKW].rearrange("p (h d) -> p h d", d=HD)
                        n = 3 if p < 2 else 2
                        ins = pool.tensor_scalar(ke[a][:, i, :, p::3, :], src.unsqueeze(2).broadcast_to([P, KVH, n, HD]),
                                                 1.0, 0.0, ALU.mult, ALU.add)
                ins.then_inc(term_ready[a], 1)

            def qkmask(*u):
                if u not in MASK:
                    return
                a, b, g, kb = u
                p = prob[:, UNIT[u] % NP, :, :]
                pool.wait_ge(exp_done, UNIT[u] + 1)
                if a == G:
                    d = p[:, :, P * (kb - 2 * b):P * (kb - 2 * b) + P]
                    pool.affine_select(out=d, in_=d, compare_op=ALU.is_ge, fill=0.0, base=0,
                                       pattern=[[0, 4], [1, P]], channel_multiplier=-1).then_inc(mask_done, 1)
                else:
                    pool.wait_ge(wf_in, 16 * 14)
                    lo, n = (0, P) if kb else (0 if b else WIN, P + 2 * WIN - (0 if b else WIN))
                    m = band[:, (WIN if kb else lo):(WIN if kb else lo) + n]
                    d = p[:, :, lo:lo + n]
                    pool.tensor_tensor(d, d, m.unsqueeze(1).broadcast_to([P, 4, n]), ALU.mult).then_inc(mask_done, 1)

            def fnorm(b):
                r = frs
                pool.wait_ge(fmv_ready, 3 * b + b * 1 + 1)
                rsqrt(r[:, 0, :], fmv[:, 0, :, 1], EPS_LN)
                pool.tensor_tensor(r[:, 1, :], r[:, 0, :], fmv[:, 0, :, 0], ALU.mult).then_inc(frs_ready, 1)
                pool.wait_ge(fmv_ready, 4 * b + 2)
                rsqrt(r[:, 2, :], fmv[:, 1, :, 1], EPS_LN)
                link(pool.tensor_tensor(r[:, 3, :], r[:, 2, :], r[:, 2, :], ALU.mult))
                link(pool.tensor_tensor(r[:, 3, :], r[:, 3, :], fmv[:, 1, :, 1], ALU.mult))
                rsqrt(r[:, 4, :], r[:, 3, :], EPS_LN)
                pool.tensor_tensor(r[:, 5, :], r[:, 2, :], r[:, 4, :], ALU.mult).then_inc(frs_ready, 1)

            def fact(b):
                pool.wait_ge(ez_ready, b + 1)
                pool.tensor_scalar(ez[:], ez[:], 1.0, 1.0, ALU.mult, ALU.add).then_inc(den_ready, 1)

            def fw2s(b, i):
                pool.wait_ge(fmv_ready, 4 * b + 3 + i)
                link(pool.tensor_scalar(frs[:, 6 + i, 0:1], fmv[:, 2, i, 1:2], 1.0, EPS_LN, ALU.mult, ALU.add))
                pool.tensor_tensor(frs[:, 6 + i, 1:2], frs[:, 6 + i, 0:1], mhalf[:, 0:1], ALU.pow).then_inc(frs_ready, 1)

            run = {"weights": weights, "norm": norm, "proj": proj, "split": split, "qk": qkmask,
                   "fnorm": fnorm, "fact": fact, "fw2s": fw2s}
            for kind, *at in PLAN:
                if kind in run:
                    run[kind](*at)

        @block.scalar
        def _(act):
            def norm(a, b):
                pass

            def xT_copy(a, b):
                s = ("xT", a, b)
                wait_full(act, s)
                if b:
                    act.wait_ge(v_ready[a], b)
                act.copy(xT[a][:], bank(s)[:, 0:QB]).then_inc(free(s), 1)

            def exp(*u):
                n = UNIT[u]
                a, b, g, kb = u
                act.wait_ge(qk_done, n + 1)
                if n >= NP:
                    act.wait_ge(pv_done, PV[UNIT_LIST[n - NP]] + 1)
                ps = pieces(a, b, kb)
                lo, hi = ps[0][3], ps[-1][3] + ps[-1][2]
                src = scores[n % 2][:].rearrange("p (m q) -> p m q", m=4)[:, :, lo:hi]
                act.activation(prob[:, n % NP, :, lo:hi], src, ACT.Exp, scale=float(HD) ** -0.5).then_inc(exp_done, 1)

            def onT_copy(a, b):
                s = ("onT", a, b)
                wait_full(act, s)
                act.copy(onT[a][:], bank(s)[:, 0:QB]).then_inc(free(s), 1)

            def fhT(b):
                s = ("fhT", b)
                wait_full(act, s)
                act.activation(hT[:], bank(s)[:, 0:QB], ACT.Identity, scale=gamma[:, 0:1],
                               bias=beta[:, 0:1]).then_inc(free(s), 1)

            def frouter(b):
                act.wait_ge(lsh_ready, b + 1)
                act.activation(lex[:], lsh[:], ACT.Exp).then_inc(lex_ready, 1)

            def fw1s(b):
                s = ("fw1s", b)
                wait_full(act, s, 0)
                act.copy(s1s[:].rearrange("p t q -> p (t q)"), bank(s, 0)[:]).then_inc(free(s, 0), 1)

            def fact(b):
                act.wait_ge(z_ready, b + 1)
                act.activation(ez[:], z[:], ACT.Exp, scale=-1.0).then_inc(ez_ready, 1)

            run = {"xT": xT_copy, "qk": exp, "onT": onT_copy, "fhT": fhT, "frouter": frouter,
                   "fw1s": fw1s, "fact": fact}
            for kind, *at in PLAN:
                if kind in run:
                    run[kind](*at)

        @block.tensor
        def _(pe):
            def weights():
                s = ("weights",)
                pe.wait_ge(small_in, 32)
                pe.wait_ge(wa_in, 16 * 6)
                take(pe, s, 0)
                pe.transpose(bank(s, 0)[0:32, 0:P], kvd[:], ident[:]).then_inc(full(s, 0), 1)
                pe.wait_ge(free(s, 0), 1)
                pe.matmul(bank(s, 1)[:, 0:64], kvdT[:], kvup[:], start=True, stop=True).then_inc(full(s, 1), 1)
                pe.transpose(bank(s, 2)[:, 0:NE], rw[:], ident[0:NE, 0:NE]).then_inc(full(s, 2), 1)

            def wturn(k):
                s = ("wturn", k)
                pe.wait_ge(tern_ready, k + 1)
                take(pe, s)
                for m, (w, r, c) in enumerate(TURNS[k]):
                    src = t1[:, r, :] if w == 1 else t2[:, r, P * c:P * c + P]
                    ins = pe.transpose(bank(s)[:].bitcast(BF16)[:, P * m:P * m + P], src, identb[:])
                ins.then_inc(full(s), 1)

            def scales():
                s = ("scales",)
                pe.wait_ge(scale_ready, 1)
                take(pe, s, 0)
                o = bank(s, 0)[0:3 * NE, :].bitcast(BF16)
                for m in range(FT):
                    pe.transpose(o[:, P * m:P * m + P], s1p[:, m, :, :].rearrange("p a e -> p (a e)"), identb[:])
                pe.transpose(o[:, P * FT:P * FT + P], s2p[:].rearrange("p a e -> p (a e)"),
                             identb[:]).then_inc(full(s, 0), 1)
                take(pe, s, 1)
                pe.wait_ge(const_ready, 4)
                pe.matmul(bank(s, 1)[:, 0:P], ones[:], s2diag[:], start=True, stop=True).then_inc(full(s, 1), 1)

            def xT_turn(a, b):
                s = ("xT", a, b)
                pe.wait_ge(xn_ready[a], b + 1)
                take(pe, s)
                for i in range(2):
                    ins = pe.transpose(bank(s)[:, P * i:P * i + P], xn[a][:, i, :], ident[:])
                ins.then_inc(full(s), 1)

            def proj(a, b):
                s = ("proj", a, b)
                if b == 0:
                    pe.wait_ge(wqkv_ready, 1 + a)
                i, n = TAKE[("xT", a, b, 0)]
                pe.wait_ge(bank_free[i], n + 1)
                take(pe, s)
                for i in range(2):
                    ins = pe.matmul(bank(s)[:, PW * i:PW * i + PW], xT[a][:, P * i:P * i + P], wqkv[a][:],
                                    start=True, stop=True)
                ins.then_inc(full(s), 1)

            def k_turn(a, b):
                s = ("kT", a, b)
                pe.wait_ge(term_ready[a], b + 1)
                take(pe, s)
                o = bank(s)[:].bitcast(BF16)
                for g in range(KVH):
                    for i in range(2):
                        src = ke[a][:, i, g, :, :].rearrange("p t d -> p (t d)")
                        for half in range(2):
                            ins = pe.transpose(o[64 * half:64 * half + 64, P * (2 * g + i):P * (2 * g + i) + P], src, identb[:])
                ins.then_inc(full(s), 1)

            def q_turn(a, b, i):
                s = ("qT", a, b, i)
                pe.wait_ge(term_ready[a], b + 1)
                take(pe, s)
                o = bank(s)[:].bitcast(BF16)
                for m in range(H // 2):
                    ins = pe.transpose(o[:, P * m:P * m + P],
                                       qe[a][:, i, 2 * m:2 * m + 2, :, :].rearrange("p h t d -> p (h t d)"), identb[:])
                ins.then_inc(full(s), 1)

            def qk_product(*u):
                a, b, g, kb = u
                n = UNIT[u]
                pe.wait_ge(qT_ready[a], 2 * b + 2)
                pe.wait_ge(kT_ready[a], b + 1)
                if n >= 2:
                    pe.wait_ge(exp_done, n - 1)
                for m in range(4):
                    r = 64 * (m % 2)
                    for t, q, w, c in pieces(a, b, kb):
                        c += 256 * SLOT_OF[m]
                        ins = pe.matmul(scores[n % 2][:, c:c + w], kT[a][r:r + 64, g, P * (t % kept[a]):P * (t % kept[a]) + P],
                                        qT[a][r:r + 64, b % 2, 2 * g + m // 2, q:q + w], start=True, stop=True)
                ins.then_inc(qk_done, 1)

            def pv_product(*u):
                a, b, g, kb = u
                n = UNIT[u]
                if a == G:
                    o = osum_g
                    if kb == 0 and OSUM[(b, g)]:
                        pe.wait_ge(o_free, OSUM[(b, g)])
                else:
                    s = ("pv", L, b, g, 0)
                    if kb == 0:
                        take(pe, s)
                    o = bank(s)
                pe.wait_ge(v_ready[a], b + 1)
                if u in MASK:
                    pe.wait_ge(mask_done, MASK[u] + 1)
                else:
                    pe.wait_ge(exp_done, n + 1)
                ps = pieces(a, b, kb)
                for k, (t, q, w, c) in enumerate(ps):
                    last = kb == (2 * b + 1 if a == G else 1)
                    for m in range(4):
                        ins = pe.matmul(o[32 * m:32 * m + 32, q:q + w], V[a][:, t % kept[a], g, :],
                                        prob[:, n % NP, SLOT_OF[m], c:c + w], start=(kb == 0 and k == 0), stop=last,
                                        skip_group_check=True)
                        if a == L and kb == 1 and m == 2:
                            ins.then_inc(full(s), 1)
                ins.then_inc(pv_done, 1)

            def o_turn(a, b, i):
                s = ("oT", a, b, i)
                pe.wait_ge(oT_ready[a], KVH * (b + 1))
                take(pe, s)
                for g in range(KVH):
                    ins = pe.transpose(bank(s)[:, P * g:P * g + P], oTs[a][:, g, P * i:P * i + P], ident[:])
                ins.then_inc(full(s), 1)

            def on_turn(a, b):
                s = ("onT", a, b)
                pe.wait_ge(on_ready[a], 2 * b + 2)
                take(pe, s)
                for i in range(2):
                    ins = pe.transpose(bank(s)[:, P * i:P * i + P], on[a][:, i, :], ident[:])
                ins.then_inc(full(s), 1)

            def wo_product(a, b):
                s = ("wo", a, b)
                if a == G and b == 0:
                    pe.wait_ge(wf_in, 16 * 14)
                i, n = TAKE[("onT", a, b, 0)]
                pe.wait_ge(bank_free[i], n + 1)
                take(pe, s)
                for i in range(2):
                    ins = pe.matmul(bank(s)[:, P * i:P * i + P], onT[a][:, P * i:P * i + P], wo_sb[a][:],
                                    start=True, stop=True)
                ins.then_inc(full(s), 1)

            def fhT(b):
                s = ("fhT", b)
                pe.wait_ge(fh_ready, b + 1)
                take(pe, s)
                for i in range(2):
                    ins = pe.transpose(bank(s)[:, P * i:P * i + P], fh[:, i, :], ident[:])
                ins.then_inc(full(s), 1)

            def frouter(b):
                s = ("frouter", b)
                i, n = TAKE[("fhT", b, 0)]
                pe.wait_ge(bank_free[i], n + 1)
                take(pe, s)
                for i in range(2):
                    ins = pe.matmul(bank(s)[:, NE * i:NE * i + NE], hT[:, P * i:P * i + P], rwT[:], start=True, stop=True)
                ins.then_inc(full(s), 1)

            def fohT(b):
                s = ("fohT", b)
                pe.wait_ge(oh_ready, b + 1)
                take(pe, s)
                for i in range(2):
                    ins = pe.transpose(bank(s)[0:24, :].bitcast(BF16)[:, P * i:P * i + P],
                                       oh[:, i, :, :].rearrange("p a e -> p (a e)"), identb[:])
                ins.then_inc(full(s), 1)

            def fmask(b, i):
                s = ("fmask", b, i)
                pe.wait_ge(oh_ready, b + 1)
                take(pe, s)
                for e in range(NE):
                    ins = pe.transpose(bank(s)[:].bitcast(BF16)[:, P * e:P * e + P],
                                       oh[:, i, 0, e:e + 1].broadcast_to([P, P]), identb[:])
                ins.then_inc(full(s), 1)

            def fw1s(b):
                s = ("fw1s", b)
                pe.wait_ge(ohT_ready, b + 1)
                take(pe, s, 0)
                for f in range(FT):
                    ins = pe.matmul(bank(s, 0)[:, QB * f:QB * f + QB], s1pT[:, f, :], ohT[:], start=True, stop=True)
                ins.then_inc(full(s, 0), 1)
                pe.wait_ge(hp_ready, b + 1)
                take(pe, s, 1)
                for f in range(FT):
                    for p in range(3):
                        ins = pe.matmul(bank(s, 1)[:, QB * f:QB * f + QB], t1T[:, NE * FT + f, :], hp[:, p, :],
                                        start=(p == 0), stop=(p == 2))
                ins.then_inc(full(s, 1), 1)

            def fw1(b, f):
                s = ("fw1", b, f)
                pe.wait_ge(hm_ready, 2 * b + 2)
                take(pe, s)
                for e in range(NE):
                    for p in range(3):
                        ins = pe.matmul(bank(s)[:, 0:QB], t1T[:, FT * e + f, :], hm[:, e, p, :],
                                        start=(e == 0 and p == 0), stop=(e == NE - 1 and p == 2))
                ins.then_inc(full(s), 1)

            def fw2(b, i):
                s = ("fw2", b, i)
                pe.wait_ge(h1p_ready, b + 1)
                for j in range(2):
                    take(pe, s, j)
                    for p in range(3):
                        for f in range(FT):
                            ins = pe.matmul(bank(s, j)[:], h1p[:, p, f, P * i:P * i + P],
                                            t2T[:, f, 4 * j:4 * j + 4, :].rearrange("p e d -> p (e d)"),
                                            start=(p == 0 and f == 0), stop=(p == 2 and f == FT - 1))
                    ins.then_inc(full(s, j), 1)

            def fw2s(b, i):
                s = ("fw2s", b, i)
                take(pe, s)
                for p in range(3):
                    for f in range(FT):
                        pe.matmul(bank(s)[:, 0:P], h1p[:, p, FT + f, P * i:P * i + P], t2T[:, f, NE, :],
                                  start=(p == 0 and f == 0), stop=(p == 2 and f == FT - 1))
                pe.matmul(bank(s)[:, P:2 * P], ohT[:, P * i:P * i + P], s2pT[:], start=True, stop=True).then_inc(full(s), 1)

            run = {"weights": weights, "wturn": wturn, "scales": scales, "xT": xT_turn, "proj": proj, "kT": k_turn, "qT": q_turn,
                   "qk": qk_product, "pv": pv_product, "oT": o_turn, "onT": on_turn, "wo": wo_product, "fhT": fhT,
                   "frouter": frouter, "fohT": fohT, "fmask": fmask, "fw1s": fw1s, "fw1": fw1, "fw2": fw2,
                   "fw2s": fw2s}
            for kind, *at in PLAN:
                if kind in run:
                    run[kind](*at)

        @block.vector
        def _(dve):
            chain = [0]

            def link(ins):
                chain[0] += 1
                ins.then_inc(dch, 1)
                dve.wait_ge(dch, chain[0])

            def weights():
                s = ("weights",)
                dve.wait_ge(small_in, 32)
                dve.wait_ge(wa_in, 16 * 6)
                dve.tensor_copy(identb[:], ident[:]).then_inc(prep_read, 1)
                wait_full(dve, s, 0)
                dve.tensor_copy(kvdT[:], bank(s, 0)[0:32, 0:P]).then_inc(free(s, 0), 1)
                dve.tensor_scalar(wqkv[G][:, 0:P], wraw[G][:, 0:P], nw[G][:, 0:1], None, ALU.mult)
                wait_full(dve, s, 1)
                link(dve.tensor_scalar(wqkv[G][:, P:PW], bank(s, 1)[:, 0:64], nw[G][:, 0:1], None, ALU.mult))
                dve.sem_inc(free(s, 1), 1)
                dve.sem_inc(wqkv_ready, 1)
                wait_full(dve, s, 2)
                dve.tensor_copy(rwT[:], bank(s, 2)[:, 0:NE]).then_inc(free(s, 2), 1)

            def prep():
                dve.wait_ge(wf_in, 16 * 14)
                dve.tensor_scalar(wqkv[L][:], wraw[L][:], nw[L][:, 0:1], None, ALU.mult).then_inc(wqkv_ready, 1)
                link(dve.tensor_reduce(s1c[:], w1n, AX.X, ALU.add, apply_absolute_value=True))
                link(dve.tensor_reduce(s2c[:], w2n, AX.X, ALU.add, apply_absolute_value=True))
                link(dve.tensor_scalar(s1c[:], s1c[:], 1.0 / P, 1e-5, ALU.mult, ALU.max))
                link(dve.tensor_scalar(s2c[:], s2c[:], 1.0 / (FT * P), 1e-5, ALU.mult, ALU.max))
                dve.tensor_scalar(half1[:, 0, :], s1c[:], 0.5, None, ALU.mult)
                dve.tensor_scalar(half2[:, 0, :], s2c[:], 0.5, None, ALU.mult)
                dve.tensor_scalar(half1[:, 1, :], s1c[:], -0.5, None, ALU.mult)
                link(dve.tensor_scalar(half2[:, 1, :], s2c[:], -0.5, None, ALU.mult))
                dve.tensor_scalar(s2diag[:], ident[:], s2c[:, NE:NE + 1], None, ALU.mult)
                v = s1c[:, 0:NE * FT].rearrange("p (e f) -> p f e", f=FT)
                link(dve.tensor_copy(s1p[:, :, 0, :], v))
                link(dve.tensor_tensor(s1q[:], v, s1p[:, :, 0, :], ALU.subtract))
                link(dve.tensor_copy(s1p[:, :, 1, :], s1q[:]))
                link(dve.tensor_tensor(s1p[:, :, 2, :], s1q[:], s1p[:, :, 1, :], ALU.subtract))
                link(dve.tensor_copy(s2p[:, 0, :], s2c[:, 0:NE]))
                link(dve.tensor_tensor(s2q[:], s2c[:, 0:NE], s2p[:, 0, :], ALU.subtract))
                link(dve.tensor_copy(s2p[:, 1, :], s2q[:]))
                dve.tensor_tensor(s2p[:, 2, :], s2q[:], s2p[:, 1, :], ALU.subtract).then_inc(scale_ready, 1)

            def ternary(k):
                rows = sorted({(w, r) for w, r, _ in TURNS[k]})
                for w, r in rows:
                    raw, low, half = (w1n, t1b, half1) if w == 1 else (w2n, t2b, half2)
                    ins = dve.tensor_scalar(low[:, r, :], raw[:, r, :], half[:, 1, r:r + 1], None, ALU.is_lt)
                link(ins)
                for w, r in rows:
                    raw, low, half, t = (w1n, t1b, half1, t1) if w == 1 else (w2n, t2b, half2, t2)
                    ins = dve.scalar_tensor_tensor(out=t[:, r, :], in0=raw[:, r, :], scalar=half[:, 0, r:r + 1],
                                                   in1=low[:, r, :], op0=ALU.is_gt, op1=ALU.subtract)
                ins.then_inc(tern_ready, 1)

            def wturn(k):
                s = ("wturn", k)
                wait_full(dve, s)
                src = bank(s)[:].bitcast(BF16)
                if k < 2:
                    ins = dve.tensor_copy(t1T[:, 8 * k:8 * k + 8, :].rearrange("p k d -> p (k d)"), src)
                elif k == 2:
                    dve.tensor_copy(t1T[:, 16:18, :].rearrange("p k d -> p (k d)"), src[:, 0:2 * P])
                    ins = dve.tensor_copy(t2T[:, :, NE, :], src[:, 2 * P:4 * P].rearrange("p (f d) -> p f d", f=FT))
                else:
                    e = 4 * (k - 3)
                    ins = dve.tensor_copy(t2T[:, :, e:e + 4, :], src.rearrange("p (e f d) -> p f e d", f=FT, d=P))
                link(ins)
                dve.sem_inc(free(s), 1)

            def scales():
                s = ("scales",)
                wait_full(dve, s, 0)
                src = bank(s, 0)[0:3 * NE, :].bitcast(BF16)
                dve.tensor_copy(s1pT[:].rearrange("p f d -> p (f d)"), src[:, 0:2 * P])
                link(dve.tensor_copy(s2pT[:], src[:, 2 * P:3 * P]))
                dve.sem_inc(free(s, 0), 1)
                wait_full(dve, s, 1)
                dve.tensor_copy(s2row[:], bank(s, 1)[:, 0:P]).then_inc(free(s, 1), 1)

            def norm(a, b):
                src = X[:, 2 * b:2 * b + 2, :] if a == G else X1[:, b, :, :]
                if a == G:
                    dve.wait_ge(x_in[b], 16)
                for i in range(2):
                    ins = dve.bn_stats(stats[a][:, i, :], src[:, i, :])
                link(ins)
                for i in range(2):
                    ins = dve.bn_aggr(mv[a][:, i, :], stats[a][:, i, :])
                ins.then_inc(mv_ready[a], 1)
                dve.wait_ge(rs_ready[a], b + 1)
                if b:
                    i, n = TAKE[("xT", a, b - 1, 0)]
                    dve.wait_ge(bank_full[i], n + 1)
                for i in range(2):
                    if a == G:
                        dve.tensor_scalar(Hn[:, b % 4, i, :], src[:, i, :], mv[a][:, i, 0:1], rs[a][:, 0, i:i + 1],
                                          ALU.subtract, ALU.mult)
                        ins = dve.tensor_scalar(xn[a][:, i, :], src[:, i, :], mv[a][:, i, 0:1], rs[a][:, 3, i:i + 1],
                                                ALU.subtract, ALU.mult)
                    else:
                        ins = dve.tensor_scalar(xn[a][:, i, :], src[:, i, :], rs[a][:, 3, i:i + 1], None, ALU.mult)
                ins.then_inc(xn_ready[a], 1)

            def proj(a, b):
                s = ("proj", a, b)
                wait_full(dve, s)
                src = bank(s)[:, 0:2 * PW].rearrange("p (i w) -> p i w", i=2)[:, :, 0:QKW]
                s4 = src.rearrange("p i (h d) -> p i h d", d=HD)
                c4, n4 = [t[a][:].rearrange("p i (h d) -> p i h d", d=HD) for t in (cosp, sinp)]
                tab = rope[:, a, :, 2 * b:2 * b + 2, :]

                def wide(t):
                    return t.unsqueeze(2).broadcast_to([P, 2, H + KVH, t.shape[2]])

                dve.tensor_tensor(c4, s4, wide(tab[:, 0]), ALU.mult)
                dve.tensor_tensor(n4[:, :, :, 0::2], s4[:, :, :, 1::2], wide(tab[:, 1, :, 0::2]), ALU.mult)
                link(dve.tensor_tensor(n4[:, :, :, 1::2], s4[:, :, :, 0::2], wide(tab[:, 1, :, 1::2]), ALU.mult))
                if a == G and b == 0:
                    dve.wait_ge(const_ready, 4)
                if a == L and b >= 2:
                    dve.wait_ge(pv_done, PV[(L, b - 1, KVH - 1, 1)] + 1)
                t = 2 * b % kept[a]
                vsrc = bank(s)[:, 0:2 * PW].rearrange("p (i w) -> p i w", i=2)[:, :, QKW:PW]
                dve.tensor_copy(V[a][:, t:t + 2, :, 0:HD],
                                vsrc.rearrange("p i (g d) -> p i g d", d=HD)).then_inc(v_ready[a], 1)
                dve.wait_ge(v_ready[a], b + 1)
                dve.sem_inc(free(s), 1)
                link(dve.tensor_tensor(qk[a][:], cosp[a][:], sinp[a][:], ALU.add))
                link(dve.tensor_tensor(cosp[a][:], qk[a][:], qk[a][:], ALU.mult))
                dve.tensor_reduce(ss[a][:], cosp[a][:].rearrange("p i (h d) -> p (i h) d", d=HD), AX.X,
                                  ALU.add).then_inc(ss_ready[a], 1)

            def split(a, b):
                dve.wait_ge(ny_ready[a], b + 1)
                if b:
                    dve.wait_ge(term_ready[a], b)
                y = ny[a][:].unsqueeze(2).broadcast_to([P, 2 * (H + KVH), HD])
                link(dve.tensor_tensor(qn[a][:].rearrange("p i (h d) -> p (i h) d", d=HD),
                                       qk[a][:].rearrange("p i (h d) -> p (i h) d", d=HD), y, ALU.mult))
                link(dve.tensor_copy(part[a][:, 0], qn[a][:]))
                link(dve.tensor_tensor(res[a][:], qn[a][:], part[a][:, 0], ALU.subtract))
                link(dve.tensor_copy(part[a][:, 1], res[a][:]))
                dve.tensor_tensor(part[a][:, 2], res[a][:], part[a][:, 1], ALU.subtract).then_inc(part_ready[a], 1)

            def k_copy(a, b):
                s = ("kT", a, b)
                wait_full(dve, s)
                if a == L and b >= 2:
                    dve.wait_ge(qk_done, UNIT[(L, b - 1, KVH - 1, 1)] + 1)
                k = P * (2 * b % kept[a])
                dve.tensor_copy(kT[a][:, :, k:k + QB],
                                bank(s)[:].bitcast(BF16).rearrange("p (g q) -> p g q", g=KVH)).then_inc(free(s), 1)
                dve.wait_ge(free(s), TAKE[(*s, 0)][1] + 1)
                dve.sem_inc(kT_ready[a], 1)

            def q_copy(a, b, i):
                s = ("qT", a, b, i)
                wait_full(dve, s)
                if b >= 2:
                    last = (a, b - 2, *units_of(a, b - 2)[-1])
                    dve.wait_ge(qk_done, UNIT[last] + 1)
                dve.tensor_copy(qT[a][:, b % 2, :, P * i:P * i + P],
                                bank(s)[:].bitcast(BF16).rearrange("p (m q) -> p m q", m=H // 2)).then_inc(free(s), 1)
                dve.wait_ge(free(s), TAKE[(*s, 0)][1] + 1)
                dve.sem_inc(qT_ready[a], 1)

            def o_copy(a, b, g):
                u = (a, b, g, 2 * b + 1 if a == G else 1)
                dve.wait_ge(pv_done, PV[u] + 1)
                if b:
                    i, n = TAKE[("oT", a, b - 1, 1, 0)]
                    dve.wait_ge(bank_full[i], n + 1)
                o, f = (osum_g, o_free) if a == G else (bank(("pv", L, b, g, 0)), free(("pv", L, b, g, 0)))
                link(dve.tensor_copy(oTs[a][:, g, :], o[:, 0:QB]))
                dve.sem_inc(f, 1)
                dve.sem_inc(oT_ready[a], 1)

            def o_scale(a, b, i):
                s = ("oT", a, b, i)
                wait_full(dve, s)
                if b:
                    j, n = TAKE[("onT", a, b - 1, 0)]
                    dve.wait_ge(bank_full[j], n + 1)
                o = bank(s)[:].rearrange("p (h c) -> p h c", c=32)
                link(dve.reciprocal(rec[a][:].unsqueeze(2), o[:, :, HD:HD + 1]))
                link(dve.tensor_tensor(on[a][:, i, :].rearrange("p (h d) -> p h d", d=HD), o[:, :, 0:HD],
                                       rec[a][:].unsqueeze(2).broadcast_to([P, H, HD]), ALU.mult))
                dve.sem_inc(free(s), 1)
                dve.sem_inc(on_ready[a], 1)

            def residual(a, b):
                s = ("wo", a, b)
                wait_full(dve, s)
                src = bank(s)[:, 0:QB].rearrange("p (i d) -> p i d", i=2)
                if a == G:
                    link(dve.tensor_tensor(X1[:, b], src, Hn[:, b % 4], ALU.add))
                else:
                    link(dve.tensor_tensor(X2[:], src, X1[:, b], ALU.add))
                dve.sem_inc(free(s), 1)

            def fnorm(b):
                for i in range(2):
                    ins = dve.bn_stats(fst[:, 0, i, :], X2[:, i, :])
                link(ins)
                for i in range(2):
                    ins = dve.bn_aggr(fmv[:, 0, i, :], fst[:, 0, i, :])
                ins.then_inc(fmv_ready, 1)
                dve.wait_ge(frs_ready, 4 * b + 1)
                for i in range(2):
                    ins = dve.tensor_scalar(ftmp[:, i, :], X2[:, i, :], frs[:, 0, i:i + 1], frs[:, 1, i:i + 1],
                                            ALU.mult, ALU.subtract)
                link(ins)
                link(dve.tensor_tensor(xa[:], X[:, 2 * b:2 * b + 2, :], ftmp[:], ALU.add))
                for i in range(2):
                    ins = dve.bn_stats(fst[:, 1, i, :], xa[:, i, :])
                link(ins)
                for i in range(2):
                    ins = dve.bn_aggr(fmv[:, 1, i, :], fst[:, 1, i, :])
                ins.then_inc(fmv_ready, 1)
                dve.wait_ge(frs_ready, 4 * b + 2)
                for i in range(2):
                    ins = dve.tensor_scalar(fh[:, i, :], xa[:, i, :], fmv[:, 1, i, 0:1], frs[:, 5, i:i + 1],
                                            ALU.subtract, ALU.mult)
                ins.then_inc(fh_ready, 1)

            def fhT(b):
                i, n = TAKE[("fhT", b, 0)]
                dve.wait_ge(bank_free[i], n + 1)
                link(dve.tensor_copy(hp[:, 0, :], hT[:]))
                link(dve.tensor_tensor(hres[:], hT[:], hp[:, 0, :], ALU.subtract))
                link(dve.tensor_copy(hp[:, 1, :], hres[:]))
                dve.tensor_tensor(hp[:, 2, :], hres[:], hp[:, 1, :], ALU.subtract).then_inc(hp_ready, 1)

            def frouter(b):
                s = ("frouter", b)
                wait_full(dve, s)
                lg = bank(s)[:, 0:2 * NE].rearrange("p (i e) -> p i e", i=2)
                wide = lambda t: t.unsqueeze(2).broadcast_to([P, 2, NE])
                link(dve.tensor_reduce(lmax[:], lg, AX.X, ALU.max))
                link(dve.tensor_tensor(lsh[:], lg, wide(lmax[:]), ALU.subtract))
                dve.sem_inc(lsh_ready, 1)
                dve.sem_inc(free(s), 1)
                link(dve.tensor_scalar(leq[:], lsh[:], 0.0, None, ALU.is_equal))
                link(dve.tensor_tensor(lrk[:], leq[:], rank[:].unsqueeze(1).broadcast_to([P, 2, NE]), ALU.mult))
                link(dve.tensor_reduce(lbest[:], lrk[:], AX.X, ALU.max))
                if b:
                    dve.wait_ge(full(("fw1s", b - 1), 0), TAKE[("fw1s", b - 1, 0)][1] + 1)
                for i in range(2):
                    ins = dve.tensor_tensor(oh[:, i], lrk[:, i].unsqueeze(1).broadcast_to([P, 3, NE]),
                                            lbest[:, i:i + 1].unsqueeze(2).broadcast_to([P, 3, NE]), ALU.is_equal)
                ins.then_inc(oh_ready, 1)
                dve.wait_ge(lex_ready, b + 1)
                link(dve.tensor_reduce(lsum[:], lex[:], AX.X, ALU.add))
                link(dve.reciprocal(tp[:], lsum[:]))

            def fohT(b):
                s = ("fohT", b)
                wait_full(dve, s)
                link(dve.tensor_copy(ohT[:], bank(s)[0:24, :].bitcast(BF16)[:, 0:QB]))
                dve.sem_inc(free(s), 1)
                dve.sem_inc(ohT_ready, 1)

            def fmask(b, i):
                s = ("fmask", b, i)
                wait_full(dve, s)
                m = bank(s)[:].bitcast(BF16).rearrange("p (e q) -> p e q", e=NE)
                h = hp[:, :, P * i:P * i + P]
                for e in range(NE):
                    ins = dve.tensor_tensor(hm[:, e, :, P * i:P * i + P], h, m[:, e, :].unsqueeze(1).broadcast_to([P, 3, P]),
                                            ALU.mult)
                link(ins)
                dve.sem_inc(free(s), 1)
                dve.sem_inc(hm_ready, 1)

            def fw1s(b):
                s = ("fw1s", b)
                wait_full(dve, s, 1)
                for f in range(FT):
                    ins = dve.tensor_scalar(z[:, FT + f, :], bank(s, 1)[:, QB * f:QB * f + QB],
                                            s1c[:, NE * FT + f:NE * FT + f + 1], None, ALU.mult)
                link(ins)
                dve.sem_inc(free(s, 1), 1)

            def fw1(b, f):
                s = ("fw1", b, f)
                wait_full(dve, s)
                i, n = TAKE[("fw1s", b, 0)]
                dve.wait_ge(bank_free[i], n + 1)
                link(dve.tensor_tensor(z[:, f, :], bank(s)[:, 0:QB], s1s[:, f, :], ALU.mult))
                dve.sem_inc(free(s), 1)
                if f == 1:
                    dve.sem_inc(z_ready, 1)

            def fact(b):
                dve.wait_ge(den_ready, b + 1)
                link(dve.reciprocal(zr[:], ez[:]))
                link(dve.tensor_tensor(h1[:], z[:], zr[:], ALU.mult))
                link(dve.tensor_copy(h1p[:, 0], h1[:]))
                link(dve.tensor_tensor(ez[:], h1[:], h1p[:, 0], ALU.subtract))
                link(dve.tensor_copy(h1p[:, 1], ez[:]))
                dve.tensor_tensor(h1p[:, 2], ez[:], h1p[:, 1], ALU.subtract).then_inc(h1p_ready, 1)

            def fw2(b, i):
                s = ("fw2", b, i)
                for j in range(2):
                    wait_full(dve, s, j)
                    link(dve.tensor_tensor(sel[:, 4 * j:4 * j + 4, :], bank(s, j)[:].rearrange("p (e d) -> p e d", e=4),
                                           oh[:, i, 0, 4 * j:4 * j + 4].unsqueeze(2).broadcast_to([P, 4, P]), ALU.mult))
                    dve.sem_inc(free(s, j), 1)
                link(dve.tensor_reduce(acc[:], sel[:].rearrange("p e d -> p d e"), AX.X, ALU.add))

            def fw2s(b, i):
                s = ("fw2s", b, i)
                wait_full(dve, s)
                link(dve.tensor_tensor(accs[:], acc[:], bank(s)[:, P:2 * P], ALU.mult))
                link(dve.tensor_tensor(shd[:], bank(s)[:, 0:P], s2row[:], ALU.mult))
                dve.sem_inc(free(s), 1)
                link(dve.scalar_tensor_tensor(out=fo[:], in0=accs[:], scalar=tp[:, i:i + 1], in1=shd[:], op0=ALU.mult,
                                              op1=ALU.add))
                link(dve.bn_stats(fst[:, 2, i, :], fo[:]))
                dve.bn_aggr(fmv[:, 2, i, :], fst[:, 2, i, :]).then_inc(fmv_ready, 1)
                dve.wait_ge(frs_ready, 4 * b + 3 + i)
                link(dve.tensor_scalar(fl[:], fo[:], fmv[:, 2, i, 0:1], frs[:, 6 + i, 1:2], ALU.subtract, ALU.mult))
                if b:
                    dve.wait_ge(y_out, 16 * (2 * b))
                dve.tensor_tensor(yout[:, i, :], xa[:, i, :], fl[:], ALU.add).then_inc(y_ready, 1)

            run = {"weights": weights, "prep": prep, "ternary": ternary, "wturn": wturn, "scales": scales,
                   "norm": norm, "proj": proj, "split": split, "kT": k_copy,
                   "qT": q_copy, "oevac": o_copy, "oT": o_scale, "wo": residual, "fnorm": fnorm, "fhT": fhT,
                   "frouter": frouter, "fohT": fohT, "fmask": fmask, "fw1s": fw1s, "fw1": fw1, "fact": fact,
                   "fw2": fw2, "fw2s": fw2s}
            for kind, *at in PLAN:
                if kind in run:
                    run[kind](*at)


def tables():
    tokens = np.arange(TILES * P, dtype=np.float32)
    rope = np.zeros((P, 2, 2, TILES, HD), np.float32)
    for a, base in enumerate((1000000.0, 10000.0)):
        inv = np.float32(1.0) / np.float32(base) ** (np.arange(0, HD, 2, dtype=np.float32) / np.float32(HD))
        freq = (tokens[:, None] * inv[None, :].astype(np.float32)).astype(np.float64)
        c = np.repeat(np.cos(freq), 2, axis=1)
        s = np.stack([-np.sin(freq), np.sin(freq)], axis=-1).reshape(TILES * P, HD)
        for k, t in enumerate((c, s)):
            rope[:, a, k] = t.astype(np.float32).reshape(TILES, P, HD).transpose(1, 0, 2)
    key = np.arange(P)[:, None]
    before = np.arange(WIN)[None, :] + P - key < WIN
    i = np.arange(P + WIN)[None, :] - key
    band = np.concatenate([before, (i >= 0) & (i < WIN)], axis=1).astype(np.float32)
    rank = np.repeat(np.arange(NE, 0, -1, dtype=np.float32)[None, :], P, axis=0)
    return {"ident": np.eye(P, dtype=np.float32), "rope": rope, "band": band, "rank": rank}


_INS = ["L0_attn_hidden", "L0_attn_norm1_w", "L0_attn_norm2_w", "L0_attn_g_wq", "L0_attn_g_kv_down",
        "L0_attn_g_k_up", "L0_attn_g_v_up", "L0_attn_g_wo", "L0_attn_l_wq", "L0_attn_l_wk", "L0_attn_l_wv",
        "L0_attn_l_wo", "L0_ffn_shared_w1", "L0_ffn_shared_w2", "L0_ffn_expert_w1", "L0_ffn_expert_w2",
        "L0_ffn_router_w", "L0_ffn_ln_gamma", "L0_ffn_ln_beta"]


def kernel(**inputs):
    import concourse.bacc as _bacc
    from concourse.bass_utils import run_bass_kernel_spmd as _run

    nc = _bacc.Bacc("TRN2", target_bir_lowering=False, num_devices=1)
    arrays, args = {}, []
    given = {name: np.ascontiguousarray(inputs[name]) for name in _INS}
    for name, a in {**given, **tables()}.items():
        arrays[f"in_{name}_dram"] = a
        args.append(nc.dram_tensor(f"in_{name}_dram", a.shape, mybir.dt.from_np(a.dtype), kind="ExternalInput").ap())
    args.append(nc.dram_tensor("out_0_dram", (1, TILES * P, P), F32, kind="ExternalOutput").ap())
    build(nc, *args)
    r = _run(nc, [arrays], core_ids=[0])
    return r.results[0]["out_0_dram"]
```

```python
from contextlib import ExitStack

import numpy as np

import concourse.bass as bass
from concourse import mybir

F32 = mybir.dt.float32
BF16 = mybir.dt.bfloat16
I32 = mybir.dt.int32
ALU = mybir.AluOpType
ACT = mybir.ActivationFunctionType
AX = mybir.AxisListType

P = 128
TILES = 16
NB = TILES // 2
QB = 2 * P
H, KVH, HD = 16, 4, 8
GRP = H // KVH
WIN = 32
NE, FT = 8, 2
QKW = (H + KVH) * HD
PW = QKW + KVH * HD
TERMS = 8
EPS_LN, EPS_RMS = 1e-5, 1e-6
MAGIC = float(0x5F3759DF)
G, L = 0, 1
NMISC = 3
NP = 5
PER = 3
LAG = 2

SLOT_OF = [0, 2, 1, 3]


def units_of(a, b):
    if a == G:
        return [(g, kb) for g in range(KVH) for kb in range(2 * b + 2)]
    return [(g, u) for g in range(KVH) for u in range(2)]


def pieces(a, b, kb):
    if a == G:
        lo = P if kb == 2 * b + 1 else 0
        return [(kb, lo, QB - lo, lo)]
    if kb == 1:
        return [(2 * b + 1, P, P, 0)]
    return ([(2 * b - 1, 0, WIN, 0)] if b else []) + [(2 * b, 0, P + WIN, WIN)]


TURNS = [[(1, k, 0) for k in range(8)], [(1, k, 0) for k in range(8, 16)],
         [(1, 16, 0), (1, 17, 0), (2, NE, 0), (2, NE, 1)],
         [(2, k, f) for k in range(4) for f in range(FT)], [(2, k, f) for k in range(4, 8) for f in range(FT)]]

GLUED = -1


def front_steps(a, b):
    return [(0, ("stat", a, b)), (3, ("norm", a, b)), (1, ("xT", a, b)), (1, ("proj", a, b)), (4, ("newton", a, b, 1)),
            (1, ("newton", a, b, 2)), (1, ("split", a, b)), (2, ("expand", a, b, 0)), (2, ("expand", a, b, 1)),
            (2, ("kT", a, b)), (1, ("qT", a, b, 0)), (1, ("qT", a, b, 1))]


def out_steps(a, b):
    return [(1, ("oT", a, b, 0)), (1, ("oT", a, b, 1)), (1, ("onT", a, b)), (1, ("wo", a, b))]


def local_steps(b):
    out = []
    for g in range(KVH):
        out += [(1, ("qk", L, b, g, 0)), (1, ("qk", L, b, g, 1))]
        out += [(2, ("pv", L, b, g, 0)), (GLUED, ("pv", L, b, g, 1)), (GLUED, ("oevac", L, b, g))]
    return out


def ffn_steps(b):
    return [(1, ("fstat", b)), (2, ("fxa", b)), (4, ("fh", b)), (1, ("fhT", b)), (1, ("frouter", b)), (0, ("fparts", b)),
            (2, ("fohT", b)), (1, ("fmask", b, 0)), (1, ("fmask", b, 1)), (1, ("fw1s", b)), (1, ("fw1", b, 0)),
            (2, ("fw1", b, 1)), (2, ("fact", b)), (2, ("fh1", b)), (4, ("fw2", b, 0)), (2, ("fw2s", b, 0)), (1, ("fw2", b, 1)),
            (1, ("fout", b, 0)), (1, ("fw2s", b, 1)), (3, ("fout", b, 1))]


def weight_steps():
    out = [(1, ("prep",))]
    for k in range(len(TURNS)):
        out += [(2, ("ternary", k)), (1, ("wturn", k))]
    return out + [(1, ("scales",))]


class Chain:

    def __init__(self, steps=()):
        self.steps, self.last = list(steps), -99

    def due(self, now):
        return bool(self.steps) and now >= self.last + self.steps[0][0]

    def pop(self, now):
        self.last = now
        return self.steps.pop(0)[1]


def make_plan():
    plan = [("weights",), *(s for _, s in front_steps(G, 0))]
    close, front, attend, feed = Chain(), Chain(), Chain(), Chain(weight_steps())
    now = 0

    units_out, sums_out = [], set()

    def room():
        return len(units_out) < NP or units_out[-NP] in sums_out

    def put(s):
        if s[0] == "qk":
            assert room()
            units_out.append(s[1:])
        if s[0] == "pv":
            sums_out.add(s[1:])
        plan.append(s)

    def fill(budget):
        for chain in (close, front, attend, feed):
            if budget and chain.due(now) and (chain.steps[0][1][0] != "qk" or room()):
                s = chain.pop(now)
                put(s)
                while chain.steps and chain.steps[0][0] == GLUED:
                    put(chain.pop(now))
                budget -= 1
                if s[:2] == ("wo", G):
                    attend.steps += front_steps(L, s[2]) + local_steps(s[2]) + out_steps(L, s[2])
                if s[:2] == ("wo", L):
                    feed.steps += ffn_steps(s[2])
        return budget

    def drain(chain, until):
        nonlocal now
        while chain.steps and not until():
            fill(3)
            now += 1

    for b in range(NB):
        if b + 1 < NB:
            front.steps += front_steps(G, b + 1)
        late = []

        def sum_late():
            w = late.pop(0)
            put(("pv", *w))
            if w[3] == 2 * b + 1:
                drain(close, lambda: not b or ("oT", G, b - 1, 1) in plan)
                put(("oevac", *w[:3]))

        for u in [(G, b, g, kb) for g, kb in units_of(G, b)]:
            while not room():
                if units_out[-NP] in late:
                    sum_late()
                else:
                    fill(PER)
                    now += 1
            put(("qk", *u))
            late.append(u)
            if len(late) > LAG:
                sum_late()
            fill(PER)
            now += 1
        while late:
            sum_late()
        drain(front, lambda: not front.steps)
        close.steps += out_steps(G, b)
    while close.steps or attend.steps or feed.steps:
        fill(3)
        now += 1
    return plan


PLAN = make_plan()
TAKES = {"weights": 3, "wturn": 1, "scales": 2, "xT": 1, "proj": 1, "qT": 1, "kT": 1, "oT": 1, "onT": 1, "wo": 1, "fhT": 1, "frouter": 1, "fohT": 1,
         "fmask": 1, "fw1s": 2, "fw1": 1, "fw2": 2, "fw2s": 1}


def number():
    unit, pv, osum, take, masks = {}, {}, {}, {}, {}
    n = 0
    for s in PLAN:
        if s[0] == "qk":
            unit[s[1:]] = len(unit)
            if s[1] == L or s[4] >= 2 * s[2]:
                masks[s[1:]] = len(masks)
        if s[0] == "pv":
            pv[s[1:]] = len(pv)
            if s[1] == G and s[4] == 0:
                osum[s[2:4]] = len(osum)
        k = TAKES.get(s[0], 0)
        if s[0] == "pv" and s[1] == L and s[4] == 0:
            k = 1
        for j in range(k):
            take[(*s, j)] = (n % NMISC, n // NMISC)
            n += 1
    return unit, pv, osum, take, masks


UNIT, PV, OSUM, TAKE, MASK = number()
UNIT_LIST = list(UNIT)


def build(nc, x, norm1_w, norm2_w, g_wq, g_kv_down, g_k_up, g_v_up, g_wo, l_wq, l_wk, l_wv, l_wo,
          sw1, sw2, ew1, ew2, router_w, ln_gamma, ln_beta, ident_d, rope_d, band_d, rank_d, out):
    with ExitStack() as ctx:
        def sb(name, shape, dt=F32):
            return ctx.enter_context(nc.sbuf_tensor(name, shape, dt))

        def sem(name):
            return ctx.enter_context(nc.semaphore(name))

        def pair(name):
            return [sem(f"{name}_g"), sem(f"{name}_l")]

        def two(name, shape, dt=F32):
            return [sb(f"{name}_g", shape, dt), sb(f"{name}_l", shape, dt)]

        scores = [ctx.enter_context(nc.psum_tensor(f"scores{i}", [P, 1024], F32)) for i in range(2)]
        osum_g = ctx.enter_context(nc.psum_tensor("osum_g", [P, 512], F32))
        misc = [ctx.enter_context(nc.psum_tensor(f"misc{i}", [P, 512], F32)) for i in range(NMISC)]

        ident = sb("ident", [P, P])
        identb = sb("identb", [P, P], BF16)
        rope = sb("rope", [P, 2, 2, TILES, HD])
        band = sb("band", [P, P + 2 * WIN])
        rank = sb("rank", [P, NE])
        mhalf = sb("mhalf", [P, 4])
        ones = sb("ones", [P, P])
        nw = [sb("nw_g", [P, 1]), sb("nw_l", [P, 1])]
        wraw = two("wraw", [P, PW])
        wqkv = two("wqkv", [P, PW])
        wo_sb = two("wo", [P, P])
        kvd = sb("kvd", [P, 32])
        kvdT = sb("kvdT", [32, P])
        kvup = sb("kvup", [32, 64])
        gamma = sb("gamma", [P, 1])
        beta = sb("beta", [P, 1])
        rw = sb("rw", [NE, P])
        rwT = sb("rwT", [P, NE])
        early = sb("early", [P, 2 * (NE + 1) * FT * P])
        w1n = early[:, 0:(NE + 1) * FT * P].rearrange("p (k d) -> p k d", d=P)
        w2n = early[:, (NE + 1) * FT * P:].rearrange("p (k d) -> p k d", d=FT * P)
        s1c = sb("s1c", [P, NE * FT + FT])
        s2c = sb("s2c", [P, NE + 1])
        half1 = sb("half1", [P, 2, NE * FT + FT])
        half2 = sb("half2", [P, 2, NE + 1])
        early2 = sb("early2", [P, 2 * (NE + 1) * FT * P])
        NW = (NE + 1) * FT * P
        tb = early2[:].bitcast(BF16)
        t1, t1b = [tb[:, k * NW:k * NW + NW].rearrange("p (k d) -> p k d", d=P) for k in (0, 1)]
        t2, t2b = [tb[:, k * NW:k * NW + NW].rearrange("p (k d) -> p k d", d=FT * P) for k in (2, 3)]
        t1T = sb("t1T", [P, NE * FT + FT, P], BF16)
        t2T = sb("t2T", [P, FT, NE + 1, P], BF16)
        s1p = sb("s1p", [P, FT, 3, NE], BF16)
        s1q = sb("s1q", [P, FT, NE])
        s2p = sb("s2p", [P, 3, NE], BF16)
        s2q = sb("s2q", [P, NE])
        s1pT = sb("s1pT", [3 * NE, FT, P], BF16)
        s2pT = sb("s2pT", [3 * NE, P], BF16)
        s2diag = sb("s2diag", [P, P])
        s2row = sb("s2row", [P, P])

        X = sb("X", [P, TILES, P])
        Hn = sb("Hn", [P, 4, 2, P])
        X1 = sb("X1", [P, NB, 2, P])
        X2 = sb("X2", [P, 2, P])
        stats = two("stats", [P, 2, 6])
        mv = two("mv", [P, 2, 2])
        rs = two("rs", [P, 8, 2])
        xn = two("xn", [P, 2, P])
        xT = two("xT", [P, QB])
        cosp = two("cosp", [P, 2, QKW])
        sinp = two("sinp", [P, 2, QKW])
        qk = two("qk", [P, 2, QKW])
        ss = two("ss", [P, 2 * (H + KVH)])
        nv = two("nv", [P, 2 * (H + KVH)])
        ny = two("ny", [P, 2 * (H + KVH)])
        nt = two("nt", [P, 2 * (H + KVH)])
        qn = two("qn", [P, 2, QKW])
        res = two("res", [P, 2, QKW])
        part = two("part", [P, 3, 2, QKW], BF16)
        qe = two("qe", [P, 2, H, TERMS, HD], BF16)
        ke = two("ke", [P, 2, KVH, TERMS, HD], BF16)
        qT = two("qT", [P, 2, H // 2, QB], BF16)
        kept = [TILES, 4]
        kT = [sb(f"kT{a}", [P, KVH, kept[a] * P], BF16) for a in (G, L)]
        V = [sb(f"V{a}", [P, kept[a], KVH, 32]) for a in (G, L)]
        prob = sb("prob", [P, NP, 4, QB])
        oTs = two("oTs", [P, KVH, QB])
        rec = two("rec", [P, H])
        on = two("on", [P, 2, P])
        onT = two("onT", [P, QB])

        fst = sb("fst", [P, 3, 2, 6])
        fmv = sb("fmv", [P, 3, 2, 2])
        frs = sb("frs", [P, 10, 2])
        ftmp = sb("ftmp", [P, 2, P])
        xa = sb("xa", [P, 2, P])
        fh = sb("fh", [P, 2, P])
        hT = sb("hT", [P, QB])
        hres = sb("hres", [P, QB])
        hp = sb("hp", [P, 3, QB], BF16)
        lmax = sb("lmax", [P, 2])
        lsh = sb("lsh", [P, 2, NE])
        lex = sb("lex", [P, 2, NE])
        lsum = sb("lsum", [P, 2])
        tp = sb("tp", [P, 2])
        leq = sb("leq", [P, 2, NE])
        lrk = sb("lrk", [P, 2, NE])
        lbest = sb("lbest", [P, 2])
        oh = sb("oh", [P, 2, 3, NE], BF16)
        ohT = sb("ohT", [3 * NE, QB], BF16)
        hm = early[:].bitcast(BF16)[:, 0:NE * 3 * QB].rearrange("p (e a q) -> p e a q", e=NE, a=3)
        s1s = sb("s1s", [P, FT, QB])
        z, ez, zr, h1 = [early2[:, 2 * FT * QB * k:2 * FT * QB * (k + 1)].rearrange("p (f q) -> p f q", q=QB)
                         for k in range(4)]
        h1p = sb("h1p", [P, 3, 2 * FT, QB], BF16)
        sel = early[:, NE * 3 * QB // 2:NE * 3 * QB // 2 + NE * P].rearrange("p (e d) -> p e d", e=NE)
        acc = sb("acc", [P, P])
        accs = sb("accs", [P, P])
        shd = sb("shd", [P, P])
        fo = sb("fo", [P, 2, P])
        fl = sb("fl", [P, P])
        yout = sb("yout", [P, 2, P])

        x_in = [sem(f"x_in{b}") for b in range(NB)]
        small_in = sem("small_in")
        wa_in = sem("wa_in")
        wf_in = sem("wf_in")
        y_out = sem("y_out")
        dch = sem("dch")
        pch = sem("pch")
        ach = sem("ach")
        const_ready = sem("const_ready")
        bank_full = [sem(f"bank_full{i}") for i in range(NMISC)]
        bank_free = [sem(f"bank_free{i}") for i in range(NMISC)]
        wqkv_ready = sem("wqkv_ready")
        tern_ready = sem("tern_ready")
        scale_ready = sem("scale_ready")
        prep_read = sem("prep_read")
        mv_ready = pair("mv_ready")
        rs_ready = pair("rs_ready")
        xn_ready = pair("xn_ready")
        xT_ready = pair("xT_ready")
        v_ready = pair("v_ready")
        ss_ready = pair("ss_ready")
        ny_ready = pair("ny_ready")
        part_ready = pair("part_ready")
        term_ready = pair("term_ready")
        qT_ready = pair("qT_ready")
        kT_ready = pair("kT_ready")
        qk_done = sem("qk_done")
        exp_done = sem("exp_done")
        mask_done = sem("mask_done")
        pv_done = sem("pv_done")
        o_free = sem("o_free")
        oT_ready = pair("oT_ready")
        on_ready = pair("on_ready")
        onT_ready = pair("onT_ready")
        fmv_ready = sem("fmv_ready")
        frs_ready = sem("frs_ready")
        fh_ready = sem("fh_ready")
        hT_ready = sem("hT_ready")
        lsh_ready = sem("lsh_ready")
        lex_ready = sem("lex_ready")
        oh_ready = sem("oh_ready")
        ohT_ready = sem("ohT_ready")
        hm_ready = sem("hm_ready")
        hp_ready = sem("hp_ready")
        s1s_ready = sem("s1s_ready")
        z_ready = sem("z_ready")
        ez_ready = sem("ez_ready")
        h1p_ready = sem("h1p_ready")
        y_ready = sem("y_ready")

        def bank(step, j=0):
            return misc[TAKE[(*step, j)][0]]

        def take(pe, step, j=0):
            i, n = TAKE[(*step, j)]
            if n:
                pe.wait_ge(bank_free[i], n)

        def full(step, j=0):
            return bank_full[TAKE[(*step, j)][0]]

        def free(step, j=0):
            return bank_free[TAKE[(*step, j)][0]]

        def wait_full(eng, step, j=0):
            i, n = TAKE[(*step, j)]
            eng.wait_ge(bank_full[i], n + 1)

        x_v = x.rearrange("a (t p) d -> p (a t) d", p=P)
        out_v = out.rearrange("a (t p) d -> p (a t) d", p=P)
        col = lambda w: w.rearrange("(p a) -> p a", a=1)

        block = ctx.enter_context(nc.Block())

        @block.sync
        def _(sp):
            sp.dma_start(X[:, 0:2, :], x_v[:, 0:2, :]).then_inc(x_in[0], 16)
            sp.dma_start(ident[:], ident_d).then_inc(small_in, 16)
            sp.dma_start(rope[:], rope_d).then_inc(small_in, 16)
            sp.dma_start(wraw[G][:, 0:P], g_wq).then_inc(wa_in, 16)
            sp.dma_start(kvd[:], g_kv_down).then_inc(wa_in, 16)
            sp.dma_start(kvup[:, 0:32], g_k_up).then_inc(wa_in, 16)
            sp.dma_start(kvup[:, 32:64], g_v_up).then_inc(wa_in, 16)
            sp.dma_start(nw[G][:], col(norm1_w)).then_inc(wa_in, 16)
            sp.dma_start(rw[:], router_w).then_inc(wa_in, 16)
            for b in range(1, NB):
                sp.dma_start(X[:, 2 * b:2 * b + 2, :], x_v[:, 2 * b:2 * b + 2, :]).then_inc(x_in[b], 16)
            for b in range(NB):
                for i in range(2):
                    sp.wait_ge(y_ready, 2 * b + i + 1)
                    sp.dma_start(out_v[:, 2 * b + i, :], yout[:, i, :]).then_inc(y_out, 16)
            sp.wait_ge(y_out, 16 * TILES)

        @block.gpsimd
        def _(pool):
            chain = [0]

            def link(ins):
                chain[0] += 1
                ins.then_inc(pch, 1)
                pool.wait_ge(pch, chain[0])

            def weights():
                pool.memset(mhalf[:], -0.5).then_inc(const_ready, 1)
                pool.memset(ones[:], 1.0).then_inc(const_ready, 1)
                pool.memset(V[G][:], 1.0).then_inc(const_ready, 1)
                pool.memset(V[L][:], 1.0).then_inc(const_ready, 1)
                pool.wait_ge(const_ready, 4)
                pool.dma_start(wraw[L][:, 0:P], l_wq).then_inc(wf_in, 16)
                pool.dma_start(wraw[L][:, P:QKW], l_wk).then_inc(wf_in, 16)
                pool.dma_start(wraw[L][:, QKW:PW], l_wv).then_inc(wf_in, 16)
                pool.dma_start(nw[L][:], col(norm2_w)).then_inc(wf_in, 16)
                pool.dma_start(wo_sb[G][:], g_wo).then_inc(wf_in, 16)
                pool.dma_start(wo_sb[L][:], l_wo).then_inc(wf_in, 16)
                pool.dma_start(band[:], band_d).then_inc(wf_in, 16)
                pool.dma_start(rank[:], rank_d).then_inc(wf_in, 16)
                pool.dma_start(gamma[:], col(ln_gamma)).then_inc(wf_in, 16)
                pool.dma_start(beta[:], col(ln_beta)).then_inc(wf_in, 16)
                pool.dma_start(w1n[:, 0:NE * FT, :], ew1.rearrange("e (t p) d -> p (e t) d", p=P)).then_inc(wf_in, 16)
                pool.dma_start(w1n[:, NE * FT:, :], sw1.rearrange("(t p) d -> p t d", p=P)).then_inc(wf_in, 16)
                pool.dma_start(w2n[:, 0:NE, :], ew2.rearrange("e p f -> p e f")).then_inc(wf_in, 16)
                pool.dma_start(w2n[:, NE, :], sw2).then_inc(wf_in, 16)

            def rsqrt(out, value, eps):
                link(pool.tensor_scalar(out, value, 1.0, eps, ALU.mult, ALU.add))
                link(pool.tensor_tensor(out, out, mhalf[:, 0:2], ALU.pow))

            def stat(a, b):
                r, m, v = rs[a], mv[a][:, :, 0], mv[a][:, :, 1]
                pool.wait_ge(mv_ready[a], b + 1)
                if a == G:
                    if b:
                        pool.wait_ge(xn_ready[a], b)
                    rsqrt(r[:, 0, :], v, EPS_LN)
                    link(pool.tensor_tensor(r[:, 1, :], r[:, 0, :], r[:, 0, :], ALU.mult))
                    link(pool.tensor_tensor(r[:, 1, :], r[:, 1, :], v, ALU.mult))
                    rsqrt(r[:, 2, :], r[:, 1, :], EPS_RMS)
                    pool.tensor_tensor(r[:, 3, :], r[:, 0, :], r[:, 2, :], ALU.mult).then_inc(rs_ready[a], 1)
                else:
                    if b:
                        pool.wait_ge(xn_ready[a], b)
                    link(pool.tensor_tensor(r[:, 1, :], m, m, ALU.mult))
                    link(pool.tensor_tensor(r[:, 1, :], r[:, 1, :], v, ALU.add))
                    link(pool.tensor_scalar(r[:, 1, :], r[:, 1, :], 1.0, EPS_RMS, ALU.mult, ALU.add))
                    pool.tensor_tensor(r[:, 3, :], r[:, 1, :], mhalf[:, 0:2], ALU.pow).then_inc(rs_ready[a], 1)

            def newton(a, b, k):
                v, y, t = nv[a][:], ny[a][:], nt[a][:]
                link(pool.tensor_tensor(t, y, y, ALU.mult))
                link(pool.tensor_tensor(t, t, v, ALU.mult))
                link(pool.tensor_scalar(t, t, -0.5, 1.5, ALU.mult, ALU.add))
                ins = pool.tensor_tensor(y, y, t, ALU.mult)
                if k < 2:
                    link(ins)
                else:
                    ins.then_inc(ny_ready[a], 1)

            def proj(a, b):
                v, y = nv[a][:], ny[a][:]
                pool.wait_ge(ss_ready[a], b + 1)
                if b:
                    pool.wait_ge(part_ready[a], b)
                link(pool.tensor_scalar(v, ss[a][:], 1.0 / HD, EPS_RMS, ALU.mult, ALU.add))
                link(pool.tensor_scalar(y.bitcast(I32), v.bitcast(I32), -0.5, MAGIC, ALU.mult, ALU.add))
                newton(a, b, 0)

            def expand(a, b, i):
                pool.wait_ge(part_ready[a], b + 1)
                if b:
                    pool.wait_ge(kT_ready[a], b)
                    pool.wait_ge(qT_ready[a], 2 * b)
                for p, (lo, n) in enumerate([(0, 3), (3, 3), (6, 2)]):
                    src = part[a][:, p, i, 0:P].rearrange("p (h d) -> p h d", d=HD)
                    pool.tensor_scalar(qe[a][:, i, :, lo:lo + n, :], src.unsqueeze(2).broadcast_to([P, H, n, HD]),
                                       1.0, 0.0, ALU.mult, ALU.add)
                for p in range(3):
                    src = part[a][:, p, i, P:QKW].rearrange("p (h d) -> p h d", d=HD)
                    n = 3 if p < 2 else 2
                    ins = pool.tensor_scalar(ke[a][:, i, :, p::3, :], src.unsqueeze(2).broadcast_to([P, KVH, n, HD]),
                                             1.0, 0.0, ALU.mult, ALU.add)
                ins.then_inc(term_ready[a], 1)

            def qkmask(*u):
                if u not in MASK:
                    return
                a, b, g, kb = u
                p = prob[:, UNIT[u] % NP, :, :]
                pool.wait_ge(exp_done, UNIT[u] + 1)
                if a == G:
                    d = p[:, :, P * (kb - 2 * b):P * (kb - 2 * b) + P]
                    pool.affine_select(out=d, in_=d, compare_op=ALU.is_ge, fill=0.0, base=0,
                                       pattern=[[0, 4], [1, P]], channel_multiplier=-1).then_inc(mask_done, 1)
                else:
                    pool.wait_ge(wf_in, 16 * 14)
                    lo, n = (0, P) if kb else (0 if b else WIN, P + 2 * WIN - (0 if b else WIN))
                    m = band[:, (WIN if kb else lo):(WIN if kb else lo) + n]
                    d = p[:, :, lo:lo + n]
                    pool.tensor_tensor(d, d, m.unsqueeze(1).broadcast_to([P, 4, n]), ALU.mult).then_inc(mask_done, 1)

            def fstat(b):
                pool.wait_ge(fmv_ready, 4 * b + 1)
                rsqrt(frs[:, 0, :], fmv[:, 0, :, 1], EPS_LN)
                pool.tensor_tensor(frs[:, 1, :], frs[:, 0, :], fmv[:, 0, :, 0], ALU.mult).then_inc(frs_ready, 1)

            def fxa(b):
                r = frs
                pool.wait_ge(fmv_ready, 4 * b + 2)
                rsqrt(r[:, 2, :], fmv[:, 1, :, 1], EPS_LN)
                link(pool.tensor_tensor(r[:, 3, :], r[:, 2, :], r[:, 2, :], ALU.mult))
                link(pool.tensor_tensor(r[:, 3, :], r[:, 3, :], fmv[:, 1, :, 1], ALU.mult))
                rsqrt(r[:, 4, :], r[:, 3, :], EPS_LN)
                pool.tensor_tensor(r[:, 5, :], r[:, 2, :], r[:, 4, :], ALU.mult).then_inc(frs_ready, 1)

            def fw2s(b, i):
                pool.wait_ge(fmv_ready, 4 * b + 3 + i)
                link(pool.tensor_scalar(frs[:, 6 + i, 0:1], fmv[:, 2, i, 1:2], 1.0, EPS_LN, ALU.mult, ALU.add))
                pool.tensor_tensor(frs[:, 6 + i, 1:2], frs[:, 6 + i, 0:1], mhalf[:, 0:1], ALU.pow).then_inc(frs_ready, 1)

            run = {"weights": weights, "stat": stat, "proj": proj, "newton": newton, "expand": expand, "qk": qkmask,
                   "fstat": fstat, "fxa": fxa, "fw2s": fw2s}
            for kind, *at in PLAN:
                if kind in run:
                    run[kind](*at)

        @block.scalar
        def _(act):
            def xT_copy(a, b):
                s = ("xT", a, b)
                wait_full(act, s)
                if b:
                    act.wait_ge(v_ready[a], b)
                act.copy(xT[a][:], bank(s)[:, 0:QB]).then_inc(free(s), 1)

            def exp(*u):
                n = UNIT[u]
                a, b, g, kb = u
                act.wait_ge(qk_done, n + 1)
                if n >= NP:
                    act.wait_ge(pv_done, PV[UNIT_LIST[n - NP]] + 1)
                ps = pieces(a, b, kb)
                lo, hi = ps[0][3], ps[-1][3] + ps[-1][2]
                src = scores[n % 2][:].rearrange("p (m q) -> p m q", m=4)[:, :, lo:hi]
                act.activation(prob[:, n % NP, :, lo:hi], src, ACT.Exp, scale=float(HD) ** -0.5).then_inc(exp_done, 1)

            def onT_copy(a, b):
                s = ("onT", a, b)
                wait_full(act, s)
                act.copy(onT[a][:], bank(s)[:, 0:QB]).then_inc(free(s), 1)

            def fhT(b):
                s = ("fhT", b)
                wait_full(act, s)
                act.activation(hT[:], bank(s)[:, 0:QB], ACT.Identity, scale=gamma[:, 0:1],
                               bias=beta[:, 0:1]).then_inc(free(s), 1)

            def frouter(b):
                act.wait_ge(lsh_ready, b + 1)
                act.activation(lex[:], lsh[:], ACT.Exp).then_inc(lex_ready, 1)

            def fw1s(b):
                s = ("fw1s", b)
                wait_full(act, s, 0)
                act.copy(s1s[:].rearrange("p t q -> p (t q)"), bank(s, 0)[:]).then_inc(free(s, 0), 1)

            def fact(b):
                act.wait_ge(z_ready, b + 1)
                act.activation(ez, z, ACT.Tanh, scale=0.5).then_inc(ez_ready, 1)

            run = {"xT": xT_copy, "qk": exp, "onT": onT_copy, "fhT": fhT, "frouter": frouter,
                   "fw1s": fw1s, "fact": fact}
            for kind, *at in PLAN:
                if kind in run:
                    run[kind](*at)

        @block.tensor
        def _(pe):
            def weights():
                s = ("weights",)
                pe.wait_ge(small_in, 32)
                pe.wait_ge(wa_in, 16 * 6)
                take(pe, s, 0)
                pe.transpose(bank(s, 0)[0:32, 0:P], kvd[:], ident[:]).then_inc(full(s, 0), 1)
                pe.wait_ge(free(s, 0), 1)
                pe.matmul(bank(s, 1)[:, 0:64], kvdT[:], kvup[:], start=True, stop=True).then_inc(full(s, 1), 1)
                pe.transpose(bank(s, 2)[:, 0:NE], rw[:], ident[0:NE, 0:NE]).then_inc(full(s, 2), 1)

            def wturn(k):
                s = ("wturn", k)
                pe.wait_ge(tern_ready, k + 1)
                take(pe, s)
                for m, (w, r, c) in enumerate(TURNS[k]):
                    src = t1[:, r, :] if w == 1 else t2[:, r, P * c:P * c + P]
                    ins = pe.transpose(bank(s)[:].bitcast(BF16)[:, P * m:P * m + P], src, identb[:])
                ins.then_inc(full(s), 1)

            def scales():
                s = ("scales",)
                pe.wait_ge(scale_ready, 1)
                take(pe, s, 0)
                o = bank(s, 0)[0:3 * NE, :].bitcast(BF16)
                for m in range(FT):
                    pe.transpose(o[:, P * m:P * m + P], s1p[:, m, :, :].rearrange("p a e -> p (a e)"), identb[:])
                pe.transpose(o[:, P * FT:P * FT + P], s2p[:].rearrange("p a e -> p (a e)"),
                             identb[:]).then_inc(full(s, 0), 1)
                take(pe, s, 1)
                pe.wait_ge(const_ready, 4)
                pe.matmul(bank(s, 1)[:, 0:P], ones[:], s2diag[:], start=True, stop=True).then_inc(full(s, 1), 1)

            def xT_turn(a, b):
                s = ("xT", a, b)
                pe.wait_ge(xn_ready[a], b + 1)
                take(pe, s)
                for i in range(2):
                    ins = pe.transpose(bank(s)[:, P * i:P * i + P], xn[a][:, i, :], ident[:])
                ins.then_inc(full(s), 1)

            def proj(a, b):
                s = ("proj", a, b)
                if b == 0:
                    pe.wait_ge(wqkv_ready, 1 + a)
                i, n = TAKE[("xT", a, b, 0)]
                pe.wait_ge(bank_free[i], n + 1)
                take(pe, s)
                for i in range(2):
                    ins = pe.matmul(bank(s)[:, PW * i:PW * i + PW], xT[a][:, P * i:P * i + P], wqkv[a][:],
                                    start=True, stop=True)
                ins.then_inc(full(s), 1)

            def k_turn(a, b):
                s = ("kT", a, b)
                pe.wait_ge(term_ready[a], 2 * b + 2)
                take(pe, s)
                o = bank(s)[:].bitcast(BF16)
                for g in range(KVH):
                    for i in range(2):
                        src = ke[a][:, i, g, :, :].rearrange("p t d -> p (t d)")
                        for half in range(2):
                            ins = pe.transpose(o[64 * half:64 * half + 64, P * (2 * g + i):P * (2 * g + i) + P], src, identb[:])
                ins.then_inc(full(s), 1)

            def q_turn(a, b, i):
                s = ("qT", a, b, i)
                pe.wait_ge(term_ready[a], 2 * b + 2)
                take(pe, s)
                o = bank(s)[:].bitcast(BF16)
                for m in range(H // 2):
                    ins = pe.transpose(o[:, P * m:P * m + P],
                                       qe[a][:, i, 2 * m:2 * m + 2, :, :].rearrange("p h t d -> p (h t d)"), identb[:])
                ins.then_inc(full(s), 1)

            def qk_product(*u):
                a, b, g, kb = u
                n = UNIT[u]
                pe.wait_ge(qT_ready[a], 2 * b + 2)
                pe.wait_ge(kT_ready[a], b + 1)
                if n >= 2:
                    pe.wait_ge(exp_done, n - 1)
                for m in range(4):
                    r = 64 * (m % 2)
                    for t, q, w, c in pieces(a, b, kb):
                        c += 256 * SLOT_OF[m]
                        ins = pe.matmul(scores[n % 2][:, c:c + w], kT[a][r:r + 64, g, P * (t % kept[a]):P * (t % kept[a]) + P],
                                        qT[a][r:r + 64, b % 2, 2 * g + m // 2, q:q + w], start=True, stop=True)
                ins.then_inc(qk_done, 1)

            def pv_product(*u):
                a, b, g, kb = u
                n = UNIT[u]
                if a == G:
                    o = osum_g
                    if kb == 0 and OSUM[(b, g)]:
                        pe.wait_ge(o_free, OSUM[(b, g)])
                else:
                    s = ("pv", L, b, g, 0)
                    if kb == 0:
                        take(pe, s)
                    o = bank(s)
                pe.wait_ge(v_ready[a], b + 1)
                if u in MASK:
                    pe.wait_ge(mask_done, MASK[u] + 1)
                else:
                    pe.wait_ge(exp_done, n + 1)
                ps = pieces(a, b, kb)
                for k, (t, q, w, c) in enumerate(ps):
                    last = kb == (2 * b + 1 if a == G else 1)
                    for m in range(4):
                        ins = pe.matmul(o[32 * m:32 * m + 32, q:q + w], V[a][:, t % kept[a], g, :],
                                        prob[:, n % NP, SLOT_OF[m], c:c + w], start=(kb == 0 and k == 0), stop=last,
                                        skip_group_check=True)
                        if a == L and kb == 1 and m == 2:
                            ins.then_inc(full(s), 1)
                ins.then_inc(pv_done, 1)

            def o_turn(a, b, i):
                s = ("oT", a, b, i)
                pe.wait_ge(oT_ready[a], KVH * (b + 1))
                take(pe, s)
                for g in range(KVH):
                    ins = pe.transpose(bank(s)[:, P * g:P * g + P], oTs[a][:, g, P * i:P * i + P], ident[:])
                ins.then_inc(full(s), 1)

            def on_turn(a, b):
                s = ("onT", a, b)
                pe.wait_ge(on_ready[a], 2 * b + 2)
                take(pe, s)
                for i in range(2):
                    ins = pe.transpose(bank(s)[:, P * i:P * i + P], on[a][:, i, :], ident[:])
                ins.then_inc(full(s), 1)

            def wo_product(a, b):
                s = ("wo", a, b)
                if a == G and b == 0:
                    pe.wait_ge(wf_in, 16 * 14)
                i, n = TAKE[("onT", a, b, 0)]
                pe.wait_ge(bank_free[i], n + 1)
                take(pe, s)
                for i in range(2):
                    ins = pe.matmul(bank(s)[:, P * i:P * i + P], onT[a][:, P * i:P * i + P], wo_sb[a][:],
                                    start=True, stop=True)
                ins.then_inc(full(s), 1)

            def fhT(b):
                s = ("fhT", b)
                pe.wait_ge(fh_ready, b + 1)
                take(pe, s)
                for i in range(2):
                    ins = pe.transpose(bank(s)[:, P * i:P * i + P], fh[:, i, :], ident[:])
                ins.then_inc(full(s), 1)

            def frouter(b):
                s = ("frouter", b)
                i, n = TAKE[("fhT", b, 0)]
                pe.wait_ge(bank_free[i], n + 1)
                take(pe, s)
                for i in range(2):
                    ins = pe.matmul(bank(s)[:, NE * i:NE * i + NE], hT[:, P * i:P * i + P], rwT[:], start=True, stop=True)
                ins.then_inc(full(s), 1)

            def fohT(b):
                s = ("fohT", b)
                pe.wait_ge(oh_ready, b + 1)
                take(pe, s)
                for i in range(2):
                    ins = pe.transpose(bank(s)[0:24, :].bitcast(BF16)[:, P * i:P * i + P],
                                       oh[:, i, :, :].rearrange("p a e -> p (a e)"), identb[:])
                ins.then_inc(full(s), 1)

            def fmask(b, i):
                s = ("fmask", b, i)
                pe.wait_ge(oh_ready, b + 1)
                take(pe, s)
                for e in range(NE):
                    ins = pe.transpose(bank(s)[:].bitcast(BF16)[:, P * e:P * e + P],
                                       oh[:, i, 0, e:e + 1].broadcast_to([P, P]), identb[:])
                ins.then_inc(full(s), 1)

            def fw1s(b):
                s = ("fw1s", b)
                pe.wait_ge(ohT_ready, b + 1)
                take(pe, s, 0)
                for f in range(FT):
                    ins = pe.matmul(bank(s, 0)[:, QB * f:QB * f + QB], s1pT[:, f, :], ohT[:], start=True, stop=True)
                ins.then_inc(full(s, 0), 1)
                pe.wait_ge(hp_ready, b + 1)
                take(pe, s, 1)
                for f in range(FT):
                    for p in range(3):
                        ins = pe.matmul(bank(s, 1)[:, QB * f:QB * f + QB], t1T[:, NE * FT + f, :], hp[:, p, :],
                                        start=(p == 0), stop=(p == 2))
                ins.then_inc(full(s, 1), 1)

            def fw1(b, f):
                s = ("fw1", b, f)
                pe.wait_ge(hm_ready, 2 * b + 2)
                take(pe, s)
                for e in range(NE):
                    for p in range(3):
                        ins = pe.matmul(bank(s)[:, 0:QB], t1T[:, FT * e + f, :], hm[:, e, p, :],
                                        start=(e == 0 and p == 0), stop=(e == NE - 1 and p == 2))
                ins.then_inc(full(s), 1)

            def fw2(b, i):
                s = ("fw2", b, i)
                pe.wait_ge(h1p_ready, b + 1)
                for j in range(2):
                    take(pe, s, j)
                    for p in range(3):
                        for f in range(FT):
                            ins = pe.matmul(bank(s, j)[:], h1p[:, p, f, P * i:P * i + P],
                                            t2T[:, f, 4 * j:4 * j + 4, :].rearrange("p e d -> p (e d)"),
                                            start=(p == 0 and f == 0), stop=(p == 2 and f == FT - 1))
                    ins.then_inc(full(s, j), 1)

            def fw2s(b, i):
                s = ("fw2s", b, i)
                take(pe, s)
                for p in range(3):
                    for f in range(FT):
                        pe.matmul(bank(s)[:, 0:P], h1p[:, p, FT + f, P * i:P * i + P], t2T[:, f, NE, :],
                                  start=(p == 0 and f == 0), stop=(p == 2 and f == FT - 1))
                pe.matmul(bank(s)[:, P:2 * P], ohT[:, P * i:P * i + P], s2pT[:], start=True, stop=True).then_inc(full(s), 1)

            run = {"weights": weights, "wturn": wturn, "scales": scales, "xT": xT_turn, "proj": proj, "kT": k_turn, "qT": q_turn,
                   "qk": qk_product, "pv": pv_product, "oT": o_turn, "onT": on_turn, "wo": wo_product, "fhT": fhT,
                   "frouter": frouter, "fohT": fohT, "fmask": fmask, "fw1s": fw1s, "fw1": fw1, "fw2": fw2,
                   "fw2s": fw2s}
            for kind, *at in PLAN:
                if kind in run:
                    run[kind](*at)

        @block.vector
        def _(dve):
            chain = [0]

            def link(ins):
                chain[0] += 1
                ins.then_inc(dch, 1)
                dve.wait_ge(dch, chain[0])

            def weights():
                s = ("weights",)
                dve.wait_ge(small_in, 32)
                dve.wait_ge(wa_in, 16 * 6)
                dve.tensor_copy(identb[:], ident[:]).then_inc(prep_read, 1)
                wait_full(dve, s, 0)
                dve.tensor_copy(kvdT[:], bank(s, 0)[0:32, 0:P]).then_inc(free(s, 0), 1)
                dve.tensor_scalar(wqkv[G][:, 0:P], wraw[G][:, 0:P], nw[G][:, 0:1], None, ALU.mult)
                wait_full(dve, s, 1)
                link(dve.tensor_scalar(wqkv[G][:, P:PW], bank(s, 1)[:, 0:64], nw[G][:, 0:1], None, ALU.mult))
                dve.sem_inc(free(s, 1), 1)
                dve.sem_inc(wqkv_ready, 1)
                wait_full(dve, s, 2)
                dve.tensor_copy(rwT[:], bank(s, 2)[:, 0:NE]).then_inc(free(s, 2), 1)

            def prep():
                dve.wait_ge(wf_in, 16 * 14)
                dve.tensor_scalar(wqkv[L][:], wraw[L][:], nw[L][:, 0:1], None, ALU.mult).then_inc(wqkv_ready, 1)
                link(dve.tensor_reduce(s1c[:], w1n, AX.X, ALU.add, apply_absolute_value=True))
                link(dve.tensor_reduce(s2c[:], w2n, AX.X, ALU.add, apply_absolute_value=True))
                link(dve.tensor_scalar(s1c[:], s1c[:], 1.0 / P, 1e-5, ALU.mult, ALU.max))
                link(dve.tensor_scalar(s2c[:], s2c[:], 1.0 / (FT * P), 1e-5, ALU.mult, ALU.max))
                dve.tensor_scalar(half1[:, 0, :], s1c[:], 0.5, None, ALU.mult)
                dve.tensor_scalar(half2[:, 0, :], s2c[:], 0.5, None, ALU.mult)
                dve.tensor_scalar(half1[:, 1, :], s1c[:], -0.5, None, ALU.mult)
                link(dve.tensor_scalar(half2[:, 1, :], s2c[:], -0.5, None, ALU.mult))
                dve.tensor_scalar(s2diag[:], ident[:], half2[:, 0, NE:NE + 1], None, ALU.mult)
                v = s1c[:, 0:NE * FT].rearrange("p (e f) -> p f e", f=FT)
                link(dve.tensor_copy(s1p[:, :, 0, :], v))
                link(dve.tensor_tensor(s1q[:], v, s1p[:, :, 0, :], ALU.subtract))
                link(dve.tensor_copy(s1p[:, :, 1, :], s1q[:]))
                link(dve.tensor_tensor(s1p[:, :, 2, :], s1q[:], s1p[:, :, 1, :], ALU.subtract))
                link(dve.tensor_copy(s2p[:, 0, :], half2[:, 0, 0:NE]))
                link(dve.tensor_tensor(s2q[:], half2[:, 0, 0:NE], s2p[:, 0, :], ALU.subtract))
                link(dve.tensor_copy(s2p[:, 1, :], s2q[:]))
                dve.tensor_tensor(s2p[:, 2, :], s2q[:], s2p[:, 1, :], ALU.subtract).then_inc(scale_ready, 1)

            def ternary(k):
                rows = sorted({(w, r) for w, r, _ in TURNS[k]})
                for w, r in rows:
                    raw, low, half = (w1n, t1b, half1) if w == 1 else (w2n, t2b, half2)
                    ins = dve.tensor_scalar(low[:, r, :], raw[:, r, :], half[:, 1, r:r + 1], None, ALU.is_lt)
                link(ins)
                for w, r in rows:
                    raw, low, half, t = (w1n, t1b, half1, t1) if w == 1 else (w2n, t2b, half2, t2)
                    ins = dve.scalar_tensor_tensor(out=t[:, r, :], in0=raw[:, r, :], scalar=half[:, 0, r:r + 1],
                                                   in1=low[:, r, :], op0=ALU.is_gt, op1=ALU.subtract)
                ins.then_inc(tern_ready, 1)

            def wturn(k):
                s = ("wturn", k)
                wait_full(dve, s)
                src = bank(s)[:].bitcast(BF16)
                if k < 2:
                    ins = dve.tensor_copy(t1T[:, 8 * k:8 * k + 8, :].rearrange("p k d -> p (k d)"), src)
                elif k == 2:
                    dve.tensor_copy(t1T[:, 16:18, :].rearrange("p k d -> p (k d)"), src[:, 0:2 * P])
                    ins = dve.tensor_copy(t2T[:, :, NE, :], src[:, 2 * P:4 * P].rearrange("p (f d) -> p f d", f=FT))
                else:
                    e = 4 * (k - 3)
                    ins = dve.tensor_copy(t2T[:, :, e:e + 4, :], src.rearrange("p (e f d) -> p f e d", f=FT, d=P))
                link(ins)
                dve.sem_inc(free(s), 1)

            def scales():
                s = ("scales",)
                wait_full(dve, s, 0)
                src = bank(s, 0)[0:3 * NE, :].bitcast(BF16)
                dve.tensor_copy(s1pT[:].rearrange("p f d -> p (f d)"), src[:, 0:2 * P])
                link(dve.tensor_copy(s2pT[:], src[:, 2 * P:3 * P]))
                dve.sem_inc(free(s, 0), 1)
                wait_full(dve, s, 1)
                dve.tensor_copy(s2row[:], bank(s, 1)[:, 0:P]).then_inc(free(s, 1), 1)

            def rows(a, b):
                return X[:, 2 * b:2 * b + 2, :] if a == G else X1[:, b, :, :]

            def stat(a, b):
                src = rows(a, b)
                if a == G:
                    dve.wait_ge(x_in[b], 16)
                if b:
                    dve.wait_ge(xn_ready[a], b)
                for i in range(2):
                    ins = dve.bn_stats(stats[a][:, i, :], src[:, i, :])
                link(ins)
                for i in range(2):
                    ins = dve.bn_aggr(mv[a][:, i, :], stats[a][:, i, :])
                ins.then_inc(mv_ready[a], 1)

            def norm(a, b):
                src = rows(a, b)
                dve.wait_ge(rs_ready[a], b + 1)
                if b:
                    i, n = TAKE[("xT", a, b - 1, 0)]
                    dve.wait_ge(bank_full[i], n + 1)
                for i in range(2):
                    if a == G:
                        dve.tensor_scalar(Hn[:, b % 4, i, :], src[:, i, :], mv[a][:, i, 0:1], rs[a][:, 0, i:i + 1],
                                          ALU.subtract, ALU.mult)
                        ins = dve.tensor_scalar(xn[a][:, i, :], src[:, i, :], mv[a][:, i, 0:1], rs[a][:, 3, i:i + 1],
                                                ALU.subtract, ALU.mult)
                    else:
                        ins = dve.tensor_scalar(xn[a][:, i, :], src[:, i, :], rs[a][:, 3, i:i + 1], None, ALU.mult)
                ins.then_inc(xn_ready[a], 1)

            def proj(a, b):
                s = ("proj", a, b)
                wait_full(dve, s)
                src = bank(s)[:, 0:2 * PW].rearrange("p (i w) -> p i w", i=2)[:, :, 0:QKW]
                s4 = src.rearrange("p i (h d) -> p i h d", d=HD)
                c4, n4 = [t[a][:].rearrange("p i (h d) -> p i h d", d=HD) for t in (cosp, sinp)]
                tab = rope[:, a, :, 2 * b:2 * b + 2, :]

                def wide(t):
                    return t.unsqueeze(2).broadcast_to([P, 2, H + KVH, t.shape[2]])

                dve.tensor_tensor(c4, s4, wide(tab[:, 0]), ALU.mult)
                dve.tensor_tensor(n4[:, :, :, 0::2], s4[:, :, :, 1::2], wide(tab[:, 1, :, 0::2]), ALU.mult)
                link(dve.tensor_tensor(n4[:, :, :, 1::2], s4[:, :, :, 0::2], wide(tab[:, 1, :, 1::2]), ALU.mult))
                if a == G and b == 0:
                    dve.wait_ge(const_ready, 4)
                if a == L and b >= 2:
                    dve.wait_ge(pv_done, PV[(L, b - 1, KVH - 1, 1)] + 1)
                t = 2 * b % kept[a]
                vsrc = bank(s)[:, 0:2 * PW].rearrange("p (i w) -> p i w", i=2)[:, :, QKW:PW]
                dve.tensor_copy(V[a][:, t:t + 2, :, 0:HD],
                                vsrc.rearrange("p i (g d) -> p i g d", d=HD)).then_inc(v_ready[a], 1)
                dve.wait_ge(v_ready[a], b + 1)
                dve.sem_inc(free(s), 1)
                link(dve.tensor_tensor(qk[a][:], cosp[a][:], sinp[a][:], ALU.add))
                link(dve.tensor_tensor(cosp[a][:], qk[a][:], qk[a][:], ALU.mult))
                dve.tensor_reduce(ss[a][:], cosp[a][:].rearrange("p i (h d) -> p (i h) d", d=HD), AX.X,
                                  ALU.add).then_inc(ss_ready[a], 1)

            def split(a, b):
                dve.wait_ge(ny_ready[a], b + 1)
                if b:
                    dve.wait_ge(term_ready[a], 2 * b)
                y = ny[a][:].unsqueeze(2).broadcast_to([P, 2 * (H + KVH), HD])
                link(dve.tensor_tensor(qn[a][:].rearrange("p i (h d) -> p (i h) d", d=HD),
                                       qk[a][:].rearrange("p i (h d) -> p (i h) d", d=HD), y, ALU.mult))
                link(dve.tensor_copy(part[a][:, 0], qn[a][:]))
                link(dve.tensor_tensor(res[a][:], qn[a][:], part[a][:, 0], ALU.subtract))
                link(dve.tensor_copy(part[a][:, 1], res[a][:]))
                dve.tensor_tensor(part[a][:, 2], res[a][:], part[a][:, 1], ALU.subtract).then_inc(part_ready[a], 1)

            def k_copy(a, b):
                s = ("kT", a, b)
                wait_full(dve, s)
                if a == L and b >= 2:
                    dve.wait_ge(qk_done, UNIT[(L, b - 1, KVH - 1, 1)] + 1)
                k = P * (2 * b % kept[a])
                dve.tensor_copy(kT[a][:, :, k:k + QB],
                                bank(s)[:].bitcast(BF16).rearrange("p (g q) -> p g q", g=KVH)).then_inc(free(s), 1)
                dve.wait_ge(free(s), TAKE[(*s, 0)][1] + 1)
                dve.sem_inc(kT_ready[a], 1)

            def q_copy(a, b, i):
                s = ("qT", a, b, i)
                wait_full(dve, s)
                if b >= 2:
                    last = (a, b - 2, *units_of(a, b - 2)[-1])
                    dve.wait_ge(qk_done, UNIT[last] + 1)
                dve.tensor_copy(qT[a][:, b % 2, :, P * i:P * i + P],
                                bank(s)[:].bitcast(BF16).rearrange("p (m q) -> p m q", m=H // 2)).then_inc(free(s), 1)
                dve.wait_ge(free(s), TAKE[(*s, 0)][1] + 1)
                dve.sem_inc(qT_ready[a], 1)

            def o_copy(a, b, g):
                u = (a, b, g, 2 * b + 1 if a == G else 1)
                dve.wait_ge(pv_done, PV[u] + 1)
                if b:
                    i, n = TAKE[("oT", a, b - 1, 1, 0)]
                    dve.wait_ge(bank_full[i], n + 1)
                o, f = (osum_g, o_free) if a == G else (bank(("pv", L, b, g, 0)), free(("pv", L, b, g, 0)))
                link(dve.tensor_copy(oTs[a][:, g, :], o[:, 0:QB]))
                dve.sem_inc(f, 1)
                dve.sem_inc(oT_ready[a], 1)

            def o_scale(a, b, i):
                s = ("oT", a, b, i)
                wait_full(dve, s)
                if b:
                    j, n = TAKE[("onT", a, b - 1, 0)]
                    dve.wait_ge(bank_full[j], n + 1)
                o = bank(s)[:].rearrange("p (h c) -> p h c", c=32)
                link(dve.reciprocal(rec[a][:].unsqueeze(2), o[:, :, HD:HD + 1]))
                link(dve.tensor_tensor(on[a][:, i, :].rearrange("p (h d) -> p h d", d=HD), o[:, :, 0:HD],
                                       rec[a][:].unsqueeze(2).broadcast_to([P, H, HD]), ALU.mult))
                dve.sem_inc(free(s), 1)
                dve.sem_inc(on_ready[a], 1)

            def residual(a, b):
                s = ("wo", a, b)
                wait_full(dve, s)
                src = bank(s)[:, 0:QB].rearrange("p (i d) -> p i d", i=2)
                if a == G:
                    link(dve.tensor_tensor(X1[:, b], src, Hn[:, b % 4], ALU.add))
                else:
                    link(dve.tensor_tensor(X2[:], src, X1[:, b], ALU.add))
                dve.sem_inc(free(s), 1)

            def fstat(b):
                for i in range(2):
                    ins = dve.bn_stats(fst[:, 0, i, :], X2[:, i, :])
                link(ins)
                for i in range(2):
                    ins = dve.bn_aggr(fmv[:, 0, i, :], fst[:, 0, i, :])
                ins.then_inc(fmv_ready, 1)

            def fxa(b):
                dve.wait_ge(frs_ready, 4 * b + 1)
                for i in range(2):
                    ins = dve.tensor_scalar(ftmp[:, i, :], X2[:, i, :], frs[:, 0, i:i + 1], frs[:, 1, i:i + 1],
                                            ALU.mult, ALU.subtract)
                link(ins)
                link(dve.tensor_tensor(xa[:], X[:, 2 * b:2 * b + 2, :], ftmp[:], ALU.add))
                for i in range(2):
                    ins = dve.bn_stats(fst[:, 1, i, :], xa[:, i, :])
                link(ins)
                for i in range(2):
                    ins = dve.bn_aggr(fmv[:, 1, i, :], fst[:, 1, i, :])
                ins.then_inc(fmv_ready, 1)

            def fh_norm(b):
                dve.wait_ge(frs_ready, 4 * b + 2)
                for i in range(2):
                    ins = dve.tensor_scalar(fh[:, i, :], xa[:, i, :], fmv[:, 1, i, 0:1], frs[:, 5, i:i + 1],
                                            ALU.subtract, ALU.mult)
                ins.then_inc(fh_ready, 1)

            def fparts(b):
                i, n = TAKE[("fhT", b, 0)]
                dve.wait_ge(bank_free[i], n + 1)
                link(dve.tensor_copy(hp[:, 0, :], hT[:]))
                link(dve.tensor_tensor(hres[:], hT[:], hp[:, 0, :], ALU.subtract))
                link(dve.tensor_copy(hp[:, 1, :], hres[:]))
                dve.tensor_tensor(hp[:, 2, :], hres[:], hp[:, 1, :], ALU.subtract).then_inc(hp_ready, 1)

            def frouter(b):
                s = ("frouter", b)
                wait_full(dve, s)
                lg = bank(s)[:, 0:2 * NE].rearrange("p (i e) -> p i e", i=2)
                wide = lambda t: t.unsqueeze(2).broadcast_to([P, 2, NE])
                link(dve.tensor_reduce(lmax[:], lg, AX.X, ALU.max))
                link(dve.tensor_tensor(lsh[:], lg, wide(lmax[:]), ALU.subtract))
                dve.sem_inc(lsh_ready, 1)
                dve.sem_inc(free(s), 1)
                link(dve.tensor_scalar(leq[:], lsh[:], 0.0, None, ALU.is_equal))
                link(dve.tensor_tensor(lrk[:], leq[:], rank[:].unsqueeze(1).broadcast_to([P, 2, NE]), ALU.mult))
                link(dve.tensor_reduce(lbest[:], lrk[:], AX.X, ALU.max))
                if b:
                    dve.wait_ge(full(("fw1s", b - 1), 0), TAKE[("fw1s", b - 1, 0)][1] + 1)
                for i in range(2):
                    ins = dve.tensor_tensor(oh[:, i], lrk[:, i].unsqueeze(1).broadcast_to([P, 3, NE]),
                                            lbest[:, i:i + 1].unsqueeze(2).broadcast_to([P, 3, NE]), ALU.is_equal)
                ins.then_inc(oh_ready, 1)

            def fohT(b):
                s = ("fohT", b)
                wait_full(dve, s)
                link(dve.tensor_copy(ohT[:], bank(s)[0:24, :].bitcast(BF16)[:, 0:QB]))
                dve.sem_inc(free(s), 1)
                dve.sem_inc(ohT_ready, 1)
                dve.wait_ge(lex_ready, b + 1)
                link(dve.tensor_reduce(lsum[:], lex[:], AX.X, ALU.add))
                link(dve.reciprocal(tp[:], lsum[:]))

            def fmask(b, i):
                s = ("fmask", b, i)
                wait_full(dve, s)
                m = bank(s)[:].bitcast(BF16).rearrange("p (e q) -> p e q", e=NE)
                h = hp[:, :, P * i:P * i + P]
                for e in range(NE):
                    ins = dve.tensor_tensor(hm[:, e, :, P * i:P * i + P], h, m[:, e, :].unsqueeze(1).broadcast_to([P, 3, P]),
                                            ALU.mult)
                link(ins)
                dve.sem_inc(free(s), 1)
                dve.sem_inc(hm_ready, 1)

            def fw1s(b):
                s = ("fw1s", b)
                wait_full(dve, s, 1)
                for f in range(FT):
                    ins = dve.tensor_scalar(z[:, FT + f, :], bank(s, 1)[:, QB * f:QB * f + QB],
                                            s1c[:, NE * FT + f:NE * FT + f + 1], None, ALU.mult)
                link(ins)
                dve.sem_inc(free(s, 1), 1)

            def fw1(b, f):
                s = ("fw1", b, f)
                wait_full(dve, s)
                i, n = TAKE[("fw1s", b, 0)]
                dve.wait_ge(bank_free[i], n + 1)
                link(dve.tensor_tensor(z[:, f, :], bank(s)[:, 0:QB], s1s[:, f, :], ALU.mult))
                dve.sem_inc(free(s), 1)
                if f == 1:
                    dve.sem_inc(z_ready, 1)

            def fh1(b):
                dve.wait_ge(ez_ready, b + 1)
                link(dve.scalar_tensor_tensor(out=h1, in0=ez, scalar=1.0, in1=z, op0=ALU.add, op1=ALU.mult))
                link(dve.tensor_copy(h1p[:, 0], h1))
                link(dve.tensor_tensor(zr, h1, h1p[:, 0], ALU.subtract))
                link(dve.tensor_copy(h1p[:, 1], zr))
                dve.tensor_tensor(h1p[:, 2], zr, h1p[:, 1], ALU.subtract).then_inc(h1p_ready, 1)

            def fw2(b, i):
                s = ("fw2", b, i)
                for j in range(2):
                    wait_full(dve, s, j)
                    link(dve.tensor_tensor(sel[:, 4 * j:4 * j + 4, :], bank(s, j)[:].rearrange("p (e d) -> p e d", e=4),
                                           oh[:, i, 0, 4 * j:4 * j + 4].unsqueeze(2).broadcast_to([P, 4, P]), ALU.mult))
                    dve.sem_inc(free(s, j), 1)
                link(dve.tensor_reduce(acc[:], sel.rearrange("p e d -> p d e"), AX.X, ALU.add))

            def fw2s(b, i):
                s = ("fw2s", b, i)
                wait_full(dve, s)
                link(dve.tensor_tensor(accs[:], acc[:], bank(s)[:, P:2 * P], ALU.mult))
                link(dve.tensor_tensor(shd[:], bank(s)[:, 0:P], s2row[:], ALU.mult))
                dve.sem_inc(free(s), 1)
                link(dve.scalar_tensor_tensor(out=fo[:, i, :], in0=accs[:], scalar=tp[:, i:i + 1], in1=shd[:], op0=ALU.mult,
                                              op1=ALU.add))
                link(dve.bn_stats(fst[:, 2, i, :], fo[:, i, :]))
                dve.bn_aggr(fmv[:, 2, i, :], fst[:, 2, i, :]).then_inc(fmv_ready, 1)

            def fout(b, i):
                dve.wait_ge(frs_ready, 4 * b + 3 + i)
                link(dve.tensor_scalar(fl[:], fo[:, i, :], fmv[:, 2, i, 0:1], frs[:, 6 + i, 1:2], ALU.subtract, ALU.mult))
                if b:
                    dve.wait_ge(y_out, 16 * (2 * b))
                dve.tensor_tensor(yout[:, i, :], xa[:, i, :], fl[:], ALU.add).then_inc(y_ready, 1)

            run = {"weights": weights, "prep": prep, "ternary": ternary, "wturn": wturn, "scales": scales,
                   "stat": stat, "norm": norm, "proj": proj, "split": split, "kT": k_copy, "qT": q_copy,
                   "oevac": o_copy, "oT": o_scale, "wo": residual, "fstat": fstat, "fxa": fxa, "fh": fh_norm,
                   "fparts": fparts, "frouter": frouter, "fohT": fohT, "fmask": fmask, "fw1s": fw1s, "fw1": fw1,
                   "fh1": fh1, "fw2": fw2, "fw2s": fw2s, "fout": fout}
            for kind, *at in PLAN:
                if kind in run:
                    run[kind](*at)


def tables():
    tokens = np.arange(TILES * P, dtype=np.float32)
    rope = np.zeros((P, 2, 2, TILES, HD), np.float32)
    for a, base in enumerate((1000000.0, 10000.0)):
        inv = np.float32(1.0) / np.float32(base) ** (np.arange(0, HD, 2, dtype=np.float32) / np.float32(HD))
        freq = (tokens[:, None] * inv[None, :].astype(np.float32)).astype(np.float64)
        c = np.repeat(np.cos(freq), 2, axis=1)
        s = np.stack([-np.sin(freq), np.sin(freq)], axis=-1).reshape(TILES * P, HD)
        for k, t in enumerate((c, s)):
            rope[:, a, k] = t.astype(np.float32).reshape(TILES, P, HD).transpose(1, 0, 2)
    key = np.arange(P)[:, None]
    before = np.arange(WIN)[None, :] + P - key < WIN
    i = np.arange(P + WIN)[None, :] - key
    band = np.concatenate([before, (i >= 0) & (i < WIN)], axis=1).astype(np.float32)
    rank = np.repeat(np.arange(NE, 0, -1, dtype=np.float32)[None, :], P, axis=0)
    return {"ident": np.eye(P, dtype=np.float32), "rope": rope, "band": band, "rank": rank}


_INS = ["L0_attn_hidden", "L0_attn_norm1_w", "L0_attn_norm2_w", "L0_attn_g_wq", "L0_attn_g_kv_down",
        "L0_attn_g_k_up", "L0_attn_g_v_up", "L0_attn_g_wo", "L0_attn_l_wq", "L0_attn_l_wk", "L0_attn_l_wv",
        "L0_attn_l_wo", "L0_ffn_shared_w1", "L0_ffn_shared_w2", "L0_ffn_expert_w1", "L0_ffn_expert_w2",
        "L0_ffn_router_w", "L0_ffn_ln_gamma", "L0_ffn_ln_beta"]


def kernel(**inputs):
    import concourse.bacc as _bacc
    from concourse.bass_utils import run_bass_kernel_spmd as _run

    nc = _bacc.Bacc("TRN2", target_bir_lowering=False, num_devices=1)
    arrays, args = {}, []
    given = {name: np.ascontiguousarray(inputs[name]) for name in _INS}
    for name, a in {**given, **tables()}.items():
        arrays[f"in_{name}_dram"] = a
        args.append(nc.dram_tensor(f"in_{name}_dram", a.shape, mybir.dt.from_np(a.dtype), kind="ExternalInput").ap())
    args.append(nc.dram_tensor("out_0_dram", (1, TILES * P, P), F32, kind="ExternalOutput").ap())
    build(nc, *args)
    r = _run(nc, [arrays], core_ids=[0])
    return r.results[0]["out_0_dram"]
```

```python
from contextlib import ExitStack

import numpy as np

import concourse.bass as bass
from concourse import mybir

F32 = mybir.dt.float32
BF16 = mybir.dt.bfloat16
I32 = mybir.dt.int32
ALU = mybir.AluOpType
ACT = mybir.ActivationFunctionType
AX = mybir.AxisListType

P = 128
TILES = 16
NB = TILES // 2
QB = 2 * P
H, KVH, HD = 16, 4, 8
GRP = H // KVH
WIN = 32
NE, FT = 8, 2
QKW = (H + KVH) * HD
PW = QKW + KVH * HD
TERMS = 8
EPS_LN, EPS_RMS = 1e-5, 1e-6
MAGIC = float(0x5F3759DF)
G, L = 0, 1
NMISC = 3
Q_KEPT = [2, 1]
KEPT = 4
NP = 5


def units_of(a, b):
    if a == G:
        return [(g, kb) for g in range(KVH) for kb in [2 * b, 2 * b + 1, *range(2 * b)]]
    return [(g, u) for g in range(KVH) for u in range(2)]


def pieces(a, b, kb):
    if a == G:
        lo = P if kb == 2 * b + 1 else 0
        return [(kb, lo, QB - lo, lo)]
    if kb == 1:
        return [(2 * b + 1, P, P, 0)]
    return ([(2 * b - 1, 0, WIN, 0)] if b else []) + [(2 * b, 0, P + WIN, WIN)]


TURNS = [[(1, k, 0) for k in range(8)], [(1, k, 0) for k in range(8, 16)],
         [(1, 16, 0), (1, 17, 0), (2, NE, 0), (2, NE, 1)],
         [(2, k, f) for k in range(4) for f in range(FT)], [(2, k, f) for k in range(4, 8) for f in range(FT)]]

GLUED = -1


def front_steps(a, b):
    return [(1, ("stat", a, b)), (1, ("norm", a, b)), (1, ("xT", a, b)), (1, ("proj", a, b)), (1, ("newton", a, b, 1)),
            (1, ("newton", a, b, 2)), (1, ("split", a, b)), (1, ("expand", a, b, 0)), (1, ("expand", a, b, 1)),
            (1, ("kT", a, b)), (0, ("qT", a, b, 0)), (0, ("qT", a, b, 1))]


def out_steps(a, b):
    return [(1, ("oT", a, b, 0)), (0, ("oT", a, b, 1)), (1, ("onT", a, b)), (1, ("wo", a, b))]


def local_scores(b):
    return [x for g in range(KVH) for x in [(int(not g), ("qk", L, b, g, 0)), (GLUED, ("qk", L, b, g, 1))]]


def local_sums(b):
    return [x for g in range(KVH)
            for x in [(1, ("pv", L, b, g, 0)), (GLUED, ("pv", L, b, g, 1)), (GLUED, ("oevac", L, b, g))]]


def norm_steps(b):
    return [(1, ("fstat", b)), (1, ("fxa", b)), (1, ("fh", b))]


def ffn_steps(b):
    return [(1, ("fhT", b)), (1, ("frouter", b)), (0, ("fparts", b)),
            (1, ("fohT", b)), (1, ("fmask", b, 0)), (0, ("fmask", b, 1)), (0, ("fw1s", b)), (1, ("fw1", b, 0)),
            (1, ("fz", b, 0)), (0, ("fw1", b, 1)), (1, ("fz", b, 1)), (1, ("fact", b)), (1, ("fh1", b)), (1, ("fw2", b, 0)),
            (1, ("fsel", b, 0)), (0, ("fw2s", b, 0)), (1, ("fsum", b, 0)), (0, ("fw2", b, 1)), (1, ("fsel", b, 1)),
            (0, ("fout", b, 0)), (0, ("fw2s", b, 1)), (1, ("fsum", b, 1)), (1, ("fout", b, 1))]


def weight_steps():
    out = [(1, ("prep",))]
    for k in range(len(TURNS)):
        out += [(1, ("ternary", k)), (1, ("wturn", k))]
    return out + [(1, ("scales",))]


PE, DVE, POOL, ACT_E = range(4)
COST = {
    "weights": [(PE, 9.0)], "prep": [(DVE, 8.0)], "ternary": [(DVE, 3.0)], "wturn": [(PE, 0.6), (DVE, 0.6)],
    "scales": [(DVE, 1.5), (PE, 0.5), (DVE, 0.8)],
    "stat": [(DVE, 0.7), (POOL, 2.0)], "norm": [(DVE, 0.7)], "xT": [(PE, 0.3), (ACT_E, 0.35)],
    "proj": [(PE, 0.8), (DVE, 2.8), (POOL, 0.5)], "newton": [(POOL, 1.9)], "split": [(DVE, 2.2)],
    "expand": [(POOL, 2.0)], "kT": [(PE, 0.8), (DVE, 0.6)], "qT": [(PE, 0.55), (DVE, 1.3)],
    "oT": [(PE, 0.45), (DVE, 0.7)], "onT": [(PE, 0.25), (ACT_E, 0.3)], "wo": [(PE, 0.5), (DVE, 0.35)],
    "oevac": [(ACT_E, 0.3)], "pv": [(PE, 0.465)],
    "fstat": [(DVE, 0.7), (POOL, 1.1)], "fxa": [(DVE, 1.8), (POOL, 2.6)], "fh": [(DVE, 0.5)],
    "fhT": [(PE, 0.3), (ACT_E, 0.45)], "frouter": [(PE, 0.4), (ACT_E, 0.15), (DVE, 1.4)], "fparts": [(DVE, 1.5)],
    "fohT": [(PE, 0.15), (DVE, 0.8)], "fmask": [(PE, 0.5), (DVE, 2.3)], "fw1s": [(PE, 1.0), (DVE, 0.8)],
    "fw1": [(PE, 2.9)], "fz": [(DVE, 0.35)], "fact": [(ACT_E, 1.0)], "fh1": [(DVE, 5.1)], "fw2": [(PE, 2.9)],
    "fsel": [(DVE, 2.6)], "fw2s": [(PE, 0.4)], "fsum": [(DVE, 1.5), (POOL, 0.7)], "fout": [(DVE, 0.6)],
}
HOP = 0.5
STALL_PE, STALL_OTHER = 0.98, 0.432
PULL = {"pv": -0.5, "close": 0.8, "local": 0.9, "attend": 0.6, "norms": 0.8, "feed": 0.0, "front": 0.5, "qk": 0.0, "evac": 0.3}


def cost(s):
    if s[0] == "qk":
        mask = [] if s[1] == G and s[4] < 2 * s[2] else [(POOL, 1.275 if s[1] == G else 1.6)]
        return [(PE, 0.419), (ACT_E, 1.0), *mask]
    return COST[s[0]]


ended = {}


class Chain:

    def __init__(self, name, steps=(), ready=0.0):
        self.name, self.steps, self.ready, self.last = name, list(steps), ready, ready

    def start(self):
        flag, s = self.steps[0]
        if s[0] == "pv":
            return ended.get((*s[1:4], 1), 0.0)
        return self.last if flag else self.ready


TAKES = {"weights": 3, "wturn": 1, "scales": 2, "xT": 1, "proj": 1, "qT": 1, "kT": 1, "oT": 1, "onT": 1, "wo": 1,
         "fhT": 1, "frouter": 1, "fohT": 1,
         "fmask": 1, "fw1s": 2, "fw1": 1, "fw2": 2, "fw2s": 1}
HELD = {"fw1": "fz", "fw2": "fsel", "fw2s": "fsum"}


FIRST = {"stat": ("norm",), "norm": ("xT",), "xT": ("proj",), "proj": ("split",), "split": ("expand", 1), "expand": ("qT", 1)}


def holds(s, held):
    if s[0] in HELD:
        held.append(s)
    for h in list(held):
        if HELD[h[0]] == s[0] and h[1:] == s[1:]:
            held.remove(h)


def make_plan():
    plan = []
    close, attend, norms, local, score = [Chain(n) for n in ("close", "attend", "norms", "local", "attend")]
    feed = Chain("feed", weight_steps(), 60.0)
    fronts = [Chain("front", [s for b in range(i, NB, 2) for s in front_steps(G, b)]) for i in range(2)]
    chains = [close, attend, score, norms, local, feed, *fronts]
    free = [0.0] * 4
    slots = [0.0, 0.0]
    banks_free = [0.0] * NMISC

    units_out, sums_out, held = [], set(), []

    def banks(s):
        return TAKES.get(s[0], 0) + sum(TAKES[h[0]] for h in held) <= NMISC

    def reads_done(s):
        kind, a, *at = s
        b = at[0] if at else a
        if kind in FIRST and b and (*[FIRST[kind][0], a, b - 1], *FIRST[kind][1:]) not in plan:
            return False
        if kind == "norm" and a == G and b >= 3:
            return ("wo", G, b - 3) in plan
        if kind == "proj" and a == L and ("prep",) not in plan:
            return False
        if kind == "proj" and a == L and b >= KEPT // 2:
            return ("oevac", L, b - KEPT // 2 + 1, KVH - 1) in plan
        if kind == "qT" and b >= Q_KEPT[a]:
            return ("qk", a, b - Q_KEPT[a], *units_of(a, b - Q_KEPT[a])[-1]) in plan
        if kind == "fh" and b:
            return ("fhT", b - 1) in plan
        return True

    def room(n=1):
        return all(u in sums_out for u in units_out[-NP:][:n]) if len(units_out) >= NP else True

    def tried(s, ready, commit=False):
        now = free[PE]
        segs, t, stall, ends = cost(s), ready, 0.0, []
        if s[0] == "qk":
            t = max(t, slots[0])
        k = TAKES.get(s[0], 0)
        if k:
            t = max(t, sorted(banks_free)[k - 1])
        for e, d in segs:
            t = max(t, free[e])
            stall += (STALL_PE if e == PE else STALL_OTHER) * max(0.0, t - max(free[e], now))
            t += d
            ends.append((e, t))
            t += HOP
        if commit:
            for e, x in ends:
                free[e] = x
            if s[0] == "qk":
                slots.pop(0)
                slots.append(ends[1][1])
            if k:
                banks_free.sort()
                banks_free[:k] = [ends[min(1, len(ends) - 1)][1] + HOP] * k
        return stall, t

    def put(s, ready):
        if s[0] == "qk":
            assert room()
            units_out.append(s[1:])
        if s[0] == "pv":
            sums_out.add(s[1:])
        assert banks(s)
        _, t = tried(s, ready, True)
        if s[0] == "qk":
            ended[s[1:]] = t
        holds(s, held)
        if s[0] in HELD.values():
            k = 2 if s[0] == "fsel" else 1
            banks_free.sort()
            banks_free[:k] = [t] * k
        plan.append(s)
        return t

    def allowed(s):
        return (s[0] != "qk" or room(2)) and (s[0] != "pv" or s[1:] in ended) and banks(s) and (len(s) == 1 or reads_done(s))

    def advance(chain):
        chain.ready = chain.start()
        s = chain.steps.pop(0)[1]
        t = put(s, chain.ready)
        while chain.steps and chain.steps[0][0] == GLUED:
            s2 = chain.steps.pop(0)[1]
            t = put(s2, t if s2[0] == "oevac" else chain.ready)
        chain.last = max(t, chain.last)
        for to, steps in ((local, front_steps(L, s[2]) if s[:2] == ("wo", G) else []),
                          (score, local_scores(s[2]) if s[:2] == ("qT", L) and s[3] else []),
                          (attend, local_sums(s[2]) + out_steps(L, s[2]) if s[:2] == ("qT", L) and s[3] else []),
                          (norms, norm_steps(s[2]) if s[:2] == ("wo", L) else []),
                          (feed, ffn_steps(s[1]) if s[0] == "fh" else [])):
            if steps:
                if not to.steps:
                    to.last = max(to.last, t)
                to.steps += steps

    put(("weights",), 0.0)
    blocks = [(b, u) for b in range(NB) for u in units_of(G, b)]
    late = []
    left = {(b, g): 2 * b + 2 for b in range(NB) for g in range(KVH)}
    evac = []
    while blocks or late or evac or any(c.steps for c in chains):
        options = []
        for c in chains:
            if c.steps and allowed(c.steps[0][1]):
                s = c.steps[0][1]
                options.append((tried(s, c.start())[0] - PULL[c.name], c.name, c))
        if blocks and room() and len(late) < NP - 1:
            b, (g, kb) = blocks[0]
            if ("qT", G, b, 1) in plan:
                options.append((tried(("qk", G, b, g, kb), 0.0)[0] - PULL["qk"], "qk", None))
        if evac:
            options.append((tried(*evac[0])[0] - PULL["evac"], "evac", None))
        elif late:
            b, g = late[0][1], late[0][2]
            if left[(b, g)] > 1 or not b or ("oT", G, b - 1, 1) in plan:
                for u in late:
                    if u[1:3] == (b, g):
                        options.append((tried(("pv", *u), ended[u])[0] - PULL["pv"], "pv", u))
        _, name, what = min(options, key=lambda o: o[0])
        if name == "qk":
            u = (G, b := blocks[0][0], *blocks[0][1])
            blocks.pop(0)
            put(("qk", *u), 0.0)
            late.append(u)
        elif name == "pv":
            late.remove(what)
            t = put(("pv", *what), ended[what])
            left[what[1:3]] -= 1
            if not left[what[1:3]]:
                evac.append((("oevac", *what[:3]), t))
        elif name == "evac":
            s, t = evac.pop(0)
            t = put(s, t)
            if s[3] == KVH - 1:
                if not close.steps:
                    close.last = max(close.last, t)
                close.steps += out_steps(G, s[2])
        else:
            advance(what)
    return plan


PLAN = make_plan()


def number():
    unit, pv, osum, take, masks, ends = {}, {}, {}, {}, {}, {}
    held, used, order = [], [0] * NMISC, list(range(NMISC))
    for s in PLAN:
        if s[0] == "qk":
            unit[s[1:]] = len(unit)
            if s[1] == L or s[4] >= 2 * s[2]:
                masks[s[1:]] = len(masks)
        if s[0] == "pv":
            pv[s[1:]] = len(pv)
            if s[1] == G and s[2:4] not in osum:
                osum[s[2:4]] = len(osum)
            ends.setdefault(s[1:4], [s[1:], s[1:]])[1] = s[1:]
        k = TAKES.get(s[0], 0)
        if s[0] == "pv" and s[1] == L and s[4] == 0:
            k = 1
        for j in range(k):
            i = next(i for i in order if i not in [take[(*h, k)][0] for h in held for k in range(TAKES[h[0]])])
            order.remove(i)
            order.append(i)
            take[(*s, j)] = (i, used[i])
            used[i] += 1
        holds(s, held)
    return unit, pv, osum, take, masks, ends


UNIT, PV, OSUM, TAKE, MASK, ENDS = number()
UNIT_LIST = list(UNIT)


def build(nc, x, norm1_w, norm2_w, g_wq, g_kv_down, g_k_up, g_v_up, g_wo, l_wq, l_wk, l_wv, l_wo,
          sw1, sw2, ew1, ew2, router_w, ln_gamma, ln_beta, ident_d, rope_d, band_d, rank_d, out):
    with ExitStack() as ctx:
        def sb(name, shape, dt=F32):
            return ctx.enter_context(nc.sbuf_tensor(name, shape, dt))

        def sem(name):
            return ctx.enter_context(nc.semaphore(name))

        def pair(name):
            return [sem(f"{name}_g"), sem(f"{name}_l")]

        def two(name, shape, dt=F32):
            return [sb(f"{name}_g", shape, dt), sb(f"{name}_l", shape, dt)]

        scores = [ctx.enter_context(nc.psum_tensor(f"scores{i}", [P, 1024], F32)) for i in range(2)]
        osum_g = ctx.enter_context(nc.psum_tensor("osum_g", [P, 512], F32))
        misc = [ctx.enter_context(nc.psum_tensor(f"misc{i}", [P, 512], F32)) for i in range(NMISC)]

        ident = sb("ident", [P, P])
        identb = sb("identb", [P, P], BF16)
        rope = sb("rope", [P, 2, 2, TILES, HD])
        band = sb("band", [P, P + 2 * WIN])
        rank = sb("rank", [P, NE])
        mhalf = sb("mhalf", [P, 4])
        ones = sb("ones", [P, P])
        nw = [sb("nw_g", [P, 1]), sb("nw_l", [P, 1])]
        wraw = two("wraw", [P, PW])
        wqkv = two("wqkv", [P, PW])
        wo_sb = two("wo", [P, P])
        kvd = sb("kvd", [P, 32])
        kvdT = sb("kvdT", [32, P])
        kvup = sb("kvup", [32, 64])
        gamma = sb("gamma", [P, 1])
        beta = sb("beta", [P, 1])
        rw = sb("rw", [NE, P])
        rwT = sb("rwT", [P, NE])
        early = sb("early", [P, 2 * (NE + 1) * FT * P])
        w1n = early[:, 0:(NE + 1) * FT * P].rearrange("p (k d) -> p k d", d=P)
        w2n = early[:, (NE + 1) * FT * P:].rearrange("p (k d) -> p k d", d=FT * P)
        s1c = sb("s1c", [P, NE * FT + FT])
        s2c = sb("s2c", [P, NE + 1])
        half1 = sb("half1", [P, 2, NE * FT + FT])
        half2 = sb("half2", [P, 2, NE + 1])
        early2 = sb("early2", [P, 2 * (NE + 1) * FT * P])
        NW = (NE + 1) * FT * P
        tb = early2[:].bitcast(BF16)
        t1, t1b = [tb[:, k * NW:k * NW + NW].rearrange("p (k d) -> p k d", d=P) for k in (0, 1)]
        t2, t2b = [tb[:, k * NW:k * NW + NW].rearrange("p (k d) -> p k d", d=FT * P) for k in (2, 3)]
        t1T = sb("t1T", [P, NE * FT + FT, P], BF16)
        t2T = sb("t2T", [P, FT, NE + 1, P], BF16)
        s1p = sb("s1p", [P, FT, 3, NE], BF16)
        s1q = sb("s1q", [P, FT, NE])
        s2p = sb("s2p", [P, 3, NE], BF16)
        s2q = sb("s2q", [P, NE])
        s1pT = sb("s1pT", [3 * NE, FT, P], BF16)
        s2pT = sb("s2pT", [3 * NE, P], BF16)
        s2diag = sb("s2diag", [P, P])
        s2row = sb("s2row", [P, P])

        X = sb("X", [P, TILES, P])
        Hn = sb("Hn", [P, 3, 2, P])
        X1 = sb("X1", [P, NB, 2, P])
        stats = two("stats", [P, 2, 6])
        mv = two("mv", [P, 2, 2])
        rs = two("rs", [P, 8, 2])
        xn = two("xn", [P, 2, P])
        xT = two("xT", [P, QB])
        cosp = two("cosp", [P, 2, QKW])
        sinp = two("sinp", [P, 2, QKW])
        qk = two("qk", [P, 2, QKW])
        ss = two("ss", [P, 2 * (H + KVH)])
        nv = two("nv", [P, 2 * (H + KVH)])
        ny = two("ny", [P, 2 * (H + KVH)])
        nt = two("nt", [P, 2 * (H + KVH)])
        qn, res = sinp, cosp
        part = two("part", [P, 3, 2, QKW], BF16)
        qe = two("qe", [P, 2, H, TERMS, HD], BF16)
        ke = two("ke", [P, 2, KVH, TERMS, HD], BF16)
        qT = [sb(f"qT{a}", [P, Q_KEPT[a], H // 2, 2, QB], BF16) for a in (G, L)]
        kept = [TILES, KEPT]
        kT = [sb(f"kT{a}", [P, KVH, kept[a] * P], BF16) for a in (G, L)]
        V = [sb(f"V{a}", [P, kept[a], KVH, 32]) for a in (G, L)]
        prob = sb("prob", [P, NP, 4, QB])
        oTs = two("oTs", [P, KVH, QB])
        rec = two("rec", [P, H])
        on = two("on", [P, 2, P])
        onT = two("onT", [P, QB])

        fst = sb("fst", [P, 3, 2, 6])
        fmv = sb("fmv", [P, 3, 2, 2])
        frs = sb("frs", [P, 10, 2])
        ftmp = sb("ftmp", [P, 2, P])
        fh = sb("fh", [P, 2, P])
        hT = sb("hT", [P, QB])
        hres = sb("hres", [P, QB])
        hp = sb("hp", [P, 3, QB], BF16)
        lmax = sb("lmax", [P, 2])
        lsh = sb("lsh", [P, 2, NE])
        lex = sb("lex", [P, 2, NE])
        lsum = sb("lsum", [P, 2])
        tp = sb("tp", [P, 2])
        leq = sb("leq", [P, 2, NE])
        lrk = sb("lrk", [P, 2, NE])
        lbest = sb("lbest", [P, 2])
        oh = sb("oh", [P, 2, 3, NE], BF16)
        ohT = sb("ohT", [3 * NE, QB], BF16)
        hm = early[:].bitcast(BF16)[:, 0:NE * 3 * QB].rearrange("p (e a q) -> p e a q", e=NE, a=3)
        s1s = sb("s1s", [P, FT, QB])
        z, ez, zr, h1 = [early2[:, 2 * FT * QB * k:2 * FT * QB * (k + 1)].rearrange("p (f q) -> p f q", q=QB)
                         for k in range(4)]
        h1p = sb("h1p", [P, 3, 2 * FT, QB], BF16)
        sel = early[:, NE * 3 * QB // 2:NE * 3 * QB // 2 + NE * P].rearrange("p (e d) -> p e d", e=NE)
        acc = sb("acc", [P, P])
        accs = sb("accs", [P, P])
        shd = sb("shd", [P, P])
        fo = sb("fo", [P, 2, P])
        fl = sb("fl", [P, P])

        x_in = [sem(f"x_in{b}") for b in range(NB)]
        small_in = sem("small_in")
        wa_in = sem("wa_in")
        wf_in = sem("wf_in")
        y_out = sem("y_out")
        dch = sem("dch")
        pch = sem("pch")
        const_ready = sem("const_ready")
        bank_full = [sem(f"bank_full{i}") for i in range(NMISC)]
        bank_free = [sem(f"bank_free{i}") for i in range(NMISC)]
        wqkv_ready = sem("wqkv_ready")
        tern_ready = sem("tern_ready")
        scale_ready = sem("scale_ready")
        prep_read = sem("prep_read")
        mv_ready = pair("mv_ready")
        rs_ready = pair("rs_ready")
        xn_ready = pair("xn_ready")
        xT_ready = pair("xT_ready")
        v_ready = pair("v_ready")
        ss_ready = pair("ss_ready")
        ny_ready = pair("ny_ready")
        part_ready = pair("part_ready")
        term_ready = pair("term_ready")
        qT_ready = pair("qT_ready")
        kT_ready = pair("kT_ready")
        qk_done = sem("qk_done")
        exp_done = sem("exp_done")
        mask_done = sem("mask_done")
        pv_done = sem("pv_done")
        o_free = sem("o_free")
        on_ready = pair("on_ready")
        onT_ready = pair("onT_ready")
        fmv_ready = sem("fmv_ready")
        frs_ready = sem("frs_ready")
        fh_ready = sem("fh_ready")
        fo_stat = sem("fo_stat")
        fo_scale = sem("fo_scale")
        hT_ready = sem("hT_ready")
        lsh_ready = sem("lsh_ready")
        lex_ready = sem("lex_ready")
        oh_ready = sem("oh_ready")
        ohT_ready = sem("ohT_ready")
        hm_ready = sem("hm_ready")
        hp_ready = sem("hp_ready")
        z_ready = sem("z_ready")
        ez_ready = sem("ez_ready")
        h1p_ready = sem("h1p_ready")
        y_ready = sem("y_ready")

        def bank(step, j=0):
            return misc[TAKE[(*step, j)][0]]

        def take(pe, step, j=0):
            i, n = TAKE[(*step, j)]
            if n:
                pe.wait_ge(bank_free[i], n)

        def full(step, j=0):
            return bank_full[TAKE[(*step, j)][0]]

        def free(step, j=0):
            return bank_free[TAKE[(*step, j)][0]]

        def wait_full(eng, step, j=0):
            i, n = TAKE[(*step, j)]
            eng.wait_ge(bank_full[i], n + 1)

        x_v = x.rearrange("a (t p) d -> p (a t) d", p=P)
        out_v = out.rearrange("a (t p) d -> p (a t) d", p=P)
        col = lambda w: w.rearrange("(p a) -> p a", a=1)

        block = ctx.enter_context(nc.Block())

        @block.sync
        def _(sp):
            sp.dma_start(X[:, 0:2, :], x_v[:, 0:2, :]).then_inc(x_in[0], 16)
            sp.dma_start(ident[:], ident_d).then_inc(small_in, 16)
            sp.dma_start(rope[:], rope_d).then_inc(small_in, 16)
            sp.dma_start(wraw[G][:, 0:P], g_wq).then_inc(wa_in, 16)
            sp.dma_start(kvd[:], g_kv_down).then_inc(wa_in, 16)
            sp.dma_start(kvup[:, 0:32], g_k_up).then_inc(wa_in, 16)
            sp.dma_start(kvup[:, 32:64], g_v_up).then_inc(wa_in, 16)
            sp.dma_start(nw[G][:], col(norm1_w)).then_inc(wa_in, 16)
            sp.dma_start(rw[:], router_w).then_inc(wa_in, 16)
            for b in range(1, NB):
                sp.dma_start(X[:, 2 * b:2 * b + 2, :], x_v[:, 2 * b:2 * b + 2, :]).then_inc(x_in[b], 16)
            for b in range(NB):
                for i in range(2):
                    sp.wait_ge(y_ready, 2 * b + i + 1)
                    sp.dma_start(out_v[:, 2 * b + i, :], X1[:, b, i, :]).then_inc(y_out, 16)
            sp.wait_ge(y_out, 16 * TILES)

        @block.gpsimd
        def _(pool):
            chain = [0]

            def link(ins):
                chain[0] += 1
                ins.then_inc(pch, 1)
                pool.wait_ge(pch, chain[0])

            def weights():
                pool.memset(mhalf[:], -0.5).then_inc(const_ready, 1)
                pool.memset(ones[:], 1.0).then_inc(const_ready, 1)
                pool.memset(V[G][:], 1.0).then_inc(const_ready, 1)
                pool.memset(V[L][:], 1.0).then_inc(const_ready, 1)
                pool.wait_ge(const_ready, 4)

            def rsqrt(out, value, eps):
                link(pool.tensor_scalar(out, value, 1.0, eps, ALU.mult, ALU.add))
                link(pool.tensor_tensor(out, out, mhalf[:, 0:2], ALU.pow))

            def stat(a, b):
                r, m, v = rs[a], mv[a][:, :, 0], mv[a][:, :, 1]
                pool.wait_ge(mv_ready[a], b + 1)
                if a == G:
                    if b:
                        pool.wait_ge(xn_ready[a], b)
                    rsqrt(r[:, 0, :], v, EPS_LN)
                    link(pool.tensor_tensor(r[:, 1, :], r[:, 0, :], r[:, 0, :], ALU.mult))
                    link(pool.tensor_tensor(r[:, 1, :], r[:, 1, :], v, ALU.mult))
                    rsqrt(r[:, 2, :], r[:, 1, :], EPS_RMS)
                    pool.tensor_tensor(r[:, 3, :], r[:, 0, :], r[:, 2, :], ALU.mult).then_inc(rs_ready[a], 1)
                else:
                    if b:
                        pool.wait_ge(xn_ready[a], b)
                    link(pool.tensor_tensor(r[:, 1, :], m, m, ALU.mult))
                    link(pool.tensor_tensor(r[:, 1, :], r[:, 1, :], v, ALU.add))
                    link(pool.tensor_scalar(r[:, 1, :], r[:, 1, :], 1.0, EPS_RMS, ALU.mult, ALU.add))
                    pool.tensor_tensor(r[:, 3, :], r[:, 1, :], mhalf[:, 0:2], ALU.pow).then_inc(rs_ready[a], 1)

            def newton(a, b, k):
                v, y, t = nv[a][:], ny[a][:], nt[a][:]
                link(pool.tensor_tensor(t, y, y, ALU.mult))
                link(pool.tensor_tensor(t, t, v, ALU.mult))
                link(pool.tensor_scalar(t, t, -0.5, 1.5, ALU.mult, ALU.add))
                ins = pool.tensor_tensor(y, y, t, ALU.mult)
                if k < 2:
                    link(ins)
                else:
                    ins.then_inc(ny_ready[a], 1)

            def proj(a, b):
                v, y = nv[a][:], ny[a][:]
                pool.wait_ge(ss_ready[a], b + 1)
                if b:
                    pool.wait_ge(part_ready[a], b)
                link(pool.tensor_scalar(v, ss[a][:], 1.0 / HD, EPS_RMS, ALU.mult, ALU.add))
                link(pool.tensor_scalar(y.bitcast(I32), v.bitcast(I32), -0.5, MAGIC, ALU.mult, ALU.add))
                newton(a, b, 0)

            def expand(a, b, i):
                pool.wait_ge(part_ready[a], b + 1)
                if b:
                    pool.wait_ge(kT_ready[a], b)
                    pool.wait_ge(qT_ready[a], 2 * b)
                for p, (lo, n) in enumerate([(0, 3), (3, 3), (6, 2)]):
                    src = part[a][:, p, i, 0:P].rearrange("p (h d) -> p h d", d=HD)
                    pool.tensor_scalar(qe[a][:, i, :, lo:lo + n, :], src.unsqueeze(2).broadcast_to([P, H, n, HD]),
                                       1.0, 0.0, ALU.mult, ALU.add)
                for p in range(3):
                    src = part[a][:, p, i, P:QKW].rearrange("p (h d) -> p h d", d=HD)
                    n = 3 if p < 2 else 2
                    ins = pool.tensor_scalar(ke[a][:, i, :, p::3, :], src.unsqueeze(2).broadcast_to([P, KVH, n, HD]),
                                             1.0, 0.0, ALU.mult, ALU.add)
                ins.then_inc(term_ready[a], 1)

            def qkmask(*u):
                if u not in MASK:
                    return
                a, b, g, kb = u
                p = prob[:, UNIT[u] % NP, :, :]
                pool.wait_ge(exp_done, UNIT[u] + 1)
                if a == G:
                    d = p[:, :, P * (kb - 2 * b):P * (kb - 2 * b) + P]
                    pool.affine_select(out=d, in_=d, compare_op=ALU.is_ge, fill=0.0, base=0,
                                       pattern=[[0, 4], [1, P]], channel_multiplier=-1).then_inc(mask_done, 1)
                else:
                    pool.wait_ge(wf_in, 16 * 14)
                    lo, n = (0, P) if kb else (0 if b else WIN, P + 2 * WIN - (0 if b else WIN))
                    m = band[:, (WIN if kb else lo):(WIN if kb else lo) + n]
                    d = p[:, :, lo:lo + n]
                    pool.tensor_tensor(d, d, m.unsqueeze(1).broadcast_to([P, 4, n]), ALU.mult).then_inc(mask_done, 1)

            def fstat(b):
                pool.wait_ge(fmv_ready, 2 * b + 1)
                rsqrt(frs[:, 0, :], fmv[:, 0, :, 1], EPS_LN)
                pool.tensor_tensor(frs[:, 1, :], frs[:, 0, :], fmv[:, 0, :, 0], ALU.mult).then_inc(frs_ready, 1)

            def fxa(b):
                r = frs
                pool.wait_ge(fmv_ready, 2 * b + 2)
                rsqrt(r[:, 2, :], fmv[:, 1, :, 1], EPS_LN)
                link(pool.tensor_tensor(r[:, 3, :], r[:, 2, :], r[:, 2, :], ALU.mult))
                link(pool.tensor_tensor(r[:, 3, :], r[:, 3, :], fmv[:, 1, :, 1], ALU.mult))
                rsqrt(r[:, 4, :], r[:, 3, :], EPS_LN)
                pool.tensor_tensor(r[:, 5, :], r[:, 2, :], r[:, 4, :], ALU.mult).then_inc(frs_ready, 1)

            def fsum(b, i):
                pool.wait_ge(fo_stat, 2 * b + 1 + i)
                link(pool.tensor_scalar(frs[:, 6 + i, 0:1], fmv[:, 2, i, 1:2], 1.0, EPS_LN, ALU.mult, ALU.add))
                pool.tensor_tensor(frs[:, 6 + i, 1:2], frs[:, 6 + i, 0:1], mhalf[:, 0:1], ALU.pow).then_inc(fo_scale, 1)

            run = {"weights": weights, "stat": stat, "proj": proj, "newton": newton, "expand": expand, "qk": qkmask,
                   "fstat": fstat, "fxa": fxa, "fsum": fsum}
            for kind, *at in PLAN:
                if kind in run:
                    run[kind](*at)

        @block.scalar
        def _(act):
            def weights():
                act.dma_start(wraw[L][:, 0:P], l_wq).then_inc(wf_in, 16)
                act.dma_start(wraw[L][:, P:QKW], l_wk).then_inc(wf_in, 16)
                act.dma_start(wraw[L][:, QKW:PW], l_wv).then_inc(wf_in, 16)
                act.dma_start(nw[L][:], col(norm2_w)).then_inc(wf_in, 16)
                act.dma_start(wo_sb[G][:], g_wo).then_inc(wf_in, 16)
                act.dma_start(wo_sb[L][:], l_wo).then_inc(wf_in, 16)
                act.dma_start(band[:], band_d).then_inc(wf_in, 16)
                act.dma_start(rank[:], rank_d).then_inc(wf_in, 16)
                act.dma_start(gamma[:], col(ln_gamma)).then_inc(wf_in, 16)
                act.dma_start(beta[:], col(ln_beta)).then_inc(wf_in, 16)
                act.dma_start(w1n[:, 0:NE * FT, :], ew1.rearrange("e (t p) d -> p (e t) d", p=P)).then_inc(wf_in, 16)
                act.dma_start(w1n[:, NE * FT:, :], sw1.rearrange("(t p) d -> p t d", p=P)).then_inc(wf_in, 16)
                act.dma_start(w2n[:, 0:NE, :], ew2.rearrange("e p f -> p e f")).then_inc(wf_in, 16)
                act.dma_start(w2n[:, NE, :], sw2).then_inc(wf_in, 16)

            def xT_copy(a, b):
                s = ("xT", a, b)
                wait_full(act, s)
                if b:
                    act.wait_ge(v_ready[a], b)
                act.copy(xT[a][:], bank(s)[:, 0:QB]).then_inc(free(s), 1)

            def exp(*u):
                n = UNIT[u]
                a, b, g, kb = u
                act.wait_ge(qk_done, n + 1)
                if n >= NP:
                    act.wait_ge(pv_done, PV[UNIT_LIST[n - NP]] + 1)
                ps = pieces(a, b, kb)
                lo, hi = ps[0][3], ps[-1][3] + ps[-1][2]
                src = scores[n % 2][:].rearrange("p (m q) -> p m q", m=4)[:, :, lo:hi]
                act.activation(prob[:, n % NP, :, lo:hi], src, ACT.Exp, scale=float(HD) ** -0.5).then_inc(exp_done, 1)

            def o_copy(a, b, g):
                act.wait_ge(pv_done, PV[ENDS[(a, b, g)][1]] + 1)
                if b:
                    i, n = TAKE[("oT", a, b - 1, 1, 0)]
                    act.wait_ge(bank_full[i], n + 1)
                o, f = (osum_g, o_free) if a == G else (bank(("pv", L, b, g, 0)), free(("pv", L, b, g, 0)))
                act.copy(oTs[a][:, g, :], o[:, 0:QB]).then_inc(f, 1)

            def onT_copy(a, b):
                s = ("onT", a, b)
                wait_full(act, s)
                act.copy(onT[a][:], bank(s)[:, 0:QB]).then_inc(free(s), 1)

            def fhT(b):
                s = ("fhT", b)
                wait_full(act, s)
                act.activation(hT[:], bank(s)[:, 0:QB], ACT.Identity, scale=gamma[:, 0:1],
                               bias=beta[:, 0:1]).then_inc(free(s), 1)

            def frouter(b):
                act.wait_ge(lsh_ready, b + 1)
                act.activation(lex[:], lsh[:], ACT.Exp).then_inc(lex_ready, 1)

            def fw1s(b):
                s = ("fw1s", b)
                wait_full(act, s, 0)
                act.copy(s1s[:].rearrange("p t q -> p (t q)"), bank(s, 0)[:]).then_inc(free(s, 0), 1)

            def fact(b):
                act.wait_ge(z_ready, b + 1)
                act.activation(ez, z, ACT.Tanh, scale=0.5).then_inc(ez_ready, 1)

            run = {"weights": weights, "xT": xT_copy, "qk": exp, "oevac": o_copy, "onT": onT_copy, "fhT": fhT, "frouter": frouter,
                   "fw1s": fw1s, "fact": fact}
            for kind, *at in PLAN:
                if kind in run:
                    run[kind](*at)

        @block.tensor
        def _(pe):
            def weights():
                s = ("weights",)
                pe.wait_ge(small_in, 32)
                pe.wait_ge(wa_in, 16 * 6)
                take(pe, s, 0)
                pe.transpose(bank(s, 0)[0:32, 0:P], kvd[:], ident[:]).then_inc(full(s, 0), 1)
                pe.wait_ge(free(s, 0), 1)
                pe.matmul(bank(s, 1)[:, 0:64], kvdT[:], kvup[:], start=True, stop=True).then_inc(full(s, 1), 1)
                pe.transpose(bank(s, 2)[:, 0:NE], rw[:], ident[0:NE, 0:NE]).then_inc(full(s, 2), 1)

            def wturn(k):
                s = ("wturn", k)
                pe.wait_ge(tern_ready, k + 1)
                take(pe, s)
                for m, (w, r, c) in enumerate(TURNS[k]):
                    src = t1[:, r, :] if w == 1 else t2[:, r, P * c:P * c + P]
                    ins = pe.transpose(bank(s)[:].bitcast(BF16)[:, P * m:P * m + P], src, identb[:])
                ins.then_inc(full(s), 1)

            def scales():
                s = ("scales",)
                pe.wait_ge(scale_ready, 1)
                take(pe, s, 0)
                o = bank(s, 0)[0:3 * NE, :].bitcast(BF16)
                for m in range(FT):
                    pe.transpose(o[:, P * m:P * m + P], s1p[:, m, :, :].rearrange("p a e -> p (a e)"), identb[:])
                pe.transpose(o[:, P * FT:P * FT + P], s2p[:].rearrange("p a e -> p (a e)"),
                             identb[:]).then_inc(full(s, 0), 1)
                take(pe, s, 1)
                pe.wait_ge(const_ready, 4)
                pe.matmul(bank(s, 1)[:, 0:P], ones[:], s2diag[:], start=True, stop=True).then_inc(full(s, 1), 1)

            def xT_turn(a, b):
                s = ("xT", a, b)
                pe.wait_ge(xn_ready[a], b + 1)
                take(pe, s)
                for i in range(2):
                    ins = pe.transpose(bank(s)[:, P * i:P * i + P], xn[a][:, i, :], ident[:])
                ins.then_inc(full(s), 1)

            def proj(a, b):
                s = ("proj", a, b)
                if b == 0:
                    pe.wait_ge(wqkv_ready, 1 + a)
                i, n = TAKE[("xT", a, b, 0)]
                pe.wait_ge(bank_free[i], n + 1)
                take(pe, s)
                for i in range(2):
                    ins = pe.matmul(bank(s)[:, PW * i:PW * i + PW], xT[a][:, P * i:P * i + P], wqkv[a][:],
                                    start=True, stop=True)
                ins.then_inc(full(s), 1)

            def k_turn(a, b):
                s = ("kT", a, b)
                pe.wait_ge(term_ready[a], 2 * b + 2)
                take(pe, s)
                o = bank(s)[:].bitcast(BF16)
                for g in range(KVH):
                    for i in range(2):
                        src = ke[a][:, i, g, :, :].rearrange("p t d -> p (t d)")
                        for half in range(2):
                            ins = pe.transpose(o[64 * half:64 * half + 64, P * (2 * g + i):P * (2 * g + i) + P], src, identb[:])
                ins.then_inc(full(s), 1)

            def q_turn(a, b, i):
                s = ("qT", a, b, i)
                pe.wait_ge(term_ready[a], 2 * b + 2)
                take(pe, s)
                o = bank(s)[:].bitcast(BF16)
                for m in range(H // 2):
                    ins = pe.transpose(o[:, P * m:P * m + P],
                                       qe[a][:, i, 2 * m:2 * m + 2, :, :].rearrange("p h t d -> p (h t d)"), identb[:])
                ins.then_inc(full(s), 1)

            def qk_product(*u):
                a, b, g, kb = u
                n = UNIT[u]
                pe.wait_ge(qT_ready[a], 2 * b + 2)
                pe.wait_ge(kT_ready[a], b + 1)
                if n >= 2:
                    pe.wait_ge(exp_done, n - 1)
                for m in range(2):
                    for t, q, w, c in pieces(a, b, kb):
                        o = scores[n % 2][:, 512 * m:512 * m + 512].rearrange("p (h q) -> p h q", h=2)
                        ins = pe.matmul(o[:, :, c:c + w], kT[a][:, g, P * (t % kept[a]):P * (t % kept[a]) + P],
                                        qT[a][:, b % Q_KEPT[a], 2 * g + m, :, q:q + w], start=True, stop=True)
                ins.then_inc(qk_done, 1)

            def pv_product(*u):
                a, b, g, kb = u
                n = UNIT[u]
                first, last = [u == x for x in ENDS[(a, b, g)]]
                if a == G:
                    o = osum_g
                    if first and OSUM[(b, g)]:
                        pe.wait_ge(o_free, OSUM[(b, g)])
                else:
                    s = ("pv", L, b, g, 0)
                    if first:
                        take(pe, s)
                    o = bank(s)
                pe.wait_ge(v_ready[a], b + 1)
                if u in MASK:
                    pe.wait_ge(mask_done, MASK[u] + 1)
                else:
                    pe.wait_ge(exp_done, n + 1)
                for k, (t, q, w, c) in enumerate(pieces(a, b, kb)):
                    for m in range(4):
                        ins = pe.matmul(o[32 * m:32 * m + 32, q:q + w], V[a][:, t % kept[a], g, :],
                                        prob[:, n % NP, m, c:c + w], start=(first and k == 0), stop=last,
                                        skip_group_check=True)
                        if a == L and last and m == 2:
                            ins.then_inc(full(s), 1)
                ins.then_inc(pv_done, 1)

            def o_turn(a, b, i):
                s = ("oT", a, b, i)
                if a == G:
                    pe.wait_ge(o_free, KVH * (b + 1))
                else:
                    for g in range(KVH):
                        j, n = TAKE[("pv", L, b, g, 0, 0)]
                        pe.wait_ge(bank_free[j], n + 1)
                take(pe, s)
                for g in range(KVH):
                    ins = pe.transpose(bank(s)[:, P * g:P * g + P], oTs[a][:, g, P * i:P * i + P], ident[:])
                ins.then_inc(full(s), 1)

            def on_turn(a, b):
                s = ("onT", a, b)
                pe.wait_ge(on_ready[a], 2 * b + 2)
                take(pe, s)
                for i in range(2):
                    ins = pe.transpose(bank(s)[:, P * i:P * i + P], on[a][:, i, :], ident[:])
                ins.then_inc(full(s), 1)

            def wo_product(a, b):
                s = ("wo", a, b)
                if a == G and b == 0:
                    pe.wait_ge(wf_in, 16 * 14)
                i, n = TAKE[("onT", a, b, 0)]
                pe.wait_ge(bank_free[i], n + 1)
                take(pe, s)
                for i in range(2):
                    ins = pe.matmul(bank(s)[:, P * i:P * i + P], onT[a][:, P * i:P * i + P], wo_sb[a][:],
                                    start=True, stop=True)
                ins.then_inc(full(s), 1)

            def fhT(b):
                s = ("fhT", b)
                pe.wait_ge(fh_ready, b + 1)
                take(pe, s)
                for i in range(2):
                    ins = pe.transpose(bank(s)[:, P * i:P * i + P], fh[:, i, :], ident[:])
                ins.then_inc(full(s), 1)

            def frouter(b):
                s = ("frouter", b)
                i, n = TAKE[("fhT", b, 0)]
                pe.wait_ge(bank_free[i], n + 1)
                take(pe, s)
                for i in range(2):
                    ins = pe.matmul(bank(s)[:, NE * i:NE * i + NE], hT[:, P * i:P * i + P], rwT[:], start=True, stop=True)
                ins.then_inc(full(s), 1)

            def fohT(b):
                s = ("fohT", b)
                pe.wait_ge(oh_ready, b + 1)
                take(pe, s)
                for i in range(2):
                    ins = pe.transpose(bank(s)[0:24, :].bitcast(BF16)[:, P * i:P * i + P],
                                       oh[:, i, :, :].rearrange("p a e -> p (a e)"), identb[:])
                ins.then_inc(full(s), 1)

            def fmask(b, i):
                s = ("fmask", b, i)
                pe.wait_ge(oh_ready, b + 1)
                take(pe, s)
                for e in range(NE):
                    ins = pe.transpose(bank(s)[:].bitcast(BF16)[:, P * e:P * e + P],
                                       oh[:, i, 0, e:e + 1].broadcast_to([P, P]), identb[:])
                ins.then_inc(full(s), 1)

            def fw1s(b):
                s = ("fw1s", b)
                pe.wait_ge(ohT_ready, b + 1)
                take(pe, s, 0)
                for f in range(FT):
                    ins = pe.matmul(bank(s, 0)[:, QB * f:QB * f + QB], s1pT[:, f, :], ohT[:], start=True, stop=True)
                ins.then_inc(full(s, 0), 1)
                pe.wait_ge(hp_ready, b + 1)
                take(pe, s, 1)
                for f in range(FT):
                    for p in range(3):
                        ins = pe.matmul(bank(s, 1)[:, QB * f:QB * f + QB], t1T[:, NE * FT + f, :], hp[:, p, :],
                                        start=(p == 0), stop=(p == 2))
                ins.then_inc(full(s, 1), 1)

            def fw1(b, f):
                s = ("fw1", b, f)
                pe.wait_ge(hm_ready, 2 * b + 2)
                take(pe, s)
                for e in range(NE):
                    for p in range(3):
                        ins = pe.matmul(bank(s)[:, 0:QB], t1T[:, FT * e + f, :], hm[:, e, p, :],
                                        start=(e == 0 and p == 0), stop=(e == NE - 1 and p == 2))
                ins.then_inc(full(s), 1)

            def fw2(b, i):
                s = ("fw2", b, i)
                pe.wait_ge(h1p_ready, b + 1)
                for j in range(2):
                    take(pe, s, j)
                    for p in range(3):
                        for f in range(FT):
                            ins = pe.matmul(bank(s, j)[:], h1p[:, p, f, P * i:P * i + P],
                                            t2T[:, f, 4 * j:4 * j + 4, :].rearrange("p e d -> p (e d)"),
                                            start=(p == 0 and f == 0), stop=(p == 2 and f == FT - 1))
                    ins.then_inc(full(s, j), 1)

            def fw2s(b, i):
                s = ("fw2s", b, i)
                take(pe, s)
                for p in range(3):
                    for f in range(FT):
                        pe.matmul(bank(s)[:, 0:P], h1p[:, p, FT + f, P * i:P * i + P], t2T[:, f, NE, :],
                                  start=(p == 0 and f == 0), stop=(p == 2 and f == FT - 1))
                pe.matmul(bank(s)[:, P:2 * P], ohT[:, P * i:P * i + P], s2pT[:], start=True, stop=True).then_inc(full(s), 1)

            run = {"weights": weights, "wturn": wturn, "scales": scales, "xT": xT_turn, "proj": proj, "kT": k_turn, "qT": q_turn,
                   "qk": qk_product, "pv": pv_product, "oT": o_turn, "onT": on_turn, "wo": wo_product, "fhT": fhT,
                   "frouter": frouter, "fohT": fohT, "fmask": fmask, "fw1s": fw1s, "fw1": fw1, "fw2": fw2,
                   "fw2s": fw2s}
            for kind, *at in PLAN:
                if kind in run:
                    run[kind](*at)

        @block.vector
        def _(dve):
            chain = [0]

            def link(ins):
                chain[0] += 1
                ins.then_inc(dch, 1)
                dve.wait_ge(dch, chain[0])

            def weights():
                s = ("weights",)
                for a in (G, L):
                    for r in range(2):
                        ins = dve.memset(qT[a][64 * r:64 * r + 64, :, :, 1 - r, :], 0)
                link(ins)
                dve.wait_ge(small_in, 32)
                dve.wait_ge(wa_in, 16 * 6)
                dve.tensor_copy(identb[:], ident[:]).then_inc(prep_read, 1)
                wait_full(dve, s, 0)
                dve.tensor_copy(kvdT[:], bank(s, 0)[0:32, 0:P]).then_inc(free(s, 0), 1)
                dve.tensor_scalar(wqkv[G][:, 0:P], wraw[G][:, 0:P], nw[G][:, 0:1], None, ALU.mult)
                wait_full(dve, s, 1)
                link(dve.tensor_scalar(wqkv[G][:, P:PW], bank(s, 1)[:, 0:64], nw[G][:, 0:1], None, ALU.mult))
                dve.sem_inc(free(s, 1), 1)
                dve.sem_inc(wqkv_ready, 1)
                wait_full(dve, s, 2)
                dve.tensor_copy(rwT[:], bank(s, 2)[:, 0:NE]).then_inc(free(s, 2), 1)

            def prep():
                dve.wait_ge(wf_in, 16 * 14)
                dve.tensor_scalar(wqkv[L][:], wraw[L][:], nw[L][:, 0:1], None, ALU.mult).then_inc(wqkv_ready, 1)
                link(dve.tensor_reduce(s1c[:], w1n, AX.X, ALU.add, apply_absolute_value=True))
                link(dve.tensor_reduce(s2c[:], w2n, AX.X, ALU.add, apply_absolute_value=True))
                link(dve.tensor_scalar(s1c[:], s1c[:], 1.0 / P, 1e-5, ALU.mult, ALU.max))
                link(dve.tensor_scalar(s2c[:], s2c[:], 1.0 / (FT * P), 1e-5, ALU.mult, ALU.max))
                dve.tensor_scalar(half1[:, 0, :], s1c[:], 0.5, None, ALU.mult)
                dve.tensor_scalar(half2[:, 0, :], s2c[:], 0.5, None, ALU.mult)
                dve.tensor_scalar(half1[:, 1, :], s1c[:], -0.5, None, ALU.mult)
                link(dve.tensor_scalar(half2[:, 1, :], s2c[:], -0.5, None, ALU.mult))
                dve.tensor_scalar(s2diag[:], ident[:], half2[:, 0, NE:NE + 1], None, ALU.mult)
                v = s1c[:, 0:NE * FT].rearrange("p (e f) -> p f e", f=FT)
                link(dve.tensor_copy(s1p[:, :, 0, :], v))
                link(dve.tensor_tensor(s1q[:], v, s1p[:, :, 0, :], ALU.subtract))
                link(dve.tensor_copy(s1p[:, :, 1, :], s1q[:]))
                link(dve.tensor_tensor(s1p[:, :, 2, :], s1q[:], s1p[:, :, 1, :], ALU.subtract))
                link(dve.tensor_copy(s2p[:, 0, :], half2[:, 0, 0:NE]))
                link(dve.tensor_tensor(s2q[:], half2[:, 0, 0:NE], s2p[:, 0, :], ALU.subtract))
                link(dve.tensor_copy(s2p[:, 1, :], s2q[:]))
                dve.tensor_tensor(s2p[:, 2, :], s2q[:], s2p[:, 1, :], ALU.subtract).then_inc(scale_ready, 1)

            def ternary(k):
                rows = sorted({(w, r) for w, r, _ in TURNS[k]})
                for w, r in rows:
                    raw, low, half = (w1n, t1b, half1) if w == 1 else (w2n, t2b, half2)
                    ins = dve.tensor_scalar(low[:, r, :], raw[:, r, :], half[:, 1, r:r + 1], None, ALU.is_lt)
                link(ins)
                for w, r in rows:
                    raw, low, half, t = (w1n, t1b, half1, t1) if w == 1 else (w2n, t2b, half2, t2)
                    ins = dve.scalar_tensor_tensor(out=t[:, r, :], in0=raw[:, r, :], scalar=half[:, 0, r:r + 1],
                                                   in1=low[:, r, :], op0=ALU.is_gt, op1=ALU.subtract)
                ins.then_inc(tern_ready, 1)

            def wturn(k):
                s = ("wturn", k)
                wait_full(dve, s)
                src = bank(s)[:].bitcast(BF16)
                if k < 2:
                    ins = dve.tensor_copy(t1T[:, 8 * k:8 * k + 8, :].rearrange("p k d -> p (k d)"), src)
                elif k == 2:
                    dve.tensor_copy(t1T[:, 16:18, :].rearrange("p k d -> p (k d)"), src[:, 0:2 * P])
                    ins = dve.tensor_copy(t2T[:, :, NE, :], src[:, 2 * P:4 * P].rearrange("p (f d) -> p f d", f=FT))
                else:
                    e = 4 * (k - 3)
                    ins = dve.tensor_copy(t2T[:, :, e:e + 4, :], src.rearrange("p (e f d) -> p f e d", f=FT, d=P))
                link(ins)
                dve.sem_inc(free(s), 1)

            def scales():
                s = ("scales",)
                wait_full(dve, s, 0)
                src = bank(s, 0)[0:3 * NE, :].bitcast(BF16)
                dve.tensor_copy(s1pT[:].rearrange("p f d -> p (f d)"), src[:, 0:2 * P])
                link(dve.tensor_copy(s2pT[:], src[:, 2 * P:3 * P]))
                dve.sem_inc(free(s, 0), 1)
                wait_full(dve, s, 1)
                dve.tensor_copy(s2row[:], bank(s, 1)[:, 0:P]).then_inc(free(s, 1), 1)

            def rows(a, b):
                return X[:, 2 * b:2 * b + 2, :] if a == G else X1[:, b, :, :]

            def stat(a, b):
                src = rows(a, b)
                if a == G:
                    dve.wait_ge(x_in[b], 16)
                if b:
                    dve.wait_ge(xn_ready[a], b)
                for i in range(2):
                    ins = dve.bn_stats(stats[a][:, i, :], src[:, i, :])
                link(ins)
                for i in range(2):
                    ins = dve.bn_aggr(mv[a][:, i, :], stats[a][:, i, :])
                ins.then_inc(mv_ready[a], 1)

            def norm(a, b):
                src = rows(a, b)
                dve.wait_ge(rs_ready[a], b + 1)
                if b:
                    i, n = TAKE[("xT", a, b - 1, 0)]
                    dve.wait_ge(bank_full[i], n + 1)
                for i in range(2):
                    if a == G:
                        dve.tensor_scalar(Hn[:, b % 3, i, :], src[:, i, :], mv[a][:, i, 0:1], rs[a][:, 0, i:i + 1],
                                          ALU.subtract, ALU.mult)
                        ins = dve.tensor_scalar(xn[a][:, i, :], src[:, i, :], mv[a][:, i, 0:1], rs[a][:, 3, i:i + 1],
                                                ALU.subtract, ALU.mult)
                    else:
                        ins = dve.tensor_scalar(xn[a][:, i, :], src[:, i, :], rs[a][:, 3, i:i + 1], None, ALU.mult)
                ins.then_inc(xn_ready[a], 1)

            def proj(a, b):
                s = ("proj", a, b)
                wait_full(dve, s)
                src = bank(s)[:, 0:2 * PW].rearrange("p (i w) -> p i w", i=2)[:, :, 0:QKW]
                s4 = src.rearrange("p i (h d) -> p i h d", d=HD)
                c4, n4 = [t[a][:].rearrange("p i (h d) -> p i h d", d=HD) for t in (cosp, sinp)]
                tab = rope[:, a, :, 2 * b:2 * b + 2, :]

                def wide(t):
                    return t.unsqueeze(2).broadcast_to([P, 2, H + KVH, t.shape[2]])

                if b:
                    dve.wait_ge(part_ready[a], b)
                dve.tensor_tensor(c4, s4, wide(tab[:, 0]), ALU.mult)
                dve.tensor_tensor(n4[:, :, :, 0::2], s4[:, :, :, 1::2], wide(tab[:, 1, :, 0::2]), ALU.mult)
                link(dve.tensor_tensor(n4[:, :, :, 1::2], s4[:, :, :, 0::2], wide(tab[:, 1, :, 1::2]), ALU.mult))
                if a == G and b == 0:
                    dve.wait_ge(const_ready, 4)
                old = b - kept[a] // 2 + 1
                if a == L and old >= 1:
                    dve.wait_ge(pv_done, PV[(L, old, KVH - 1, 1)] + 1)
                t = 2 * b % kept[a]
                vsrc = bank(s)[:, 0:2 * PW].rearrange("p (i w) -> p i w", i=2)[:, :, QKW:PW]
                dve.tensor_copy(V[a][:, t:t + 2, :, 0:HD],
                                vsrc.rearrange("p i (g d) -> p i g d", d=HD)).then_inc(v_ready[a], 1)
                dve.wait_ge(v_ready[a], b + 1)
                dve.sem_inc(free(s), 1)
                link(dve.tensor_tensor(qk[a][:], cosp[a][:], sinp[a][:], ALU.add))
                link(dve.tensor_tensor(cosp[a][:], qk[a][:], qk[a][:], ALU.mult))
                dve.tensor_reduce(ss[a][:], cosp[a][:].rearrange("p i (h d) -> p (i h) d", d=HD), AX.X,
                                  ALU.add).then_inc(ss_ready[a], 1)

            def split(a, b):
                dve.wait_ge(ny_ready[a], b + 1)
                if b:
                    dve.wait_ge(term_ready[a], 2 * b)
                y = ny[a][:].unsqueeze(2).broadcast_to([P, 2 * (H + KVH), HD])
                link(dve.tensor_tensor(qn[a][:].rearrange("p i (h d) -> p (i h) d", d=HD),
                                       qk[a][:].rearrange("p i (h d) -> p (i h) d", d=HD), y, ALU.mult))
                link(dve.tensor_copy(part[a][:, 0], qn[a][:]))
                link(dve.tensor_tensor(res[a][:], qn[a][:], part[a][:, 0], ALU.subtract))
                link(dve.tensor_copy(part[a][:, 1], res[a][:]))
                dve.tensor_tensor(part[a][:, 2], res[a][:], part[a][:, 1], ALU.subtract).then_inc(part_ready[a], 1)

            def k_copy(a, b):
                s = ("kT", a, b)
                wait_full(dve, s)
                old = b - kept[a] // 2 + 1
                if a == L and old >= 1:
                    dve.wait_ge(qk_done, UNIT[(L, old, KVH - 1, 1)] + 1)
                k = P * (2 * b % kept[a])
                dve.tensor_copy(kT[a][:, :, k:k + QB],
                                bank(s)[:].bitcast(BF16).rearrange("p (g q) -> p g q", g=KVH)).then_inc(free(s), 1)
                dve.wait_ge(free(s), TAKE[(*s, 0)][1] + 1)
                dve.sem_inc(kT_ready[a], 1)

            def q_copy(a, b, i):
                s = ("qT", a, b, i)
                wait_full(dve, s)
                old = b - Q_KEPT[a]
                if old >= 0:
                    dve.wait_ge(qk_done, UNIT[(a, old, *units_of(a, old)[-1])] + 1)
                for r in range(2):
                    rows = slice(64 * r, 64 * r + 64)
                    ins = dve.tensor_copy(qT[a][rows, b % Q_KEPT[a], :, r, P * i:P * i + P],
                                          bank(s)[rows].bitcast(BF16).rearrange("p (m q) -> p m q", m=H // 2))
                ins.then_inc(free(s), 1)
                dve.wait_ge(free(s), TAKE[(*s, 0)][1] + 1)
                dve.sem_inc(qT_ready[a], 1)

            def o_scale(a, b, i):
                s = ("oT", a, b, i)
                wait_full(dve, s)
                if b:
                    j, n = TAKE[("onT", a, b - 1, 0)]
                    dve.wait_ge(bank_full[j], n + 1)
                o = bank(s)[:].rearrange("p (h c) -> p h c", c=32)
                link(dve.reciprocal(rec[a][:].unsqueeze(2), o[:, :, HD:HD + 1]))
                link(dve.tensor_tensor(on[a][:, i, :].rearrange("p (h d) -> p h d", d=HD), o[:, :, 0:HD],
                                       rec[a][:].unsqueeze(2).broadcast_to([P, H, HD]), ALU.mult))
                dve.sem_inc(free(s), 1)
                dve.sem_inc(on_ready[a], 1)

            def residual(a, b):
                s = ("wo", a, b)
                wait_full(dve, s)
                src = bank(s)[:, 0:QB].rearrange("p (i d) -> p i d", i=2)
                if a == G:
                    link(dve.tensor_tensor(X1[:, b], src, Hn[:, b % 3], ALU.add))
                else:
                    link(dve.tensor_tensor(X1[:, b], src, X1[:, b], ALU.add))
                dve.sem_inc(free(s), 1)

            def fstat(b):
                for i in range(2):
                    ins = dve.bn_stats(fst[:, 0, i, :], X1[:, b, i, :])
                link(ins)
                for i in range(2):
                    ins = dve.bn_aggr(fmv[:, 0, i, :], fst[:, 0, i, :])
                ins.then_inc(fmv_ready, 1)

            def fxa(b):
                dve.wait_ge(frs_ready, 2 * b + 1)
                for i in range(2):
                    ins = dve.tensor_scalar(ftmp[:, i, :], X1[:, b, i, :], frs[:, 0, i:i + 1], frs[:, 1, i:i + 1],
                                            ALU.mult, ALU.subtract)
                link(ins)
                link(dve.tensor_tensor(X1[:, b], X[:, 2 * b:2 * b + 2, :], ftmp[:], ALU.add))
                for i in range(2):
                    ins = dve.bn_stats(fst[:, 1, i, :], X1[:, b, i, :])
                link(ins)
                for i in range(2):
                    ins = dve.bn_aggr(fmv[:, 1, i, :], fst[:, 1, i, :])
                ins.then_inc(fmv_ready, 1)

            def fh_norm(b):
                dve.wait_ge(frs_ready, 2 * b + 2)
                if b:
                    i, n = TAKE[("fhT", b - 1, 0)]
                    dve.wait_ge(bank_full[i], n + 1)
                for i in range(2):
                    ins = dve.tensor_scalar(fh[:, i, :], X1[:, b, i, :], fmv[:, 1, i, 0:1], frs[:, 5, i:i + 1],
                                            ALU.subtract, ALU.mult)
                ins.then_inc(fh_ready, 1)

            def fparts(b):
                i, n = TAKE[("fhT", b, 0)]
                dve.wait_ge(bank_free[i], n + 1)
                link(dve.tensor_copy(hp[:, 0, :], hT[:]))
                link(dve.tensor_tensor(hres[:], hT[:], hp[:, 0, :], ALU.subtract))
                link(dve.tensor_copy(hp[:, 1, :], hres[:]))
                dve.tensor_tensor(hp[:, 2, :], hres[:], hp[:, 1, :], ALU.subtract).then_inc(hp_ready, 1)

            def frouter(b):
                s = ("frouter", b)
                wait_full(dve, s)
                lg = bank(s)[:, 0:2 * NE].rearrange("p (i e) -> p i e", i=2)
                wide = lambda t: t.unsqueeze(2).broadcast_to([P, 2, NE])
                link(dve.tensor_reduce(lmax[:], lg, AX.X, ALU.max))
                link(dve.tensor_tensor(lsh[:], lg, wide(lmax[:]), ALU.subtract))
                dve.sem_inc(lsh_ready, 1)
                dve.sem_inc(free(s), 1)
                link(dve.tensor_scalar(leq[:], lsh[:], 0.0, None, ALU.is_equal))
                link(dve.tensor_tensor(lrk[:], leq[:], rank[:].unsqueeze(1).broadcast_to([P, 2, NE]), ALU.mult))
                link(dve.tensor_reduce(lbest[:], lrk[:], AX.X, ALU.max))
                if b:
                    dve.wait_ge(full(("fw1s", b - 1), 0), TAKE[("fw1s", b - 1, 0)][1] + 1)
                for i in range(2):
                    ins = dve.tensor_tensor(oh[:, i], lrk[:, i].unsqueeze(1).broadcast_to([P, 3, NE]),
                                            lbest[:, i:i + 1].unsqueeze(2).broadcast_to([P, 3, NE]), ALU.is_equal)
                ins.then_inc(oh_ready, 1)

            def fohT(b):
                s = ("fohT", b)
                wait_full(dve, s)
                link(dve.tensor_copy(ohT[:], bank(s)[0:24, :].bitcast(BF16)[:, 0:QB]))
                dve.sem_inc(free(s), 1)
                dve.sem_inc(ohT_ready, 1)
                dve.wait_ge(lex_ready, b + 1)
                link(dve.tensor_reduce(lsum[:], lex[:], AX.X, ALU.add))
                link(dve.reciprocal(tp[:], lsum[:]))

            def fmask(b, i):
                s = ("fmask", b, i)
                wait_full(dve, s)
                m = bank(s)[:].bitcast(BF16).rearrange("p (e q) -> p e q", e=NE)
                h = hp[:, :, P * i:P * i + P]
                for e in range(NE):
                    ins = dve.tensor_tensor(hm[:, e, :, P * i:P * i + P], h, m[:, e, :].unsqueeze(1).broadcast_to([P, 3, P]),
                                            ALU.mult)
                link(ins)
                dve.sem_inc(free(s), 1)
                dve.sem_inc(hm_ready, 1)

            def fw1s(b):
                s = ("fw1s", b)
                wait_full(dve, s, 1)
                for f in range(FT):
                    ins = dve.tensor_scalar(z[:, FT + f, :], bank(s, 1)[:, QB * f:QB * f + QB],
                                            s1c[:, NE * FT + f:NE * FT + f + 1], None, ALU.mult)
                link(ins)
                dve.sem_inc(free(s, 1), 1)

            def fz(b, f):
                s = ("fw1", b, f)
                wait_full(dve, s)
                i, n = TAKE[("fw1s", b, 0)]
                dve.wait_ge(bank_free[i], n + 1)
                link(dve.tensor_tensor(z[:, f, :], bank(s)[:, 0:QB], s1s[:, f, :], ALU.mult))
                dve.sem_inc(free(s), 1)
                if f == 1:
                    dve.sem_inc(z_ready, 1)

            def fh1(b):
                dve.wait_ge(ez_ready, b + 1)
                link(dve.scalar_tensor_tensor(out=h1, in0=ez, scalar=1.0, in1=z, op0=ALU.add, op1=ALU.mult))
                link(dve.tensor_copy(h1p[:, 0], h1))
                link(dve.tensor_tensor(zr, h1, h1p[:, 0], ALU.subtract))
                link(dve.tensor_copy(h1p[:, 1], zr))
                dve.tensor_tensor(h1p[:, 2], zr, h1p[:, 1], ALU.subtract).then_inc(h1p_ready, 1)

            def fsel(b, i):
                s = ("fw2", b, i)
                for j in range(2):
                    wait_full(dve, s, j)
                    link(dve.tensor_tensor(sel[:, 4 * j:4 * j + 4, :], bank(s, j)[:].rearrange("p (e d) -> p e d", e=4),
                                           oh[:, i, 0, 4 * j:4 * j + 4].unsqueeze(2).broadcast_to([P, 4, P]), ALU.mult))
                    dve.sem_inc(free(s, j), 1)
                link(dve.tensor_reduce(acc[:], sel.rearrange("p e d -> p d e"), AX.X, ALU.add))

            def fsum(b, i):
                s = ("fw2s", b, i)
                wait_full(dve, s)
                link(dve.tensor_tensor(accs[:], acc[:], bank(s)[:, P:2 * P], ALU.mult))
                link(dve.tensor_tensor(shd[:], bank(s)[:, 0:P], s2row[:], ALU.mult))
                dve.sem_inc(free(s), 1)
                link(dve.scalar_tensor_tensor(out=fo[:, i, :], in0=accs[:], scalar=tp[:, i:i + 1], in1=shd[:], op0=ALU.mult,
                                              op1=ALU.add))
                link(dve.bn_stats(fst[:, 2, i, :], fo[:, i, :]))
                dve.bn_aggr(fmv[:, 2, i, :], fst[:, 2, i, :]).then_inc(fo_stat, 1)

            def fout(b, i):
                dve.wait_ge(fo_scale, 2 * b + 1 + i)
                link(dve.tensor_scalar(fl[:], fo[:, i, :], fmv[:, 2, i, 0:1], frs[:, 6 + i, 1:2], ALU.subtract, ALU.mult))
                dve.tensor_tensor(X1[:, b, i, :], X1[:, b, i, :], fl[:], ALU.add).then_inc(y_ready, 1)

            run = {"weights": weights, "prep": prep, "ternary": ternary, "wturn": wturn, "scales": scales,
                   "stat": stat, "norm": norm, "proj": proj, "split": split, "kT": k_copy, "qT": q_copy,
                   "oT": o_scale, "wo": residual, "fstat": fstat, "fxa": fxa, "fh": fh_norm,
                   "fparts": fparts, "frouter": frouter, "fohT": fohT, "fmask": fmask, "fw1s": fw1s, "fz": fz,
                   "fh1": fh1, "fsel": fsel, "fsum": fsum, "fout": fout}
            for kind, *at in PLAN:
                if kind in run:
                    run[kind](*at)


def tables():
    tokens = np.arange(TILES * P, dtype=np.float32)
    rope = np.zeros((P, 2, 2, TILES, HD), np.float32)
    for a, base in enumerate((1000000.0, 10000.0)):
        inv = np.float32(1.0) / np.float32(base) ** (np.arange(0, HD, 2, dtype=np.float32) / np.float32(HD))
        freq = (tokens[:, None] * inv[None, :].astype(np.float32)).astype(np.float64)
        c = np.repeat(np.cos(freq), 2, axis=1)
        s = np.stack([-np.sin(freq), np.sin(freq)], axis=-1).reshape(TILES * P, HD)
        for k, t in enumerate((c, s)):
            rope[:, a, k] = t.astype(np.float32).reshape(TILES, P, HD).transpose(1, 0, 2)
    key = np.arange(P)[:, None]
    before = np.arange(WIN)[None, :] + P - key < WIN
    i = np.arange(P + WIN)[None, :] - key
    band = np.concatenate([before, (i >= 0) & (i < WIN)], axis=1).astype(np.float32)
    rank = np.repeat(np.arange(NE, 0, -1, dtype=np.float32)[None, :], P, axis=0)
    return {"ident": np.eye(P, dtype=np.float32), "rope": rope, "band": band, "rank": rank}


_INS = ["L0_attn_hidden", "L0_attn_norm1_w", "L0_attn_norm2_w", "L0_attn_g_wq", "L0_attn_g_kv_down",
        "L0_attn_g_k_up", "L0_attn_g_v_up", "L0_attn_g_wo", "L0_attn_l_wq", "L0_attn_l_wk", "L0_attn_l_wv",
        "L0_attn_l_wo", "L0_ffn_shared_w1", "L0_ffn_shared_w2", "L0_ffn_expert_w1", "L0_ffn_expert_w2",
        "L0_ffn_router_w", "L0_ffn_ln_gamma", "L0_ffn_ln_beta"]


def kernel(**inputs):
    import concourse.bacc as _bacc
    from concourse.bass_utils import run_bass_kernel_spmd as _run

    nc = _bacc.Bacc("TRN2", target_bir_lowering=False, num_devices=1)
    arrays, args = {}, []
    given = {name: np.ascontiguousarray(inputs[name]) for name in _INS}
    for name, a in {**given, **tables()}.items():
        arrays[f"in_{name}_dram"] = a
        args.append(nc.dram_tensor(f"in_{name}_dram", a.shape, mybir.dt.from_np(a.dtype), kind="ExternalInput").ap())
    args.append(nc.dram_tensor("out_0_dram", (1, TILES * P, P), F32, kind="ExternalOutput").ap())
    build(nc, *args)
    r = _run(nc, [arrays], core_ids=[0])
    return r.results[0]["out_0_dram"]
```
